# Optimizing a Trainium2 kernel written in Bass

```python
import numpy as np
import jax
import jax.numpy as jnp

def _softmax(x, axis=-1):
    return jax.nn.softmax(x, axis=axis)

def _gelu(x):
    return jax.nn.gelu(x, approximate=True)

def _silu(x):
    return jax.nn.silu(x)

def _sigmoid(x):
    return jax.nn.sigmoid(x)

def _layernorm(x, axis=-1, eps=1e-05):
    m = jnp.mean(x, axis=axis, keepdims=True)
    v = jnp.var(x, axis=axis, keepdims=True)
    return (x - m) / jnp.sqrt(v + eps)

def _scatter_add(tgt, idx, src, axis=0):
    return tgt.at[idx].add(src)

def _segment_sum(src, seg, n):
    return jax.ops.segment_sum(src, seg, n)
kernel_name = 'mk_decoder_postln_d1_seqx_r4_5fa3fe'

def setup_inputs(seed: int=0):
    np.random.seed(seed)
    _w = jnp.asarray

    def _rec_inputs():
        import jax
        import jax.numpy as jnp
        _rk = jax.random.key(seed)
        x = -0.0005207 + 1.001 * jax.random.normal(jax.random.fold_in(_rk, 1), (2, 1024, 256), jnp.float32)
        _lenS = 1024 - jax.random.randint(jax.random.fold_in(_rk, 7), (2,), 0, max(1, 1024 // 4) + 1, jnp.int32)
        _lenS2 = 77 - jax.random.randint(jax.random.fold_in(_rk, 8), (2,), 0, max(1, 77 // 4) + 1, jnp.int32)
        _ctx_1024P = jax.random.normal(jax.random.fold_in(_rk, 11), (2, 16, 256), jnp.float32)
        _ctx_1024c = jax.random.dirichlet(jax.random.fold_in(_rk, 511), 0.3 * jnp.ones((16,), jnp.float32), (2, 77))
        _ctx_1024t = jnp.einsum('bsk,bkd->bsd', _ctx_1024c, _ctx_1024P)
        _ctx_1024t = _ctx_1024t * jax.lax.rsqrt(jnp.mean(jnp.square(_ctx_1024t)) + 1e-12) * 0.953939
        ctx_1024 = 4.13588e-05 + 0.999923 * (_ctx_1024t + 0.3 * jax.random.normal(jax.random.fold_in(_rk, 611), (2, 77, 256), jnp.float32))
        return (x, ctx_1024)
    x, ctx_1024 = _rec_inputs()

    def _L0_attn_setup():
        import jax, jax.numpy as jnp
        import numpy as np
        NUM_BLOCKS = 4
        B, S, D = (4, 1024, 256)
        A, FF = (256, 1024)
        LN_EPS = 1e-06

        def _ln(x, s, b):
            m = jnp.mean(x, axis=-1, keepdims=True)
            v = jnp.mean(jnp.square(x - m), axis=-1, keepdims=True)
            return (x - m) * jax.lax.rsqrt(v + LN_EPS) * s + b
        key = jax.random.key(seed)
        ks = jax.random.split(key, 8)
        w = lambda k, shape: jax.random.normal(k, shape, dtype=jnp.float32) * 0.02
        return {'x': jax.random.normal(ks[0], (B, S, D), dtype=jnp.float32), 'Wq': w(ks[1], (NUM_BLOCKS, D, A)), 'bq': jnp.zeros((NUM_BLOCKS, A), jnp.float32), 'Wk': w(ks[2], (NUM_BLOCKS, D, A)), 'bk': jnp.zeros((NUM_BLOCKS, A), jnp.float32), 'Wv': w(ks[3], (NUM_BLOCKS, D, A)), 'bv': jnp.zeros((NUM_BLOCKS, A), jnp.float32), 'Wo': w(ks[4], (NUM_BLOCKS, A, D)), 'bo': jnp.zeros((NUM_BLOCKS, D), jnp.float32), 'ln1_s': jnp.ones((NUM_BLOCKS, D), jnp.float32), 'ln1_b': jnp.zeros((NUM_BLOCKS, D), jnp.float32), 'W1': w(ks[5], (NUM_BLOCKS, D, FF)), 'b1': jnp.zeros((NUM_BLOCKS, FF), jnp.float32), 'W2': w(ks[6], (NUM_BLOCKS, FF, D)), 'b2': jnp.zeros((NUM_BLOCKS, D), jnp.float32), 'ln2_s': jnp.ones((NUM_BLOCKS, D), jnp.float32), 'ln2_b': jnp.zeros((NUM_BLOCKS, D), jnp.float32)}
    _L0_attn_all = _L0_attn_setup()
    _L0_attn_in = {k: v for k, v in _L0_attn_all.items() if k in ('Wq', 'bq', 'Wk', 'bk', 'Wv', 'bv', 'Wo', 'bo', 'ln1_s', 'ln1_b', 'W1', 'b1', 'W2', 'b2', 'ln2_s', 'ln2_b')}
    del _L0_attn_all

    def _L0_xattn_setup():
        import jax, jax.numpy as jnp
        import numpy as np
        D_MODEL = 256
        N_HEADS = 16
        HEAD_DIM = D_MODEL // N_HEADS
        key = jax.random.key(seed)
        ks = jax.random.split(key, 10)
        B, Lq, Lkv = (4, 128, 512)
        s = 1.0 / np.sqrt(D_MODEL)
        return {'q': jax.random.normal(ks[0], (B, Lq, D_MODEL), jnp.float32), 'kv': jax.random.normal(ks[1], (B, Lkv, D_MODEL), jnp.float32), 'Wq': jax.random.normal(ks[2], (D_MODEL, D_MODEL), jnp.float32) * s, 'bq': jnp.zeros((D_MODEL,), jnp.float32), 'Wk': jax.random.normal(ks[3], (D_MODEL, D_MODEL), jnp.float32) * s, 'bk': jnp.zeros((D_MODEL,), jnp.float32), 'Wv': jax.random.normal(ks[4], (D_MODEL, D_MODEL), jnp.float32) * s, 'bv': jnp.zeros((D_MODEL,), jnp.float32), 'Wo': jax.random.normal(ks[5], (D_MODEL, D_MODEL), jnp.float32) * s, 'bo': jnp.zeros((D_MODEL,), jnp.float32)}
    _L0_xattn_all = _L0_xattn_setup()
    _L0_xattn_in = {k: v for k, v in _L0_xattn_all.items() if k in ('Wq', 'bq', 'Wk', 'bk', 'Wv', 'bv', 'Wo', 'bo')}
    del _L0_xattn_all

    def _L0_ffn_setup():
        import math
        import jax, jax.numpy as jnp
        import numpy as np
        B, T, D = (4, 1024, 256)
        H = 16
        HD = D // H
        CAP = int(1024 * 0.125)
        DFF = int(D * 4 * 2 / 3)
        EPS = 1e-06

        def rmsnorm(x, g):
            return x * jax.lax.rsqrt(jnp.mean(x * x, axis=-1, keepdims=True) + EPS) * g
        key = jax.random.key(seed)
        ks = jax.random.split(key, 9)
        s = lambda k, shape: jax.random.normal(k, shape, jnp.float32) * 0.02
        return {'x': jax.random.normal(ks[0], (B, T, D), jnp.float32), 'w_router': s(ks[1], (D,)), 'W_qkv': s(ks[2], (3 * D, D)), 'W_out': s(ks[3], (D, D)), 'g1': jnp.ones((D,), jnp.float32), 'g2': jnp.ones((D,), jnp.float32), 'W1': s(ks[4], (DFF, D)), 'W2': s(ks[5], (DFF, D)), 'W3': s(ks[6], (D, DFF))}
    _L0_ffn_all = _L0_ffn_setup()
    _L0_ffn_in = {k: v for k, v in _L0_ffn_all.items() if k in ('w_router', 'W_qkv', 'W_out', 'g1', 'g2', 'W1', 'W2', 'W3')}
    del _L0_ffn_all
    return {'x': x, 'ctx_1024': ctx_1024, 'L0_attn_Wq': _L0_attn_in['Wq'], 'L0_attn_bq': _L0_attn_in['bq'], 'L0_attn_Wk': _L0_attn_in['Wk'], 'L0_attn_bk': _L0_attn_in['bk'], 'L0_attn_Wv': _L0_attn_in['Wv'], 'L0_attn_bv': _L0_attn_in['bv'], 'L0_attn_Wo': _L0_attn_in['Wo'], 'L0_attn_bo': _L0_attn_in['bo'], 'L0_attn_ln1_s': _L0_attn_in['ln1_s'], 'L0_attn_ln1_b': _L0_attn_in['ln1_b'], 'L0_attn_W1': _L0_attn_in['W1'], 'L0_attn_b1': _L0_attn_in['b1'], 'L0_attn_W2': _L0_attn_in['W2'], 'L0_attn_b2': _L0_attn_in['b2'], 'L0_attn_ln2_s': _L0_attn_in['ln2_s'], 'L0_attn_ln2_b': _L0_attn_in['ln2_b'], 'L0_xattn_Wq': _L0_xattn_in['Wq'], 'L0_xattn_bq': _L0_xattn_in['bq'], 'L0_xattn_Wk': _L0_xattn_in['Wk'], 'L0_xattn_bk': _L0_xattn_in['bk'], 'L0_xattn_Wv': _L0_xattn_in['Wv'], 'L0_xattn_bv': _L0_xattn_in['bv'], 'L0_xattn_Wo': _L0_xattn_in['Wo'], 'L0_xattn_bo': _L0_xattn_in['bo'], 'L0_ffn_w_router': _L0_ffn_in['w_router'], 'L0_ffn_W_qkv': _L0_ffn_in['W_qkv'], 'L0_ffn_W_out': _L0_ffn_in['W_out'], 'L0_ffn_g1': _L0_ffn_in['g1'], 'L0_ffn_g2': _L0_ffn_in['g2'], 'L0_ffn_W1': _L0_ffn_in['W1'], 'L0_ffn_W2': _L0_ffn_in['W2'], 'L0_ffn_W3': _L0_ffn_in['W3']}

def reference(x, ctx_1024, L0_attn_Wq, L0_attn_bq, L0_attn_Wk, L0_attn_bk, L0_attn_Wv, L0_attn_bv, L0_attn_Wo, L0_attn_bo, L0_attn_ln1_s, L0_attn_ln1_b, L0_attn_W1, L0_attn_b1, L0_attn_W2, L0_attn_b2, L0_attn_ln2_s, L0_attn_ln2_b, L0_xattn_Wq, L0_xattn_bq, L0_xattn_Wk, L0_xattn_bk, L0_xattn_Wv, L0_xattn_bv, L0_xattn_Wo, L0_xattn_bo, L0_ffn_w_router, L0_ffn_W_qkv, L0_ffn_W_out, L0_ffn_g1, L0_ffn_g2, L0_ffn_W1, L0_ffn_W2, L0_ffn_W3):
    import jax
    import jax.numpy as jnp

    def _L0_attn_ref(x, Wq, bq, Wk, bk, Wv, bv, Wo, bo, ln1_s, ln1_b, W1, b1, W2, b2, ln2_s, ln2_b):
        import jax, jax.numpy as jnp
        import numpy as np
        NUM_BLOCKS = 4
        B, S, D = (4, 1024, 256)
        A, FF = (256, 1024)
        LN_EPS = 1e-06

        def _ln(x, s, b):
            m = jnp.mean(x, axis=-1, keepdims=True)
            v = jnp.mean(jnp.square(x - m), axis=-1, keepdims=True)
            return (x - m) * jax.lax.rsqrt(v + LN_EPS) * s + b
        for i in range(NUM_BLOCKS):
            residual = x
            q = x @ Wq[i] + bq[i]
            k = x @ Wk[i] + bk[i]
            v = x @ Wv[i] + bv[i]
            Q = jax.nn.elu(q) + 1.0
            K = jax.nn.elu(k) + 1.0
            KV = jnp.einsum('nsh,nsh->nh', K, v, precision='highest')
            Ksum = jnp.sum(K, axis=1)
            Z = 1.0 / (Q * Ksum[:, None, :] + 1e-06)
            V = Q * KV[:, None, :] * Z
            a = jax.nn.gelu(V @ Wo[i] + bo[i])
            a = jax.nn.gelu(a)
            x = _ln(a + residual, ln1_s[i], ln1_b[i])
            residual = x
            h = jax.nn.gelu(x @ W1[i] + b1[i])
            f = jax.nn.gelu(h @ W2[i] + b2[i])
            x = _ln(f + residual, ln2_s[i], ln2_b[i])
        return x

    def _L0_xattn_ref(q, kv, Wq, bq, Wk, bk, Wv, bv, Wo, bo):
        import jax, jax.numpy as jnp
        import numpy as np
        D_MODEL = 256
        N_HEADS = 16
        HEAD_DIM = D_MODEL // N_HEADS
        B, Lq, _ = q.shape
        Lkv = kv.shape[1]
        qh = (q @ Wq.T + bq).reshape(B, Lq, N_HEADS, HEAD_DIM)
        kh = (kv @ Wk.T + bk).reshape(B, Lkv, N_HEADS, HEAD_DIM)
        vh = (kv @ Wv.T + bv).reshape(B, Lkv, N_HEADS, HEAD_DIM)
        scale = 1.0 / np.sqrt(HEAD_DIM).astype(np.float32)
        scores = jnp.einsum('bqhd,bkhd->bhqk', qh, kh) * scale
        attn = jax.nn.softmax(scores, axis=-1)
        ctx = jnp.einsum('bhqk,bkhd->bqhd', attn, vh).reshape(B, Lq, D_MODEL)
        out = ctx @ Wo.T + bo
        return out

    def _L0_ffn_ref(x, w_router, W_qkv, W_out, g1, g2, W1, W2, W3):
        import math
        import jax, jax.numpy as jnp
        import numpy as np
        B, T, D = (4, 1024, 256)
        H = 16
        HD = D // H
        CAP = int(1024 * 0.125)
        DFF = int(D * 4 * 2 / 3)
        EPS = 1e-06

        def rmsnorm(x, g):
            return x * jax.lax.rsqrt(jnp.mean(x * x, axis=-1, keepdims=True) + EPS) * g
        Bq, Tq, Dq = x.shape
        scores = x @ w_router
        _, idx = jax.lax.top_k(scores, CAP)
        x_sel = jnp.take_along_axis(x, idx[:, :, None], axis=1)
        h = rmsnorm(x_sel, g1)
        qkv = (h @ W_qkv.T).reshape(Bq, CAP, 3, H, HD)
        q, k, v = jnp.moveaxis(qkv, 2, 0)
        att = jnp.einsum('bqhd,bkhd->bhqk', q, k) / math.sqrt(HD)
        mask = jnp.triu(jnp.ones((CAP, CAP), bool), 1)
        att = jnp.where(mask, -jnp.inf, att)
        att = jax.nn.softmax(att, axis=-1)
        o = jnp.einsum('bhqk,bkhd->bqhd', att, v).reshape(Bq, CAP, Dq)
        x_attn = o @ W_out.T
        h2 = rmsnorm(x_sel + x_attn, g2)
        x_ff = jax.nn.silu(h2 @ W1.T) * (h2 @ W2.T) @ W3.T
        x_proc = x_sel + x_attn + x_ff
        out = x.at[jnp.arange(Bq)[:, None], idx].set(x_proc)
        return out
    x = _layernorm(x + _L0_attn_ref(x, L0_attn_Wq, L0_attn_bq, L0_attn_Wk, L0_attn_bk, L0_attn_Wv, L0_attn_bv, L0_attn_Wo, L0_attn_bo, L0_attn_ln1_s, L0_attn_ln1_b, L0_attn_W1, L0_attn_b1, L0_attn_W2, L0_attn_b2, L0_attn_ln2_s, L0_attn_ln2_b), axis=-1)
    x = _layernorm(x + _L0_xattn_ref(x, ctx_1024, L0_xattn_Wq, L0_xattn_bq, L0_xattn_Wk, L0_xattn_bk, L0_xattn_Wv, L0_xattn_bv, L0_xattn_Wo, L0_xattn_bo), axis=-1)
    x = _layernorm(x + _L0_ffn_ref(x, L0_ffn_w_router, L0_ffn_W_qkv, L0_ffn_W_out, L0_ffn_g1, L0_ffn_g2, L0_ffn_W1, L0_ffn_W2, L0_ffn_W3), axis=-1)
    return x

_drawn_inputs = setup_inputs


def setup_inputs(seed=0):
    import zlib

    import numpy as np

    out = dict(_drawn_inputs(seed))
    spreads = {'L0_attn_bq': (0.0, 2.0),
     'L0_attn_bk': (0.0, 0.8),
     'L0_attn_bv': (0.0, 0.8),
     'L0_attn_bo': (0.0, 0.356),
     'L0_attn_ln1_s': (1.0, 0.2),
     'L0_attn_ln1_b': (0.0, 0.1),
     'L0_attn_b1': (0.0, 0.513),
     'L0_attn_b2': (0.0, 0.1),
     'L0_attn_ln2_s': (1.0, 0.2),
     'L0_attn_ln2_b': (0.0, 0.1),
     'L0_xattn_bq': (0.0, 0.345),
     'L0_xattn_bk': (0.0, 2.0),
     'L0_xattn_bv': (0.0, 0.1),
     'L0_xattn_bo': (0.0, 0.1),
     'L0_ffn_g1': (1.0, 0.6),
     'L0_ffn_g2': (1.0, 0.6)}
    factors = {'L0_attn_Wq': 64.0,
     'L0_attn_Wk': 8.0,
     'L0_attn_Wv': 8.0,
     'L0_attn_Wo': 6.604,
     'L0_ffn_w_router': 5.63,
     'L0_ffn_W_qkv': 5.813,
     'L0_ffn_W_out': 5.849,
     'L0_ffn_W1': 8.0,
     'L0_ffn_W2': 8.0,
     'L0_ffn_W3': 8.0}
    for name, (base, spread) in spreads.items():
        noise = np.random.default_rng([zlib.crc32(name.encode()), seed]).standard_normal(out[name].shape)
        drawn = base * np.exp(spread * noise) if base else spread * noise
        out[name] = jnp.asarray(drawn.astype(out[name].dtype))
    for name, factor in factors.items():
        out[name] = (out[name] * factor).astype(out[name].dtype)
    return out
```

```python
from contextlib import ExitStack

import concourse.bass as bass
from concourse import mybir

F32 = mybir.dt.float32
F32R = mybir.dt.float32r
ALU = mybir.AluOpType
ACT = mybir.ActivationFunctionType
AX = mybir.AxisListType

P = 128
BATCH, SEQ, D = 2, 1024, 256
TOKENS = BATCH * SEQ
LAYERS = 4
FF = 1024
KC = D // P
FC = FF // P
TW = 512
TILES = TOKENS // TW
ATTN_LN_EPS = 1e-6
LN_EPS = 1e-5
LOG_EXP, GELU, SILU = "natural_log_exp_and_others", "gelu_apprx_tanh_and_others", "silu_and_others"

_PARTS = (("bq", KC), ("bk", KC), ("bv", KC), ("bo", KC), ("ln1_s", KC), ("ln1_b", KC),
          ("b1", FC), ("b2", KC), ("ln2_s", KC), ("ln2_b", KC))
VEC = {name: sum(n for _, n in _PARTS[:i]) for i, (name, _) in enumerate(_PARTS)}
NVEC = sum(n for _, n in _PARTS)

ORDER = [("WQ", 0), ("X", 0), ("X", 1), ("A", 0), ("WO", 0), ("A", 1), ("X", 2), ("V", 0), ("W1", 0),
         ("A", 2), ("O", 0), ("X", 3), ("V", 1), ("M1", 0), ("A", 3), ("W2", 0), ("R1", 0), ("O", 1), ("V", 2),
         ("M1", 1), ("U", 0), ("R1", 1), ("O", 2), ("V", 3), ("T", 0), ("M1", 2), ("M2", 0), ("U", 1),
         ("R1", 2), ("R2", 0), ("O", 3), ("T", 1), ("M1", 3), ("M2", 1), ("U", 2), ("R1", 3), ("R2", 1),
         ("T", 2), ("M2", 2), ("U", 3), ("R2", 2), ("T", 3), ("M2", 3), ("R2", 3)]
NORMS = [(int(s[1]), t) for s, t in ORDER if s in ("M1", "M2")]
assert NORMS == [(int(s[1]), t) for s, t in ORDER if s in ("R1", "R2")]
assert NORMS == [({"O": 1, "T": 2}[s], t) for s, t in ORDER if s in ("O", "T")]
NN = len(NORMS)
JOBS = []
for _s, _t in ORDER:
    JOBS += {"A": [("k", _t, 0), ("v", _t, 0), ("q", _t, 0)], "O": [("o", _t, 0)],
             "U": [("u", _t, j) for j in range(FC // 2)]}.get(_s, [])
assert len(JOBS) % 2 == 0


def layers_stage(nc, sem, XF, ones_inv, consts, x_t, vecs, w_qkvo, w1, w2):
    with ExitStack() as ctx:
        def sb(name, shape, dt=F32):
            return ctx.enter_context(nc.sbuf_tensor(name, shape, dt))

        stgA = sb("stgA", [P, 4, KC, D])
        stgB = sb("stgB", [P, KC * FF])
        WAh, WAl = sb("WAh", [P, 4, KC, D], F32R), sb("WAl", [P, 4, KC, D], F32R)
        W1h, W1l = sb("W1h", [P, KC, FF], F32R), sb("W1l", [P, KC, FF], F32R)
        W2h, W2l = sb("W2h", [P, FC, D], F32R), sb("W2l", [P, FC, D], F32R)
        allvec = sb("allvec", [P, LAYERS * NVEC])
        vec = sb("vec", [P, NVEC])
        bq1, bk1, nbq, nbk = (sb(n, [P, KC]) for n in ("bq1", "bk1", "nbq", "nbk"))
        nls = {n: sb(f"nls{n}", [P, KC]) for n in (1, 2)}

        xh, xl = sb("xh", [P, 2, KC, TW], F32R), sb("xl", [P, 2, KC, TW], F32R)
        Ek, Eq = sb("Ek", [P, KC, TW]), sb("Eq", [P, KC, TW])
        Q = sb("Q", [P, KC, TOKENS])
        kpart, kvpart = sb("kpart", [P, KC, TILES]), sb("kvpart", [P, KC, TILES])
        ksum, nkvsum = sb("ksum", [P, KC, BATCH]), sb("nkvsum", [P, KC, BATCH])
        den, rec = sb("den", [P, KC, TW]), sb("rec", [P, KC, TW])
        vh, vl = sb("vh", [P, KC, TW], F32R), sb("vl", [P, KC, TW], F32R)
        R = {1: sb("R1", [P, 2, KC, TW]), 2: sb("R2", [P, 2, KC, TW])}
        RS = sb("RS", [P, TW])
        SQ, SS = sb("SQ", [P, KC, TW]), sb("SS", [P, 2, TW])
        Y0, Y2 = sb("Y0", [P, TW]), sb("Y2", [P, TW])
        x1 = sb("x1", [P, 2, KC, TW])
        x1h, x1l = sb("x1h", [P, KC, TW], F32R), sb("x1l", [P, KC, TW], F32R)
        HF = sb("HF", [P, 4, TW])
        hh, hl = sb("hh", [P, 4, TW], F32R), sb("hl", [P, 4, TW], F32R)

        pair = [ctx.enter_context(nc.psum_tensor(f"pair{i}", [P, KC, TW], F32)) for i in range(2)]
        pD = ctx.enter_context(nc.psum_tensor("pD", [P, KC, TW], F32))
        pMean = ctx.enter_context(nc.psum_tensor("pMean", [P, TW], F32))
        pVar = ctx.enter_context(nc.psum_tensor("pVar", [P, TW], F32))

        per_tile = {"k_mm": 1, "v_mm": 1, "q_mm": 1, "o_mm": 1, "u_mm": 4, "d_mm": 4,
                    "nk": 2, "nq": 2, "ek": 1, "eq": 1, "ekr": 1, "eqr": 1, "kdone": 2, "qdone": 2, "kvdone": 2,
                    "den": 2, "lnd": 1, "rec0": 1, "dy": 1, "rec": 1, "vdone": 2, "vh": 1, "vl": 1, "xh": 1, "xl": 1,
                    "go": 2, "go2": 1, "gd": 2, "r1": 1, "r2": 1, "x1": 2, "x1h": 1, "x1l": 1,
                    "h": 8, "hh": 8, "hl_dve": 4, "hl_pool": 4, "xnew": 2}
        per_layer = {"mean_mm": NN, "var_mm": NN, "rs": NN, "xc": NN, "sq": NN, "ss": NN, "guess": 3 * NN,
                     "newton": NN,
                     "rstd": NN, "y": NN, "wh": 4, "wl": 4, "sums": 4}
        S = {n: sem("l_" + n) for n in (*per_tile, *per_layer)}
        s_vec, s_stgA, s_stgB, s_allvec, s_x0 = (sem("l_" + n) for n in ("vec", "stgA", "stgB", "allvec", "x0"))
        owners = {"pe": ["k_mm", "v_mm", "q_mm", "o_mm", "u_mm", "d_mm", "mean_mm", "var_mm"],
                  "act": ["lnd", "rec0", "guess", "nk", "nq", "ek", "eq", "vh", "xh", "go", "go2", "gd", "x1h", "h",
                         "sq", "wh"],
                  "dve": ["ekr", "eqr", "kdone", "qdone", "kvdone", "den", "dy", "rec", "vdone", "r1", "r2", "x1", "hh",
                          "hl_dve", "xc", "newton", "rstd", "y", "wl", "sums"],
                  "pool": ["vl", "xl", "x1l", "hl_pool", "rs", "ss"]}

        def start_counts(eng, who):
            for n in owners[who]:
                eng.sem_inc(S[n], TILES * per_tile[n] if n in per_tile else per_layer[n])

        def tile_event(eng, name, L, t, n=None):
            e = per_tile[name]
            eng.wait_ge(S[name], L * (e * TILES) + (e * t + (e if n is None else n + 1)))

        def guess_event(eng, L, i, n):
            eng.wait_ge(S["guess"], L * (3 * NN) + (3 * i + n))

        def norm_event(eng, name, L, i):
            eng.wait_ge(S[name], L * NN + (i + 1))

        def weights_event(eng, name, L, i):
            eng.wait_ge(S[name], L * 4 + (i + 1))

        def slot(what, t, j=0):
            return pair[JOBS.index((what, t, j)) % 2]

        def slot_free(eng, what, t, j, L):
            i = JOBS.index((what, t, j)) - 2
            w, tt, jj = JOBS[i]
            tt -= TILES * (i < 0)
            name, n = {"k": ("kdone", 1), "v": ("kvdone", 1), "q": ("qdone", 1), "o": ("go", 1),
                       "u": ("h", 2 * jj + 1)}[w]
            tile_event(eng, name, L, tt, n)

        def col(name, c):
            return vec[:, VEC[name] + c:VEC[name] + c + 1]

        def chunks(t):
            return slice(t * TW, (t + 1) * TW)

        def three(eng, out, wh, wl, h, l, start, stop):
            eng.matmul(out, wh, l, start=start, stop=False)
            eng.matmul(out, wl, h, start=False, stop=False)
            return eng.matmul(out, wh, h, start=False, stop=stop)

        block = ctx.enter_context(nc.Block())

        @block.sync
        def _(sp):
            sp.dma_start(XF[:, :, :], x_t.rearrange("(k p) n -> p k n", p=P)).then_inc(s_x0, 16)
            sp.dma_start(allvec[:, :], vecs).then_inc(s_allvec, 16)
            with sp.Fori(1, LAYERS + 1) as L:
                weights_event(sp, "wl", L - 1, 1)
                sp.dma_start(stgA[:, :, :, :].rearrange("p w k n -> p (w k n)"),
                             w_qkvo[bass.ds((L - 1) * P, P), :]).then_inc(s_stgA, 16)
                weights_event(sp, "wl", L - 1, 3)
                sp.dma_start(stgB[:, :], w1[bass.ds((L - 1) * P, P), :]).then_inc(s_stgB, 16)
                weights_event(sp, "wl", L, 2)
                sp.dma_start(stgB[:, :], w2[bass.ds((L - 1) * P, P), :]).then_inc(s_stgB, 16)

        def weight_parts(i):
            if i < 2:
                w = slice(0, 3) if i == 0 else slice(3, 4)
                return tuple(x[:, w, :, :].rearrange("p w k n -> p (w k n)") for x in (stgA, WAh, WAl))
            a, b = ((W1h, W1l), (W2h, W2l))[i - 2]
            return stgB[:, :], a[:, :, :].rearrange("p k n -> p (k n)"), b[:, :, :].rearrange("p k n -> p (k n)")

        WSTEP = {"WQ": 0, "WO": 1, "W1": 2, "W2": 3}

        def weights_staged(eng, i, L):
            if i < 2:
                eng.wait_ge(s_stgA, L * 16)
            else:
                eng.wait_ge(s_stgB, L * 32 - 16 * (3 - i))

        def weights_used(eng, i, L):
            tile_event(eng, ("q_mm", "o_mm", "u_mm", "d_mm")[i], L - 1, TILES - 1)

        @block.scalar
        def _(act):
            start_counts(act, "act")
            with act.Fori(1, LAYERS + 1) as L:
                act.wait_ge(s_vec, L * 7)
                table = None
                for step, t in ORDER:
                    need = {"A": LOG_EXP, "V": LOG_EXP, "R1": LOG_EXP, "R2": LOG_EXP, "O": GELU, "U": GELU,
                            "T": GELU}.get(step)
                    if need and need != table:
                        act.preload_act_table_set(need)
                        table = need
                    if step in WSTEP:
                        i = WSTEP[step]
                        w, wh, _ = weight_parts(i)
                        weights_staged(act, i, L)
                        weights_used(act, i, L)
                        act.activation(wh, w, ACT.Copy).then_inc(S["wh"], 1)
                    if step == "X":
                        tile_event(act, "xnew", L - 1, t)
                        tile_event(act, "q_mm", L, t - 2)
                        act.activation(xh[:, t % 2], XF[:, :, chunks(t)], ACT.Copy).then_inc(S["xh"], 1)
                    if step == "A":
                        for what, E, nb, neg, done, before in (("k", Ek, nbk, "nk", "ek", "kvdone"),
                                                             ("q", Eq, nbq, "nq", "eq", "qdone")):
                            tile_event(act, what + "_mm", L, t)
                            for c in range(KC):
                                tile_event(act, before, L, t - 1, c)
                                act.activation(E[:, c], slot(what, t)[:, c], ACT.Relu, bias=nb[:, c:c + 1],
                                               scale=-1.0).then_inc(S[neg], 1)
                            tile_event(act, neg, L, t)
                            act.activation(E[:, :, :], E[:, :, :], ACT.Exp, scale=-1.0).then_inc(S[done], 1)
                    if step == "V":
                        tile_event(act, "den", L, t)
                        tile_event(act, "rec", L, t - 1)
                        act.activation(rec[:, :, :], den[:, :, :], ACT.Ln).then_inc(S["lnd"], 1)
                        tile_event(act, "lnd", L, t)
                        act.activation(rec[:, :, :], rec[:, :, :], ACT.Exp, scale=-1.0).then_inc(S["rec0"], 1)
                        tile_event(act, "vdone", L, t)
                        tile_event(act, "o_mm", L, t - 1)
                        act.activation(vh[:, :, :], Q[:, :, chunks(t)], ACT.Copy).then_inc(S["vh"], 1)
                    if step == "O":
                        tile_event(act, "o_mm", L, t)
                        tile_event(act, "x1", L, t - 2)
                        for c in range(KC):
                            act.activation(R[1][:, t % 2, c], slot("o", t)[:, c], ACT.Gelu_apprx_tanh,
                                           bias=col("bo", c)).then_inc(S["go"], 1)
                        tile_event(act, "go", L, t)
                        act.activation(R[1][:, t % 2], R[1][:, t % 2], ACT.Gelu_apprx_tanh).then_inc(S["go2"], 1)
                    if step in ("M1", "M2"):
                        n, i = int(step[1]), NORMS.index((int(step[1]), t))
                        norm_event(act, "xc", L, i)
                        norm_event(act, "ss", L, i - 1)
                        act.activation(SQ[:, :, :], R[n][:, t % 2], ACT.Square).then_inc(S["sq"], 1)
                    if step in ("R1", "R2"):
                        n, i = int(step[1]), NORMS.index((int(step[1]), t))
                        norm_event(act, "var_mm", L, i)
                        norm_event(act, "y", L, i - 1)
                        act.activation(Y0[:, :], pVar[:, :], ACT.Ln, bias=consts[:, 0:1]).then_inc(S["guess"], 1)
                        guess_event(act, L, i, 1)
                        act.activation(Y0[:, :], Y0[:, :], ACT.Exp, scale=-0.5).then_inc(S["guess"], 1)
                        guess_event(act, L, i, 2)
                        act.activation(Y2[:, :], Y0[:, :], ACT.Square, scale=0.5 ** 0.5).then_inc(S["guess"], 1)
                        if n == 1:
                            tile_event(act, "x1", L, t)
                            tile_event(act, "u_mm", L, t - 1)
                            act.activation(x1h[:, :, :], x1[:, t % 2], ACT.Copy).then_inc(S["x1h"], 1)
                    if step == "U":
                        for f in range(FC):
                            tile_event(act, "u_mm", L, t, f // 2)
                            tile_event(act, "hl_pool" if f % 2 else "hl_dve", L, t, f // 2 - 2)
                            act.activation(HF[:, f % 4], slot("u", t, f // 2)[:, f % 2], ACT.Gelu_apprx_tanh,
                                           bias=col("b1", f)).then_inc(S["h"], 1)
                    if step == "T":
                        tile_event(act, "d_mm", L, t)
                        tile_event(act, "xnew", L, t - 2)
                        for c in range(KC):
                            act.activation(R[2][:, t % 2, c], pD[:, c], ACT.Gelu_apprx_tanh,
                                           bias=col("b2", c)).then_inc(S["gd"], 1)

        @block.vector
        def _(dve):
            start_counts(dve, "dve")
            dve.wait_ge(s_x0, 16)
            dve.sem_inc(S["xnew"], TILES * per_tile["xnew"])
            dve.wait_ge(s_allvec, 16)
            with dve.Fori(1, LAYERS + 1) as L:
                tile_event(dve, "xnew", L - 1, TILES - 1)
                o = (L - 1) * NVEC
                dve.tensor_copy(vec[:, :], allvec[:, bass.ds(o, NVEC)]).then_inc(s_vec, 1)
                dve.wait_ge(s_vec, L * 7 - 6)
                for name, plus, minus in (("bq", bq1, nbq), ("bk", bk1, nbk)):
                    v = vec[:, VEC[name]:VEC[name] + KC]
                    dve.tensor_scalar(plus[:, :], v, 1.0, None, ALU.add).then_inc(s_vec, 1)
                    dve.tensor_scalar(minus[:, :], v, -1.0, None, ALU.mult).then_inc(s_vec, 1)
                for name, minus in (("ln1_s", nls[1]), ("ln2_s", nls[2])):
                    dve.tensor_scalar(minus[:, :], vec[:, VEC[name]:VEC[name] + KC], -1.0, None,
                                      ALU.mult).then_inc(s_vec, 1)
                dve.wait_ge(s_vec, L * 7)
                for step, t in ORDER:
                    if step in WSTEP:
                        i = WSTEP[step]
                        w, wh, wl = weight_parts(i)
                        weights_event(dve, "wh", L, i)
                        dve.tensor_tensor(wl, w, wh.bitcast(F32), ALU.subtract).then_inc(S["wl"], 1)
                    if step == "A":
                        for what, E, src, rnd, done, b1, out in (
                                ("k", Ek, "ek", "ekr", "kdone", bk1, Ek), ("v", None, None, None, "kvdone", None, None),
                                ("q", Eq, "eq", "eqr", "qdone", bq1, Q[:, :, chunks(t)])):
                            ps = slot(what, t)
                            if what == "v":
                                tile_event(dve, "v_mm", L, t)
                                tile_event(dve, "kdone", L, t)
                                for c in range(KC):
                                    dve.scalar_tensor_tensor(
                                        out=Ek[:, c], in0=ps[:, c], scalar=col("bv", c), in1=Ek[:, c], op0=ALU.add,
                                        op1=ALU.mult, accum_out=kvpart[:, c, t:t + 1]).then_inc(S[done], 1)
                                continue
                            tile_event(dve, src, L, t)
                            dve.tensor_scalar(E[:, :, :], E[:, :, :], -1.0, 1.0, ALU.add, ALU.add).then_inc(S[rnd], 1)
                            tile_event(dve, rnd, L, t)
                            for c in range(KC):
                                if what == "k":
                                    if t % 2 == 0:
                                        dve.wait_ge(S["sums"], L * 4 + (t - 2))
                                    dve.scalar_tensor_tensor(
                                        out=Ek[:, c], in0=ps[:, c], scalar=b1[:, c:c + 1], in1=E[:, c], op0=ALU.add,
                                        op1=ALU.max, accum_out=kpart[:, c, t:t + 1]).then_inc(S[done], 1)
                                else:
                                    tile_event(dve, "vdone", L - 1, t, c)
                                    dve.scalar_tensor_tensor(
                                        out=out[:, c], in0=ps[:, c], scalar=b1[:, c:c + 1], in1=E[:, c], op0=ALU.add,
                                        op1=ALU.max).then_inc(S[done], 1)
                    if step == "V":
                        b = t // 2
                        if t % 2 == 0:
                            tile_event(dve, "kvdone", L, t + 1)
                            tile_event(dve, "vdone", L - 1, t + 1)
                            dve.tensor_tensor(ksum[:, :, b:b + 1], kpart[:, :, t:t + 1], kpart[:, :, t + 1:t + 2],
                                              ALU.add).then_inc(S["sums"], 1)
                            dve.scalar_tensor_tensor(out=nkvsum[:, :, b], in0=kvpart[:, :, t], scalar=-1.0,
                                                     in1=kvpart[:, :, t + 1], op0=ALU.mult,
                                                     op1=ALU.subtract).then_inc(S["sums"], 1)
                            dve.wait_ge(S["sums"], L * 4 + (t + 2))
                        tile_event(dve, "qdone", L, t)
                        tile_event(dve, "vdone", L, t - 1)
                        for c in range(KC):
                            dve.tensor_scalar(den[:, c], Q[:, c, chunks(t)], ksum[:, c, b:b + 1], 1e-6,
                                              ALU.mult, ALU.add).then_inc(S["den"], 1)
                        tile_event(dve, "rec0", L, t)
                        dve.tensor_tensor(den[:, :, :], den[:, :, :], rec[:, :, :], ALU.mult).then_inc(S["dy"], 1)
                        tile_event(dve, "dy", L, t)
                        dve.scalar_tensor_tensor(out=den[:, :, :], in0=den[:, :, :], scalar=-2.0, in1=rec[:, :, :],
                                                 op0=ALU.add, op1=ALU.mult).then_inc(S["rec"], 1)
                        tile_event(dve, "rec", L, t)
                        for c in range(KC):
                            dve.scalar_tensor_tensor(out=Q[:, c, chunks(t)], in0=Q[:, c, chunks(t)],
                                                     scalar=nkvsum[:, c, b:b + 1], in1=den[:, c], op0=ALU.mult,
                                                     op1=ALU.mult).then_inc(S["vdone"], 1)
                    if step == "O":
                        tile_event(dve, "go2", L, t)
                        dve.tensor_tensor(R[1][:, t % 2], R[1][:, t % 2], XF[:, :, chunks(t)],
                                          ALU.add).then_inc(S["r1"], 1)
                    if step == "T":
                        tile_event(dve, "gd", L, t)
                        dve.tensor_tensor(R[2][:, t % 2], R[2][:, t % 2], x1[:, t % 2],
                                          ALU.add).then_inc(S["r2"], 1)
                    if step in ("M1", "M2"):
                        n, i = int(step[1]), NORMS.index((int(step[1]), t))
                        norm_event(dve, "mean_mm", L, i)
                        r = R[n][:, t % 2]
                        dve.tensor_tensor(r, r, pMean[:, None, :].to_broadcast([P, KC, TW]),
                                          ALU.subtract).then_inc(S["xc"], 1)
                    if step in ("R1", "R2"):
                        n, i = int(step[1]), NORMS.index((int(step[1]), t))
                        guess_event(dve, L, i, 3)
                        dve.scalar_tensor_tensor(out=Y2[:, :], in0=pVar[:, :], scalar=ATTN_LN_EPS, in1=Y2[:, :],
                                                 op0=ALU.add, op1=ALU.mult).then_inc(S["newton"], 1)
                        norm_event(dve, "newton", L, i)
                        dve.scalar_tensor_tensor(out=Y0[:, :], in0=Y2[:, :], scalar=-1.5, in1=Y0[:, :],
                                                 op0=ALU.add, op1=ALU.mult).then_inc(S["rstd"], 1)
                        norm_event(dve, "rstd", L, i)
                        norm_event(dve, "sq", L, i)
                        r = R[n][:, t % 2]
                        dve.tensor_tensor(r, r, Y0[:, None, :].to_broadcast([P, KC, TW]),
                                          ALU.mult).then_inc(S["y"], 1)
                        norm_event(dve, "y", L, i)
                        if n == 1:
                            tile_event(dve, "r2", L, t - 2)
                            tile_event(dve, "x1l", L, t - 2)
                        else:
                            tile_event(dve, "xl", L, t)
                        for c in range(KC):
                            to, done = (x1[:, t % 2, c], "x1") if n == 1 else (XF[:, c, chunks(t)], "xnew")
                            dve.tensor_scalar(to, r[:, c], nls[n][:, c:c + 1], col(f"ln{n}_b", c), ALU.mult,
                                              ALU.add).then_inc(S[done], 1)
                    if step == "U":
                        for f in range(FC):
                            tile_event(dve, "h", L, t, f)
                            tile_event(dve, "d_mm", L, t, f // 2 - 2)
                            dve.tensor_copy(hh[:, f % 4], HF[:, f % 4]).then_inc(S["hh"], 1)
                            if f % 2 == 0:
                                tile_event(dve, "hh", L, t, f)
                                dve.tensor_tensor(hl[:, f % 4], HF[:, f % 4], hh[:, f % 4].bitcast(F32),
                                                  ALU.subtract).then_inc(S["hl_dve"], 1)

        @block.gpsimd
        def _(pool):
            start_counts(pool, "pool")
            with pool.Fori(1, LAYERS + 1) as L:
                for step, t in ORDER:
                    if step == "X":
                        tile_event(pool, "xh", L, t)
                        pool.tensor_tensor(xl[:, t % 2], XF[:, :, chunks(t)], xh[:, t % 2].bitcast(F32),
                                           ALU.subtract).then_inc(S["xl"], 1)
                    if step == "V":
                        tile_event(pool, "vh", L, t)
                        pool.tensor_tensor(vl[:, :, :], Q[:, :, chunks(t)], vh[:, :, :].bitcast(F32),
                                           ALU.subtract).then_inc(S["vl"], 1)
                    if step in ("O", "T"):
                        n = 1 if step == "O" else 2
                        i = NORMS.index((n, t))
                        tile_event(pool, f"r{n}", L, t)
                        norm_event(pool, "mean_mm", L, i - 1)
                        pool.tensor_tensor(RS[:, :], R[n][:, t % 2, 0], R[n][:, t % 2, 1],
                                           ALU.add).then_inc(S["rs"], 1)
                    if step in ("M1", "M2"):
                        i = NORMS.index((int(step[1]), t))
                        norm_event(pool, "sq", L, i)
                        norm_event(pool, "var_mm", L, i - 2)
                        pool.tensor_tensor(SS[:, i % 2], SQ[:, 0], SQ[:, 1], ALU.add).then_inc(S["ss"], 1)
                    if step == "R1":
                        tile_event(pool, "x1h", L, t)
                        pool.tensor_tensor(x1l[:, :, :], x1[:, t % 2], x1h[:, :, :].bitcast(F32),
                                           ALU.subtract).then_inc(S["x1l"], 1)
                    if step == "U":
                        for f in range(1, FC, 2):
                            tile_event(pool, "hh", L, t, f)
                            pool.tensor_tensor(hl[:, f % 4], HF[:, f % 4], hh[:, f % 4].bitcast(F32),
                                               ALU.subtract).then_inc(S["hl_pool"], 1)

        @block.tensor
        def _(pe):
            start_counts(pe, "pe")

            def project(what, w, t, L, h, l):
                slot_free(pe, what, t, 0, L)
                ps = slot(what, t)
                for m in range(KC):
                    cols = slice(m * P, (m + 1) * P)
                    for k in range(KC):
                        mm = three(pe, ps[:, m], WAh[:, w, k, cols], WAl[:, w, k, cols], h[:, k], l[:, k],
                                   k == 0, k == KC - 1)
                mm.then_inc(S[what + "_mm"], 1)

            def down(t, j, L):
                tile_event(pe, "hl_dve", L, t, j)
                tile_event(pe, "hl_pool", L, t, j)
                if j == 0:
                    tile_event(pe, "gd", L, t - 1)
                for m in range(KC):
                    for f in (2 * j, 2 * j + 1):
                        cols = slice(m * P, (m + 1) * P)
                        mm = three(pe, pD[:, m], W2h[:, f, cols], W2l[:, f, cols], hh[:, f % 4], hl[:, f % 4],
                                   f == 0, f == FC - 1)
                mm.then_inc(S["d_mm"], 1)

            with pe.Fori(1, LAYERS + 1) as L:
                for step, t in ORDER:
                    if step == "A":
                        if t == 0:
                            weights_event(pe, "wl", L, 0)
                        tile_event(pe, "xl", L, t)
                        for what, w in (("k", 1), ("v", 2), ("q", 0)):
                            project(what, w, t, L, xh[:, t % 2], xl[:, t % 2])
                    if step == "O":
                        if t == 0:
                            weights_event(pe, "wl", L, 1)
                        tile_event(pe, "vl", L, t)
                        project("o", 3, t, L, vh, vl)
                    if step in ("M1", "M2"):
                        i = NORMS.index((int(step[1]), t))
                        norm_event(pe, "rs", L, i)
                        norm_event(pe, "xc", L, i - 1)
                        pe.matmul(pMean[:, :], ones_inv[:, :], RS[:, :], start=True,
                                  stop=True).then_inc(S["mean_mm"], 1)
                    if step in ("R1", "R2"):
                        i = NORMS.index((int(step[1]), t))
                        norm_event(pe, "ss", L, i)
                        norm_event(pe, "newton", L, i - 1)
                        pe.matmul(pVar[:, :], ones_inv[:, :], SS[:, i % 2], start=True,
                                  stop=True).then_inc(S["var_mm"], 1)
                    if step == "U":
                        if t == 0:
                            weights_event(pe, "wl", L, 2)
                        tile_event(pe, "x1l", L, t)
                        for j in range(FC // 2):
                            slot_free(pe, "u", t, j, L)
                            for f in (2 * j, 2 * j + 1):
                                cols = slice(f * P, (f + 1) * P)
                                for k in range(KC):
                                    mm = three(pe, slot("u", t, j)[:, f % 2], W1h[:, k, cols], W1l[:, k, cols],
                                               x1h[:, k], x1l[:, k], k == 0, k == KC - 1)
                            mm.then_inc(S["u_mm"], 1)
                            if j == 1 and t == 0:
                                weights_event(pe, "wl", L, 3)
                            if j:
                                down(t, j - 1, L)
                    if step == "T":
                        down(t, FC // 2 - 1, L)


HEADS, HD, KEYS = 16, 16, 77
HC = P // HD
HB = HC // 2
SUB = TW // P
UNITS = SUB * KC
BT = SEQ // TW


def cross_order():
    order = [("L", 0, 0), ("L", 1, 0), ("M", 0, 0), ("M", 1, 0), ("R", 0, 0), ("R", 1, 0), ("Q", 0, 0), ("Q", 1, 0)]
    n = BT * UNITS
    order += [("S", 0, 0), ("S", 0, 1)]
    for i in range(n + 2):
        for step, j in (("T", i), ("P", i - 1), ("C", i - 2), ("S", i + 2)):
            if 0 <= j < n and not (step == "S" and j < 2):
                order.append((step, j // UNITS, j % UNITS))
        for t in range(BT):
            last = (t + 1) * UNITS - 1 + 2
            order += {last: [("O", t, 1)], last + 1: [("M", t, 1)], last + 3: [("R", t, 1)]}.get(i, [])
    order += [("M", BT - 1, 1), ("R", BT - 1, 1)]
    return order


def cross_stage(nc, sem, XF, ones_inv, consts, ident, headmask, x_t, ctx_t, cvecs, cw):
    ORDER2 = cross_order()
    NORMS2 = [(n, t) for s, t, n in ORDER2 if s == "M"]
    assert NORMS2 == [(n, t) for s, t, n in ORDER2 if s == "R"]
    assert NORMS2 == [(n, t) for s, t, n in ORDER2 if s in ("L", "O")]
    NN2 = len(NORMS2)
    with ExitStack() as ctx:
        def sb(name, shape, dt=F32):
            return ctx.enter_context(nc.sbuf_tensor(name, shape, dt))

        W = sb("c_W", [P, 4, KC, D])
        cvec = sb("c_vec", [P, 4, KC])
        cT = sb("c_T", [P, KC, BATCH * KEYS])
        kT = sb("c_kT", [P, KC, BATCH * KEYS])
        KB = sb("c_KB", [P, BATCH * KC, HC, KEYS])
        V17 = sb("c_V17", [KEYS, BATCH, HEADS, HD + 1])
        B = sb("c_B", [P, BT, KC, TW])
        RS, SS = sb("c_RS", [P, TW]), sb("c_SS", [P, TW])
        SQ = sb("c_SQ", [P, KC, TW])
        Y0, Y2 = sb("c_Y0", [P, TW]), sb("c_Y2", [P, TW])
        q2 = sb("c_q2", [P, BT, KC, TW])
        Pb = sb("c_Pb", [P, 2, HC, KEYS])
        PT = sb("c_PT", [KEYS, 2, HC, P])
        mx = sb("c_mx", [P, 2, HC])
        rec = sb("c_rec", [P, 2, HC])
        Cx = sb("c_Cx", [P, 2, HC, HD])
        cxT = sb("c_cxT", [P, BT, KC, TW])

        psS = [ctx.enter_context(nc.psum_tensor(f"c_psS{i}", [P, 2, 512], F32)) for i in range(2)]
        psT = ctx.enter_context(nc.psum_tensor("c_psT", [P, 2, HB, P], F32))
        psO = ctx.enter_context(nc.psum_tensor("c_psO", [P, 512], F32))
        psX = ctx.enter_context(nc.psum_tensor("c_psX", [P, TW], F32))

        per_tile = {"r0": 1, "r1": 2, "q_mm": 2, "q": 2, "s_mm": UNITS, "mx": UNITS, "sub": UNITS,
                    "exp": UNITS, "t_mm": 2 * UNITS, "ta": UNITS, "tv": UNITS, "pv": UNITS, "rec": UNITS,
                    "cx": UNITS, "c_mm": UNITS, "cxT": UNITS, "o_mm": 2}
        per_turn = {"rs": NN2, "mean_mm": NN2, "xc": NN2, "sq": NN2, "ss": NN2, "var_mm": NN2, "guess": 3 * NN2,
                    "newton": NN2, "rstd": NN2, "norm": NN2}
        S = {n: sem("c_" + n) for n in (*per_tile, *per_turn)}
        s_xo = [sem(f"c_xo{t}") for t in range(BT)]
        s_load, s_pre, s_kmm, s_kev, s_kb, s_vmm, s_vev = (sem("c_" + n) for n in
                                                           ("load", "pre", "kmm", "kev", "kb", "vmm", "vev"))
        owners = {"pe": ["q_mm", "s_mm", "t_mm", "pv", "c_mm", "o_mm", "mean_mm", "var_mm"],
                  "act": ["q", "exp", "ta", "cxT", "sq", "guess"],
                  "dve": ["r0", "r1", "mx", "sub", "tv", "rec", "cx", "xc", "newton", "rstd", "norm"],
                  "pool": ["rs", "ss"]}

        def start_counts(eng, who):
            for n in owners[who]:
                eng.sem_inc(S[n], BT * per_tile[n] if n in per_tile else per_turn[n])

        def tile_event(eng, name, L, t, n=None):
            e = per_tile[name]
            eng.wait_ge(S[name], L * (e * BT) + (e * t + (e if n is None else n + 1)))

        def guess_event(eng, L, i, n):
            eng.wait_ge(S["guess"], L * (3 * NN2) + (3 * i + n))

        def norm_event(eng, name, L, i):
            eng.wait_ge(S[name], L * NN2 + (i + 1))

        USES = []
        for step, t, n in ORDER2:
            i = NORMS2.index((n, t)) if step in "MR" else 0
            USES += {"M": [("mean", i, 0, ("xc", i))], "R": [("var", i, 0, ("newton", i))],
                     "Q": [("q", t, m, ("q", t, m)) for m in range(KC)],
                     "C": [("c", t, n, ("cxT", t, n))],
                     "O": [("o", t, m, ("r1", t, m)) for m in range(KC)]}.get(step, [])

        def bank_free(pe, what, a, b, L):
            i = [u[:3] for u in USES].index((what, a, b)) - 1
            name, *at = USES[i][3]
            back = i < 0
            if len(at) == 1:
                norm_event(pe, name, L, at[0] - NN2 * back)
            else:
                tile_event(pe, name, L, at[0] - BT * back, at[1])

        def x_tile(L, t):
            return XF[:, :, bass.ds((L - 1) * SEQ + t * TW, TW)]

        block = ctx.enter_context(nc.Block())

        @block.sync
        def _(sp):
            sp.dma_start(cT[:, :, :], ctx_t.rearrange("(k p) n -> p k n", p=P)).then_inc(s_load, 16)
            sp.dma_start(W[:, :, :, :].rearrange("p w k n -> p (w k n)"), cw).then_inc(s_load, 16)
            sp.dma_start(cvec[:, :, :].rearrange("p v c -> p (v c)"), cvecs).then_inc(s_load, 16)
            with sp.Fori(1, BATCH + 1) as L:
                for t in range(BT):
                    norm_event(sp, "norm", L - 1, NORMS2.index((1, t)))
                    sp.dma_start(B[:, t], x_t.rearrange("(k p) n -> p k n", p=P)[
                        :, :, bass.ds((L - 1) * SEQ + t * TW, TW)]).then_inc(s_xo[t], 16)

        @block.scalar
        def _(act):
            start_counts(act, "act")
            act.wait_ge(s_load, 48)
            act.preload_act_table_set(LOG_EXP)
            for m in range(KC):
                act.wait_ge(s_kmm, m + 1)
                act.activation(kT[:, m, :], psX[:, m * 256:m * 256 + BATCH * KEYS], ACT.Identity,
                               bias=cvec[:, 1, m:m + 1]).then_inc(s_kev, 1)
            with act.Fori(1, BATCH + 1) as L:
                for step, t, n in ORDER2:
                    if step == "M":
                        i = NORMS2.index((n, t))
                        norm_event(act, "xc", L, i)
                        norm_event(act, "ss", L, i - 1)
                        act.activation(SQ[:, :, :], B[:, t], ACT.Square).then_inc(S["sq"], 1)
                    if step == "R":
                        i = NORMS2.index((n, t))
                        norm_event(act, "var_mm", L, i)
                        norm_event(act, "norm", L, i - 1)
                        act.activation(Y0[:, :], psX[:, :], ACT.Ln, bias=consts[:, 1:2]).then_inc(S["guess"], 1)
                        guess_event(act, L, i, 1)
                        act.activation(Y0[:, :], Y0[:, :], ACT.Exp, scale=-0.5).then_inc(S["guess"], 1)
                        guess_event(act, L, i, 2)
                        act.activation(Y2[:, :], Y0[:, :], ACT.Square, scale=0.5 ** 0.5).then_inc(S["guess"], 1)
                    if step == "Q":
                        for m in range(KC):
                            tile_event(act, "q_mm", L, t, m)
                            tile_event(act, "s_mm", L - 1, t)
                            act.activation(q2[:, t, m], psX[:, :], ACT.Identity,
                                           bias=cvec[:, 0, m:m + 1]).then_inc(S["q"], 1)
                    if step == "S":
                        tile_event(act, "sub", L, t, n)
                        act.activation(Pb[:, n % 2], Pb[:, n % 2], ACT.Exp, scale=HD ** -0.5).then_inc(S["exp"], 1)
                    if step == "T":
                        tile_event(act, "t_mm", L, t, 2 * n)
                        tile_event(act, "pv", L, t, n - 2)
                        act.activation(PT[:, n % 2, 0:HB], psT[0:KEYS, 0], ACT.Copy).then_inc(S["ta"], 1)
                    if step == "C":
                        s, c = n // KC, n % KC
                        tile_event(act, "c_mm", L, t, n)
                        tile_event(act, "o_mm", L - 1, t)
                        act.activation(cxT[:, t, c, s * P:(s + 1) * P], psX[:, 0:P], ACT.Identity,
                                       bias=cvec[:, 2, c:c + 1]).then_inc(S["cxT"], 1)

        @block.vector
        def _(dve):
            start_counts(dve, "dve")
            dve.memset(V17[:, :, :, :], 1.0).then_inc(s_pre, 1)
            dve.wait_ge(s_kev, KC)
            for b in range(BATCH):
                for c in range(KC):
                    dve.tensor_tensor(KB[:, b * KC + c],
                                      kT[:, c, None, b * KEYS:(b + 1) * KEYS].to_broadcast([P, HC, KEYS]),
                                      headmask[:, :, None].to_broadcast([P, HC, KEYS]), ALU.mult).then_inc(s_kb, 1)
            dve.wait_ge(s_pre, 1)
            for b in range(BATCH):
                dve.wait_ge(s_vmm, b + 1)
                dve.tensor_copy(V17[:, b, :, 0:HD], psO[0:KEYS, b * D:(b + 1) * D]
                                .rearrange("p (h d) -> p h d", d=HD)).then_inc(s_vev, 1)
            with dve.Fori(1, BATCH + 1) as L:
                for step, t, n in ORDER2:
                    if step == "L":
                        dve.wait_ge(s_xo[t], L * 16)
                        dve.tensor_tensor(B[:, t], x_tile(L, t), B[:, t], ALU.add).then_inc(S["r0"], 1)
                    if step == "M":
                        i = NORMS2.index((n, t))
                        norm_event(dve, "mean_mm", L, i)
                        norm_event(dve, "rs", L, i)
                        dve.tensor_tensor(B[:, t], psX[:, None, :].to_broadcast([P, KC, TW]), B[:, t],
                                          ALU.subtract).then_inc(S["xc"], 1)
                    if step == "R":
                        i = NORMS2.index((n, t))
                        guess_event(dve, L, i, 3)
                        dve.scalar_tensor_tensor(out=Y2[:, :], in0=psX[:, :], scalar=LN_EPS, in1=Y2[:, :],
                                                 op0=ALU.add, op1=ALU.mult).then_inc(S["newton"], 1)
                        norm_event(dve, "newton", L, i)
                        dve.scalar_tensor_tensor(out=Y0[:, :], in0=Y2[:, :], scalar=-1.5, in1=Y0[:, :],
                                                 op0=ALU.add, op1=ALU.mult).then_inc(S["rstd"], 1)
                        norm_event(dve, "rstd", L, i)
                        norm_event(dve, "sq", L, i)
                        out = B[:, t] if n == 0 else x_tile(L, t)
                        dve.tensor_tensor(out, B[:, t], Y0[:, None, :].to_broadcast([P, KC, TW]),
                                          ALU.mult).then_inc(S["norm"], 1)
                    if step == "S":
                        tile_event(dve, "s_mm", L, t, n)
                        ps = psS[n % 2][:, :, 0:HB * KEYS].rearrange("p g (h k) -> p g h k", k=KEYS)
                        m = mx[:, n % 2].rearrange("p (g h) -> p g h", g=2)
                        dve.tensor_reduce(m, ps, AX.X, ALU.max).then_inc(S["mx"], 1)
                        tile_event(dve, "mx", L, t, n)
                        tile_event(dve, "t_mm", L, t, 2 * (n - 2) + 1)
                        dve.tensor_tensor(Pb[:, n % 2].rearrange("p (g h) k -> p g h k", g=2), ps,
                                          m[:, :, :, None].to_broadcast([P, 2, HB, KEYS]),
                                          ALU.subtract).then_inc(S["sub"], 1)
                    if step == "T":
                        tile_event(dve, "t_mm", L, t, 2 * n + 1)
                        tile_event(dve, "pv", L, t, n - 2)
                        dve.tensor_copy(PT[:, n % 2, HB:HC], psT[0:KEYS, 1]).then_inc(S["tv"], 1)
                    if step == "P":
                        o = psO[:, 0:HC * (HD + 1)].rearrange("p (h d) -> p h d", d=HD + 1)
                        tile_event(dve, "pv", L, t, n)
                        tile_event(dve, "cx", L, t, n - 2)
                        dve.reciprocal(rec[:, n % 2], o[:, :, HD]).then_inc(S["rec"], 1)
                        tile_event(dve, "rec", L, t, n)
                        tile_event(dve, "c_mm", L, t, n - 2)
                        dve.tensor_tensor(Cx[:, n % 2], o[:, :, 0:HD],
                                          rec[:, n % 2, :, None].to_broadcast([P, HC, HD]),
                                          ALU.mult).then_inc(S["cx"], 1)
                    if step == "O":
                        for m in range(KC):
                            tile_event(dve, "o_mm", L, t, m)
                            dve.scalar_tensor_tensor(out=B[:, t, m], in0=psX[:, :], scalar=cvec[:, 3, m:m + 1],
                                                     in1=B[:, t, m], op0=ALU.add, op1=ALU.add).then_inc(S["r1"], 1)

        @block.gpsimd
        def _(pool):
            start_counts(pool, "pool")
            with pool.Fori(1, BATCH + 1) as L:
                for step, t, n in ORDER2:
                    if step in ("L", "O"):
                        i = NORMS2.index((n, t))
                        tile_event(pool, f"r{n}", L, t)
                        norm_event(pool, "mean_mm", L, i - 1)
                        pool.tensor_tensor(RS[:, :], B[:, t, 0], B[:, t, 1], ALU.add).then_inc(S["rs"], 1)
                    if step == "M":
                        i = NORMS2.index((n, t))
                        norm_event(pool, "sq", L, i)
                        norm_event(pool, "var_mm", L, i - 1)
                        pool.tensor_tensor(SS[:, :], SQ[:, 0], SQ[:, 1], ALU.add).then_inc(S["ss"], 1)

        @block.tensor
        def _(pe):
            start_counts(pe, "pe")
            pe.wait_ge(s_load, 48)
            for m in range(KC):
                for k in range(KC):
                    mm = pe.matmul(psX[:, m * 256:m * 256 + BATCH * KEYS], W[:, 1, k, m * P:(m + 1) * P], cT[:, k, :],
                                   start=(k == 0), stop=(k == KC - 1))
                mm.then_inc(s_kmm, 1)
                if m == 0:
                    pe.wait_ge(s_kev, 1)
            for b in range(BATCH):
                for k in range(KC):
                    mm = pe.matmul(psO[0:KEYS, b * D:(b + 1) * D], cT[:, k, b * KEYS:(b + 1) * KEYS], W[:, 2, k, :],
                                   start=(k == 0), stop=(k == KC - 1))
                mm.then_inc(s_vmm, 1)
                pe.wait_ge(s_vev, b + 1)
            pe.wait_ge(s_kb, BATCH * KC)
            pe.wait_ge(s_kev, KC)
            with pe.Fori(1, BATCH + 1) as L:
                for step, t, n in ORDER2:
                    s, c = n // KC, n % KC
                    if step == "M":
                        i = NORMS2.index((n, t))
                        norm_event(pe, "rs", L, i)
                        bank_free(pe, "mean", i, 0, L)
                        pe.matmul(psX[:, :], ones_inv[:, :], RS[:, :], start=True, stop=True).then_inc(S["mean_mm"], 1)
                    if step == "R":
                        i = NORMS2.index((n, t))
                        norm_event(pe, "ss", L, i)
                        bank_free(pe, "var", i, 0, L)
                        pe.matmul(psX[:, :], ones_inv[:, :], SS[:, :], start=True, stop=True).then_inc(S["var_mm"], 1)
                    if step in ("Q", "O"):
                        w, src, done = (0, B, "q_mm") if step == "Q" else (3, cxT, "o_mm")
                        if step == "Q":
                            norm_event(pe, "norm", L, NORMS2.index((0, t)))
                        else:
                            tile_event(pe, "cxT", L, t)
                        for m in range(KC):
                            bank_free(pe, step.lower(), t, m, L)
                            for k in range(KC):
                                mm = pe.matmul(psX[:, :], W[:, w, k, m * P:(m + 1) * P], src[:, t, k],
                                               start=(k == 0), stop=(k == KC - 1))
                            mm.then_inc(S[done], 1)
                    if step == "S":
                        tile_event(pe, "q", L, t)
                        tile_event(pe, "sub", L, t, n - 2)
                        for g in range(2):
                            mm = pe.matmul(psS[n % 2][:, g, 0:HB * KEYS], q2[:, t, c, s * P:(s + 1) * P],
                                           KB[:, bass.ds((L - 1) * KC + c, 1), g * HB:(g + 1) * HB, :]
                                           .rearrange("p a h k -> p (a h k)"), start=True, stop=True)
                        mm.then_inc(S["s_mm"], 1)
                    if step == "T":
                        tile_event(pe, "exp", L, t, n)
                        for g in range(2):
                            tile_event(pe, ("ta", "tv")[g], L, t, n - 1)
                            for h in range(HB):
                                mm = pe.transpose(psT[0:KEYS, g, h], Pb[:, n % 2, g * HB + h], ident[:, :])
                            mm.then_inc(S["t_mm"], 1)
                    if step == "P":
                        tile_event(pe, "ta", L, t, n)
                        tile_event(pe, "tv", L, t, n)
                        tile_event(pe, "cx", L, t, n - 1)
                        for h in range(HC):
                            mm = pe.matmul(psO[:, h * (HD + 1):(h + 1) * (HD + 1)], PT[:, n % 2, h],
                                           V17[:, bass.ds(L - 1, 1), c * HC + h, :].rearrange("p a d -> p (a d)"),
                                           start=True, stop=True)
                        mm.then_inc(S["pv"], 1)
                    if step == "C":
                        tile_event(pe, "cx", L, t, n)
                        bank_free(pe, "c", t, n, L)
                        pe.transpose(psX[:, 0:P], Cx[:, n % 2].rearrange("p h d -> p (h d)"),
                                     ident[:, :]).then_inc(S["c_mm"], 1)


CAP = SEQ // 8
assert CAP == P
ST = SEQ // P
DFF = D * 4 * 2 // 3
DC = -(-DFF // P)
CR = BATCH * CAP
NEG = -1e30


def routed_stage(nc, sem, XF, ones_inv, consts, ident, headmask, x_out, fvecs, f_qkv, f_out, f_w12, f_w3):
    with ExitStack() as ctx:
        def sb(name, shape, dt=F32):
            return ctx.enter_context(nc.sbuf_tensor("f_" + name, shape, dt))

        fvec = sb("vec", [P, 3, KC])
        ng = sb("ng", [P, 2, KC])
        Wqkv = sb("Wqkv", [P, KC, 3 * D])
        Wout = sb("Wout", [P, KC, D])
        W12 = sb("W12", [P, 2, KC, DFF])
        W3 = sb("W3", [P, DC, D])
        wr = sb("wr", [P, KC, P])
        iota = sb("iota", [P, P])
        causal = sb("causal", [P, P])
        before = sb("before", [P, P])
        Srow = sb("Srow", [P, BATCH, SEQ])
        tmp = sb("tmp", [P, SEQ])
        scol = sb("scol", [P, BATCH, ST])
        cnt = sb("cnt", [P, BATCH, ST, 3])
        rank = sb("rank", [P, BATCH, ST])
        OH = sb("OH", [P, BATCH, ST, P])
        OHT = sb("OHT", [P, BATCH, SEQ])
        xN = sb("xN", [P, BATCH * ST, D])
        xs = sb("xs", [P, KC, CR])
        sq = sb("sq", [P, KC, CR])
        y0, y2 = sb("y0", [P, CR]), sb("y2", [P, CR])
        hT = sb("hT", [P, KC, CR])
        qT = sb("qT", [P, KC, CR])
        KB = sb("KB", [P, BATCH, KC, HC, P])
        V17 = sb("V17", [P, BATCH, HEADS, HD + 1])
        Pb = sb("Pb", [P, 2, HC, P])
        PT = sb("PT", [P, 2, HC, P])
        mx, rec = sb("mx", [P, 4, HC]), sb("rec", [P, 4, HC])
        Cx = sb("Cx", [P, 4, HC, HD])
        oT = sb("oT", [P, KC, CR])
        x1 = sb("x1", [P, KC, CR])
        sg = sb("sg", [P, DC, CR])
        dN = sb("dN", [P, BATCH, D])
        R = sb("R", [P, 2, KC, TW])
        RS, SS = sb("RS", [P, TW]), sb("SS", [P, TW])
        Z0, Z2 = sb("Z0", [P, TW]), sb("Z2", [P, TW])

        psS = [ctx.enter_context(nc.psum_tensor(f"f_psS{i}", [P, 2, 512], F32)) for i in range(2)]
        psT = ctx.enter_context(nc.psum_tensor("f_psT", [P, 2, 512], F32))
        psO = ctx.enter_context(nc.psum_tensor("f_psO", [P, 512], F32))
        psX = ctx.enter_context(nc.psum_tensor("f_psX", [P, 512], F32))

        names = ("vec w c_pool c_ng c_wr s_mm srow prod scol cnt rank oh xt_mm xn g_mm xs oht_mm oht "
                 "sq m_mm guess nw rs h qkv_mm q kb v sc_mm msk mx sub exp t_mm ta tv pv rec cx c_mm ot a_mm x1 "
                 "f1_mm f2_mm sil g d_mm d sct r rsum mean xc sqr ss var guess2 znw zrs out st").split()
        S = {n: sem("f_" + n) for n in names}

        NU = BATCH * KC
        block = ctx.enter_context(nc.Block())

        @block.sync
        def _(sp):
            sp.dma_start(fvec[:, :, :].rearrange("p v c -> p (v c)"), fvecs).then_inc(S["vec"], 16)
            sp.dma_start(Wqkv[:, :, :].rearrange("p k n -> p (k n)"), f_qkv).then_inc(S["w"], 16)
            sp.dma_start(Wout[:, :, :].rearrange("p k n -> p (k n)"), f_out).then_inc(S["w"], 16)
            sp.dma_start(W12[:, :, :, :].rearrange("p w k n -> p (w k n)"), f_w12).then_inc(S["w"], 16)
            sp.dma_start(W3[:, 0:DC - 1, :], f_w3[0:(DC - 1) * P, :].rearrange("(k p) n -> p k n", p=P)) \
                .then_inc(S["w"], 16)
            sp.dma_start(W3[0:DFF - (DC - 1) * P, DC - 1, :], f_w3[(DC - 1) * P:DFF, :]).then_inc(S["w"], 16)
            for t in range(TILES):
                sp.wait_ge(S["out"], t + 1)
                sp.dma_start(x_out.rearrange("(k p) n -> p k n", p=P)[:, :, t * TW:(t + 1) * TW],
                             R[:, t % 2]).then_inc(S["st"], 16)
                if t >= 1:
                    sp.wait_ge(S["st"], 16 * t)
            sp.wait_ge(S["st"], 16 * TILES)

        @block.gpsimd
        def _(pool):
            pool.iota(iota[:, :], pattern=[[1, P]], base=0, channel_multiplier=0,
                      allow_small_or_imprecise_dtypes=True).then_inc(S["c_pool"], 1)
            pool.memset(causal[:, :], 0.0).then_inc(S["c_pool"], 1)
            pool.memset(before[:, :], 1.0).then_inc(S["c_pool"], 1)
            pool.memset(V17[:, :, :, :], 1.0).then_inc(S["c_pool"], 1)
            pool.wait_ge(S["c_pool"], 4)
            pool.affine_select(out=causal[:, :], in_=causal[:, :], compare_op=ALU.is_ge, fill=NEG, base=0,
                               pattern=[[-1, P]], channel_multiplier=1).then_inc(S["c_pool"], 1)
            pool.affine_select(out=before[:, :], in_=before[:, :], compare_op=ALU.is_ge, fill=0.0, base=-1,
                               pattern=[[-1, P]], channel_multiplier=1).then_inc(S["c_pool"], 1)
            for t in range(TILES):
                pool.wait_ge(S["r"], 2 * t + 2)
                if t:
                    pool.wait_ge(S["mean"], t)
                pool.tensor_tensor(RS[:, :], R[:, t % 2, 0], R[:, t % 2, 1], ALU.add).then_inc(S["rsum"], 1)
                pool.wait_ge(S["sqr"], t + 1)
                if t:
                    pool.wait_ge(S["var"], t)
                pool.tensor_tensor(SS[:, :], tmp[:, 0:TW], tmp[:, TW:2 * TW], ALU.add).then_inc(S["ss"], 1)

        @block.scalar
        def _(act):
            act.preload_act_table_set(LOG_EXP)
            for b in range(BATCH):
                act.wait_ge(S["s_mm"], b + 1)
                act.activation(Srow[:, b].rearrange("p (g n) -> p g n", g=2), psS[b][:, :, :],
                               ACT.Copy).then_inc(S["srow"], 1)
            for i in range(BATCH * ST // 2):
                act.wait_ge(S["xt_mm"], i + 1)
                act.activation(xN[:, 2 * i:2 * i + 2, :].rearrange("p t n -> p (t n)"), psT[:, i % 2],
                               ACT.Copy).then_inc(S["xn"], 1)
            act.wait_ge(S["g_mm"], NU)
            act.activation(xs[:, :, :].rearrange("p c n -> p (c n)"), psO[:, :], ACT.Copy).then_inc(S["xs"], 1)
            for norm in range(2):
                src, ready, k = ((xs, "xs", 1), (x1, "x1", KC))[norm]
                act.wait_ge(S[ready], k)
                if norm:
                    act.wait_ge(S["m_mm"], norm)
                act.activation(sq[:, :, :], src[:, :, :], ACT.Square).then_inc(S["sq"], 1)
                act.wait_ge(S["m_mm"], norm + 1)
                ps = (psX, psO)[norm][:, 0:CR]
                if norm:
                    act.wait_ge(S["h"], KC * norm)
                act.activation(y0[:, :], ps, ACT.Ln, bias=consts[:, 0:1]).then_inc(S["guess"], 1)
                act.wait_ge(S["guess"], 3 * norm + 1)
                act.activation(y0[:, :], y0[:, :], ACT.Exp, scale=-0.5).then_inc(S["guess"], 1)
                act.wait_ge(S["guess"], 3 * norm + 2)
                act.activation(y2[:, :], y0[:, :], ACT.Square, scale=0.5 ** 0.5).then_inc(S["guess"], 1)
                if norm:
                    break
                for b in range(BATCH):
                    act.wait_ge(S["oht_mm"], b + 1)
                    act.activation(OHT[:, b].rearrange("p (g n) -> p g n", g=2), psS[b][:, :, :],
                                   ACT.Copy).then_inc(S["oht"], 1)
                act.wait_ge(S["qkv_mm"], 1)
                act.activation(qT[:, :, :].rearrange("p c n -> p (c n)"), psT[:, 0], ACT.Copy).then_inc(S["q"], 1)
                for i in range(NU + 2):
                    if i < NU:
                        act.wait_ge(S["sub"], i + 1)
                        act.activation(Pb[:, i % 2], Pb[:, i % 2], ACT.Exp, scale=HD ** -0.5).then_inc(S["exp"], 1)
                        act.wait_ge(S["t_mm"], 2 * i + 1)
                        if i >= 2:
                            act.wait_ge(S["pv"], i - 1)
                        act.activation(PT[:, i % 2, 0:HB].rearrange("p h n -> p (h n)"), psT[:, 0],
                                       ACT.Copy).then_inc(S["ta"], 1)
                    if i >= 2:
                        j = i - 2
                        b, c = j // KC, j % KC
                        act.wait_ge(S["c_mm"], j + 1)
                        act.activation(oT[:, c, b * P:(b + 1) * P], psX[:, 0:P], ACT.Copy).then_inc(S["ot"], 1)
            act.preload_act_table_set(SILU)
            for k in range(DC):
                w = min(P, DFF - k * P)
                act.wait_ge(S["f1_mm"], k // 2 * 2 + 2)
                act.activation(sg[0:w, k], (psS[0][0:w, k // 2, (k % 2) * CR:(k % 2 + 1) * CR] if k < 4 else
                                            psT[0:w, 0, (k % 2) * CR:(k % 2 + 1) * CR]),
                               ACT.Silu).then_inc(S["sil"], 1)
            act.preload_act_table_set(LOG_EXP)
            act.wait_ge(S["d_mm"], 1)
            act.activation(dN[:, :, :].rearrange("p b n -> p (b n)"), psO[:, :], ACT.Copy).then_inc(S["d"], 1)
            for t in range(TILES):
                act.wait_ge(S["xc"], t + 1)
                if t:
                    act.wait_ge(S["ss"], t)
                act.activation(tmp[:, :].rearrange("p (c n) -> p c n", c=KC), R[:, t % 2],
                               ACT.Square).then_inc(S["sqr"], 1)
                act.wait_ge(S["var"], t + 1)
                if t:
                    act.wait_ge(S["out"], t)
                act.activation(Z0[:, :], psX[:, :], ACT.Ln, bias=consts[:, 1:2]).then_inc(S["guess2"], 1)
                act.wait_ge(S["guess2"], 3 * t + 1)
                act.activation(Z0[:, :], Z0[:, :], ACT.Exp, scale=-0.5).then_inc(S["guess2"], 1)
                act.wait_ge(S["guess2"], 3 * t + 2)
                act.activation(Z2[:, :], Z0[:, :], ACT.Square, scale=0.5 ** 0.5).then_inc(S["guess2"], 1)

        @block.vector
        def _(dve):
            dve.wait_ge(S["vec"], 16)
            dve.tensor_copy(wr[:, :, :], fvec[:, 0, :, None].to_broadcast([P, KC, P])).then_inc(S["c_wr"], 1)
            dve.tensor_scalar(ng[:, :, :], fvec[:, 1:3, :], -1.0, None, ALU.mult).then_inc(S["c_ng"], 1)
            dve.memset(cnt[:, :, :, :], 0.0).then_inc(S["cnt"], 1)
            n_cnt = 1

            dve.wait_ge(S["c_pool"], 6)
            for b in range(BATCH):
                dve.wait_ge(S["srow"], b + 1)
                if n_cnt > 1:
                    dve.wait_ge(S["cnt"], n_cnt)
                row = Srow[:, b].rearrange("p (t n) -> p t n", n=P)
                t3 = tmp[:, :].rearrange("p (t n) -> p t n", n=P)
                dve.tensor_tensor(t3, row, ident[:, None, :].to_broadcast([P, ST, P]), ALU.mult).then_inc(S["prod"], 1)
                dve.wait_ge(S["prod"], b + 1)
                dve.tensor_reduce(scol[:, b], t3, AX.X, ALU.add).then_inc(S["scol"], 1)
                dve.wait_ge(S["scol"], b + 1)
                for t in range(ST):
                    s = scol[:, b, t:t + 1]
                    for part, lo, hi, op, mask in ((0, 0, t * P, ALU.is_ge, None), (1, t * P, SEQ, ALU.is_gt, None),
                                                   (2, t * P, (t + 1) * P, ALU.is_equal, before)):
                        if lo == hi:
                            continue
                        in1 = iota[:, 1:2].to_broadcast([P, hi - lo]) if mask is None else mask[:, :]
                        dve.wait_ge(S["cnt"], n_cnt)
                        dve.scalar_tensor_tensor(out=tmp[:, 0:hi - lo], in0=Srow[:, b, lo:hi], scalar=s, in1=in1,
                                                 op0=op, op1=ALU.mult,
                                                 accum_out=cnt[:, b, t, part:part + 1]).then_inc(S["cnt"], 1)
                        n_cnt += 1
                dve.wait_ge(S["cnt"], n_cnt)
                dve.tensor_reduce(rank[:, b], cnt[:, b], AX.X, ALU.add).then_inc(S["rank"], 1)
                dve.wait_ge(S["rank"], b + 1)
                dve.tensor_tensor(OH[:, b], iota[:, None, :].to_broadcast([P, ST, P]),
                                  rank[:, b, :, None].to_broadcast([P, ST, P]), ALU.is_equal).then_inc(S["oh"], 1)

            def rms(norm, src):
                ps = (psX, psO)[norm][:, 0:CR]
                dve.wait_ge(S["guess"], 3 * norm + 3)
                dve.scalar_tensor_tensor(out=y2[:, :], in0=ps, scalar=ATTN_LN_EPS, in1=y2[:, :], op0=ALU.add,
                                         op1=ALU.mult).then_inc(S["nw"], 1)
                dve.wait_ge(S["nw"], norm + 1)
                dve.scalar_tensor_tensor(out=y0[:, :], in0=y2[:, :], scalar=-1.5, in1=y0[:, :], op0=ALU.add,
                                         op1=ALU.mult).then_inc(S["rs"], 1)
                dve.wait_ge(S["rs"], norm + 1)
                dve.wait_ge(S["c_ng"], 1)
                if norm:
                    dve.wait_ge(S["qkv_mm"], 4)
                for c in range(KC):
                    dve.scalar_tensor_tensor(out=hT[:, c], in0=src[:, c], scalar=ng[:, norm, c:c + 1], in1=y0[:, :],
                                             op0=ALU.mult, op1=ALU.mult).then_inc(S["h"], 1)

            rms(0, xs)
            dve.wait_ge(S["qkv_mm"], 2)
            for b in range(BATCH):
                for c in range(KC):
                    dve.tensor_tensor(KB[:, b, c],
                                      psT[:, 1, None, c * CR + b * P:c * CR + (b + 1) * P].to_broadcast([P, HC, P]),
                                      headmask[:, :, None].to_broadcast([P, HC, P]), ALU.mult).then_inc(S["kb"], 1)
            dve.wait_ge(S["qkv_mm"], 4)
            for b in range(BATCH):
                dve.tensor_copy(V17[:, b, :, 0:HD], psO[:, b * D:(b + 1) * D].rearrange("p (h d) -> p h d", d=HD)) \
                    .then_inc(S["v"], 1)
            for i in range(NU + 1):
                if i < NU:
                    dve.wait_ge(S["sc_mm"], i + 1)
                    if i >= 2:
                        dve.wait_ge(S["t_mm"], 2 * (i - 1))
                    ps = psS[i % 2][:, :, :].rearrange("p g (h k) -> p (g h) k", k=P)
                    dve.tensor_tensor(Pb[:, i % 2], ps, causal[:, None, :].to_broadcast([P, HC, P]),
                                      ALU.add).then_inc(S["msk"], 1)
                    dve.wait_ge(S["msk"], i + 1)
                    dve.tensor_reduce(mx[:, i], Pb[:, i % 2], AX.X, ALU.max).then_inc(S["mx"], 1)
                    dve.wait_ge(S["mx"], i + 1)
                    dve.tensor_tensor(Pb[:, i % 2], Pb[:, i % 2], mx[:, i, :, None].to_broadcast([P, HC, P]),
                                      ALU.subtract).then_inc(S["sub"], 1)
                if i >= 1:
                    j = i - 1
                    dve.wait_ge(S["t_mm"], 2 * j + 2)
                    if j >= 2:
                        dve.wait_ge(S["pv"], j - 1)
                    dve.tensor_copy(PT[:, j % 2, HB:HC].rearrange("p h n -> p (h n)"), psT[:, 1]) \
                        .then_inc(S["tv"], 1)
                    dve.wait_ge(S["pv"], j + 1)
                    o = psO[:, 0:HC * (HD + 1)].rearrange("p (h d) -> p h d", d=HD + 1)
                    dve.reciprocal(rec[:, j], o[:, :, HD]).then_inc(S["rec"], 1)
                    dve.wait_ge(S["rec"], j + 1)
                    dve.tensor_tensor(Cx[:, j], o[:, :, 0:HD], rec[:, j, :, None].to_broadcast([P, HC, HD]),
                                      ALU.mult).then_inc(S["cx"], 1)
            dve.wait_ge(S["a_mm"], 1)
            dve.tensor_tensor(x1[:, 0], psX[:, 0:CR], xs[:, 0], ALU.add).then_inc(S["x1"], 1)
            dve.tensor_tensor(x1[:, 1], psX[:, CR:2 * CR], xs[:, 1], ALU.add).then_inc(S["x1"], 1)
            rms(1, x1)
            for k in range(DC):
                w = min(P, DFF - k * P)
                dve.wait_ge(S["sil"], k + 1)
                dve.wait_ge(S["f2_mm"], k // 2 * 2 + 2)
                ps = (psS[1][0:w, k // 2, (k % 2) * CR:(k % 2 + 1) * CR] if k < 4 else
                      psX[0:w, (k % 2) * CR:(k % 2 + 1) * CR])
                dve.tensor_tensor(sg[0:w, k], sg[0:w, k], ps, ALU.mult).then_inc(S["g"], 1)
            for i in range(TILES + 1):
                if i < TILES:
                    t = i
                    for c in range(KC):
                        dve.wait_ge(S["sct"], 2 * t + c + 1)
                        if t >= 2:
                            dve.wait_ge(S["st"], 16 * (t - 1))
                        dve.scalar_tensor_tensor(out=R[:, t % 2, c], in0=XF[:, c, t * TW:(t + 1) * TW], scalar=2.0,
                                                 in1=psS[t % 2][:, c], op0=ALU.mult, op1=ALU.add).then_inc(S["r"], 1)
                if i >= 1:
                    t = i - 1
                    dve.wait_ge(S["guess2"], 3 * t + 3)
                    dve.scalar_tensor_tensor(out=Z2[:, :], in0=psX[:, :], scalar=LN_EPS, in1=Z2[:, :], op0=ALU.add,
                                             op1=ALU.mult).then_inc(S["znw"], 1)
                    dve.wait_ge(S["znw"], t + 1)
                    dve.scalar_tensor_tensor(out=Z0[:, :], in0=Z2[:, :], scalar=-1.5, in1=Z0[:, :], op0=ALU.add,
                                             op1=ALU.mult).then_inc(S["zrs"], 1)
                    dve.wait_ge(S["zrs"], t + 1)
                    dve.tensor_tensor(R[:, t % 2], R[:, t % 2], Z0[:, None, :].to_broadcast([P, KC, TW]),
                                      ALU.mult).then_inc(S["out"], 1)
                if i < TILES:
                    dve.wait_ge(S["mean"], i + 1)
                    dve.tensor_tensor(R[:, i % 2], psT[:, 0, None, :].to_broadcast([P, KC, TW]), R[:, i % 2],
                                      ALU.subtract).then_inc(S["xc"], 1)

        @block.tensor
        def _(pe):
            pe.wait_ge(S["c_wr"], 1)
            for b in range(BATCH):
                for g in range(2):
                    cols = slice(b * SEQ + g * TW, b * SEQ + (g + 1) * TW)
                    for k in range(KC):
                        mm = pe.matmul(psS[b][:, g], wr[:, k], XF[:, k, cols], start=(k == 0), stop=(k == KC - 1))
                mm.then_inc(S["s_mm"], 1)
            for i in range(BATCH * ST // 2):
                if i >= 2:
                    pe.wait_ge(S["xn"], i - 1)
                for t in (2 * i, 2 * i + 1):
                    for c in range(KC):
                        o = (t % 2) * D + c * P
                        mm = pe.transpose(psT[:, i % 2, o:o + P], XF[:, c, t * P:(t + 1) * P], ident[:, :])
                mm.then_inc(S["xt_mm"], 1)
            for b in range(BATCH):
                pe.wait_ge(S["oh"], b + 1)
                pe.wait_ge(S["xn"], (b + 1) * ST // 2)
                pe.wait_ge(S["srow"], b + 1)
                for c in range(KC):
                    for t in range(ST):
                        mm = pe.matmul(psO[:, c * CR + b * P:c * CR + (b + 1) * P],
                                       xN[:, b * ST + t, c * P:(c + 1) * P], OH[:, b, t], start=(t == 0),
                                       stop=(t == ST - 1))
                    mm.then_inc(S["g_mm"], 1)
                for t in range(ST):
                    mm = pe.transpose(psS[b][:, t // 4, (t % 4) * P:(t % 4 + 1) * P], OH[:, b, t], ident[:, :])
                mm.then_inc(S["oht_mm"], 1)

            def mean_square(norm):
                pe.wait_ge(S["sq"], norm + 1)
                for k in range(KC):
                    mm = pe.matmul((psX, psO)[norm][:, 0:CR], ones_inv[:, :], sq[:, k], start=(k == 0),
                                   stop=(k == KC - 1))
                mm.then_inc(S["m_mm"], 1)

            mean_square(0)
            pe.wait_ge(S["w"], 80)
            pe.wait_ge(S["h"], KC)
            pe.wait_ge(S["xn"], BATCH * ST // 2)
            for part in range(2):
                for m in range(KC):
                    for k in range(KC):
                        mm = pe.matmul(psT[:, part, m * CR:(m + 1) * CR],
                                       Wqkv[:, k, part * D + m * P:part * D + (m + 1) * P], hT[:, k], start=(k == 0),
                                       stop=(k == KC - 1))
                mm.then_inc(S["qkv_mm"], 1)
            for b in range(BATCH):
                for k in range(KC):
                    mm = pe.matmul(psO[:, b * D:(b + 1) * D], hT[:, k, b * P:(b + 1) * P], Wqkv[:, k, 2 * D:3 * D],
                                   start=(k == 0), stop=(k == KC - 1))
                mm.then_inc(S["qkv_mm"], 1)
            for i in range(NU + 3):
                if i < NU:
                    b, c = i // KC, i % KC
                    if i == 0:
                        pe.wait_ge(S["q"], 1)
                        pe.wait_ge(S["oht"], BATCH)
                    pe.wait_ge(S["kb"], i + 1)
                    if i >= 2:
                        pe.wait_ge(S["msk"], i - 1)
                    for g in range(2):
                        mm = pe.matmul(psS[i % 2][:, g], qT[:, c, b * P:(b + 1) * P],
                                       KB[:, b, c, g * HB:(g + 1) * HB].rearrange("p h k -> p (h k)"), start=True,
                                       stop=True)
                    mm.then_inc(S["sc_mm"], 1)
                if 1 <= i <= NU:
                    j = i - 1
                    b, c = j // KC, j % KC
                    pe.wait_ge(S["exp"], j + 1)
                    if j == 0:
                        pe.wait_ge(S["kb"], NU)
                    for g in range(2):
                        if j:
                            pe.wait_ge(S[("ta", "tv")[g]], j)
                        for h in range(HB):
                            mm = pe.transpose(psT[:, g, h * P:(h + 1) * P], Pb[:, j % 2, g * HB + h], ident[:, :])
                        mm.then_inc(S["t_mm"], 1)
                    pe.wait_ge(S["ta"], j + 1)
                    pe.wait_ge(S["tv"], j + 1)
                    pe.wait_ge(S["v"], BATCH)
                    if j:
                        pe.wait_ge(S["cx"], j)
                    for h in range(HC):
                        mm = pe.matmul(psO[:, h * (HD + 1):(h + 1) * (HD + 1)], PT[:, j % 2, h],
                                       V17[:, b, c * HC + h], start=True, stop=True)
                    mm.then_inc(S["pv"], 1)
                if i >= 2 and i - 2 < NU:
                    j = i - 2
                    pe.wait_ge(S["cx"], j + 1)
                    pe.wait_ge(S["rs"], 1)
                    if j:
                        pe.wait_ge(S["ot"], j)
                    pe.transpose(psX[:, 0:P], Cx[:, j].rearrange("p h d -> p (h d)"), ident[:, :]) \
                        .then_inc(S["c_mm"], 1)
            pe.wait_ge(S["ot"], NU)
            for m in range(KC):
                for k in range(KC):
                    mm = pe.matmul(psX[:, m * CR:(m + 1) * CR], Wout[:, k, m * P:(m + 1) * P], oT[:, k],
                                   start=(k == 0), stop=(k == KC - 1))
            mm.then_inc(S["a_mm"], 1)
            mean_square(1)
            pe.wait_ge(S["h"], 2 * KC)
            pe.wait_ge(S["x1"], KC)
            for k in range(DC):
                w = min(P, DFF - k * P)
                for part, name in ((0, "f1_mm"), (1, "f2_mm")):
                    ps = (psS[part][0:w, k // 2, (k % 2) * CR:(k % 2 + 1) * CR] if k < 4 else
                          (psT[0:w, 0], psX[0:w])[part][:, (k % 2) * CR:(k % 2 + 1) * CR])
                    for j in range(KC):
                        mm = pe.matmul(ps, W12[:, part, j, k * P:k * P + w], hT[:, j], start=(j == 0),
                                       stop=(j == KC - 1))
                    mm.then_inc(S[name], 1)
            pe.wait_ge(S["rs"], 2)
            for b in range(BATCH):
                for k in range(KC):
                    pe.matmul(psO[:, b * D:(b + 1) * D], oT[:, k, b * P:(b + 1) * P], Wout[:, k, :], start=(k == 0),
                              stop=False)
                for k in range(DC):
                    w = min(P, DFF - k * P)
                    pe.wait_ge(S["g"], k + 1)
                    mm = pe.matmul(psO[:, b * D:(b + 1) * D], sg[0:w, k, b * P:(b + 1) * P], W3[0:w, k, :],
                                   start=False, stop=(k == DC - 1))
            mm.then_inc(S["d_mm"], 1)
            pe.wait_ge(S["d"], 1)
            for i in range(TILES + 2):
                if i < TILES:
                    b, t = i // BT, i
                    for c in range(KC):
                        if t >= 2:
                            pe.wait_ge(S["r"], 2 * (t - 2) + c + 1)
                        pe.matmul(psS[t % 2][:, c], dN[:, b, c * P:(c + 1) * P],
                                  OHT[:, b, (t % BT) * TW:(t % BT + 1) * TW], start=True,
                                  stop=True).then_inc(S["sct"], 1)
                if 1 <= i <= TILES:
                    t = i - 1
                    pe.wait_ge(S["rsum"], t + 1)
                    if t:
                        pe.wait_ge(S["xc"], t)
                    pe.matmul(psT[:, 0], ones_inv[:, :], RS[:, :], start=True, stop=True).then_inc(S["mean"], 1)
                    pe.wait_ge(S["ss"], t + 1)
                    if t:
                        pe.wait_ge(S["znw"], t)
                    pe.matmul(psX[:, :], ones_inv[:, :], SS[:, :], start=True, stop=True).then_inc(S["var"], 1)


def constants(nc, sem, ones_inv, consts):
    s = sem("const")
    with nc.Block() as block:
        @block.gpsimd
        def _(pool):
            pool.memset(ones_inv[:, :], 1.0 / D).then_inc(s, 1)
            pool.memset(consts[:, 0:1], ATTN_LN_EPS).then_inc(s, 1)
            pool.memset(consts[:, 1:2], LN_EPS).then_inc(s, 1)
            pool.wait_ge(s, 3)


def head_constants(nc, sem, ident, headmask):
    s = sem("headconst")
    with nc.Block() as block:
        @block.gpsimd
        def _(pool):
            pool.memset(ident[:, :], 0.0).then_inc(s, 1)
            pool.memset(headmask[:, :], 1.0).then_inc(s, 1)
            pool.wait_ge(s, 2)
            pool.affine_select(out=ident[:, :], in_=ident[:, :], compare_op=ALU.not_equal, fill=1.0, base=0,
                               pattern=[[-1, P]], channel_multiplier=1).then_inc(s, 1)
            pool.affine_select(out=headmask[:, :], in_=headmask[:, :], compare_op=ALU.is_ge, fill=0.0, base=0,
                               pattern=[[-HD, HC]], channel_multiplier=1).then_inc(s, 1)
            pool.wait_ge(s, 4)
            pool.affine_select(out=headmask[:, :], in_=headmask[:, :], compare_op=ALU.is_ge, fill=0.0, base=HD - 1,
                               pattern=[[HD, HC]], channel_multiplier=-1).then_inc(s, 1)
            pool.wait_ge(s, 5)


def program(nc, x_t, vecs, w_qkvo, w1, w2, ctx_t, cvecs, cw, fvecs, f_qkv, f_out, f_w12, f_w3, out_t):
    with ExitStack() as ctx:
        def sem(name):
            return ctx.enter_context(nc.semaphore(name))

        def sb(name, shape):
            return ctx.enter_context(nc.sbuf_tensor(name, shape, F32))

        XF = sb("XF", [P, KC, TOKENS])
        ones_inv, consts = sb("ones_inv", [P, P]), sb("consts", [P, 2])
        constants(nc, sem, ones_inv, consts)
        layers_stage(nc, sem, XF, ones_inv, consts, x_t, vecs, w_qkvo, w1, w2)
        ident, headmask = sb("ident", [P, P]), sb("headmask", [P, HC])
        head_constants(nc, sem, ident, headmask)
        cross_stage(nc, sem, XF, ones_inv, consts, ident, headmask, x_t, ctx_t, cvecs, cw)
        routed_stage(nc, sem, XF, ones_inv, consts, ident, headmask, out_t, fvecs, f_qkv, f_out, f_w12, f_w3)


def kernel(**inputs):
    import numpy as np
    import concourse.bacc as bacc
    from concourse import mybir as _mybir
    from concourse.bass_utils import run_bass_kernel_spmd

    i = {k: np.asarray(v) for k, v in inputs.items()}
    a = lambda n: i["L0_attn_" + n]
    x = lambda n: i["L0_xattn_" + n]
    f = lambda n: i["L0_ffn_" + n]

    def per_feature(v):
        return np.moveaxis(v.reshape(*v.shape[:-1], -1, P), -1, 0)

    def rows_in(w):
        return np.moveaxis(w.reshape(*w.shape[:-2], -1, P, w.shape[-1]), -2, -3)

    arrays = {
        "x_t": i["x"].reshape(TOKENS, D).T,
        "vecs": np.concatenate([per_feature(a(n)) for n in ("bq", "bk", "bv", "bo", "ln1_s", "ln1_b", "b1", "b2",
                                                            "ln2_s", "ln2_b")], axis=2).reshape(P, -1),
        "w_qkvo": np.stack([rows_in(a(n)) for n in ("Wq", "Wk", "Wv", "Wo")], axis=2).reshape(LAYERS * P, -1),
        "w1": rows_in(a("W1")).reshape(LAYERS * P, -1),
        "w2": rows_in(a("W2")).reshape(LAYERS * P, -1),
        "ctx_t": i["ctx_1024"].reshape(BATCH * KEYS, D).T,
        "cvecs": per_feature(np.stack([x(n) for n in ("bq", "bk", "bv", "bo")])).reshape(P, -1),
        "cw": np.stack([rows_in(x(n).T) for n in ("Wq", "Wk", "Wv", "Wo")], axis=1).reshape(P, -1),
        "fvecs": per_feature(np.stack([f(n) for n in ("w_router", "g1", "g2")])).reshape(P, -1),
        "f_qkv": rows_in(f("W_qkv").T).reshape(P, -1),
        "f_out": rows_in(f("W_out").T).reshape(P, -1),
        "f_w12": np.stack([rows_in(f(n).T) for n in ("W1", "W2")], axis=1).reshape(P, -1),
        "f_w3": f("W3").T,
    }
    arrays = {k: np.ascontiguousarray(v) for k, v in arrays.items()}
    nc = bacc.Bacc("TRN2", target_bir_lowering=False, num_devices=1)
    args = {k: nc.dram_tensor(k, v.shape, _mybir.dt.from_np(v.dtype), kind="ExternalInput").ap()
            for k, v in arrays.items()}
    args["out_t"] = nc.dram_tensor("out_t", (D, TOKENS), F32, kind="ExternalOutput").ap()
    program(nc, **args)
    r = run_bass_kernel_spmd(nc, [arrays], core_ids=[0])
    return np.ascontiguousarray(r.results[0]["out_t"].T).reshape(BATCH, SEQ, D)
```

```python
from contextlib import ExitStack

import concourse.bass as bass
from concourse import mybir

F32 = mybir.dt.float32
F32R = mybir.dt.float32r
ALU = mybir.AluOpType
ACT = mybir.ActivationFunctionType
AX = mybir.AxisListType

P = 128
BATCH, SEQ, D = 2, 1024, 256
TOKENS = BATCH * SEQ
LAYERS = 4
FF = 1024
KC = D // P
FC = FF // P
TW = 512
TILES = TOKENS // TW
ATTN_LN_EPS = 1e-6
LN_EPS = 1e-5
LOG_EXP, GELU, SILU = "natural_log_exp_and_others", "gelu_apprx_tanh_and_others", "silu_and_others"

_PARTS = (("bq", KC), ("bk", KC), ("bv", KC), ("bo", KC), ("ln1_s", KC), ("ln1_b", KC),
          ("b1", FC), ("b2", KC), ("ln2_s", KC), ("ln2_b", KC))
VEC = {name: sum(n for _, n in _PARTS[:i]) for i, (name, _) in enumerate(_PARTS)}
NVEC = sum(n for _, n in _PARTS)

def steps_of(text):
    return [(w.rstrip("+")[:-1], int(w.rstrip("+")[-1]), int(w[-1] == "+")) for w in text.split()]


PE_ORDER = steps_of("""
    M20 U21 D01 R20 D11 O2 U31 D21 O3 M12 D31 R1a2 M13 Ak0+ Aq0+ M21 R1a3 U02 U12 U22 R21 U32 D02 Av0+ D12
    Ak1+ D22 D32 Av1+ U03 U13 U23 M22 Aq1+ U33 D03 O0+ D13 R22 D23 M10+ D33 O1+ R1a0+ M11+ Ak2+ R1a1+ M23
    Av2+ U00+ U10+ U20+ R23 Aq2+ U30+ D00+ D10+ Ak3+ Av3+ D20+ D30+ U01+ U11+ Aq3+
    """)
ACT_ORDER = steps_of("""
    X0+ WQ0+ O3 M12 T1 R1a2 WO0+ M13 Ak0+ R1b2 Aq0+ R1a3 M21 U02 U12 R21 U22 X1+ R1b3 U32 Ak1+ T2 U03 Va0+
    U13 U23 Aq1+ Vb0+ M22 W10+ Va1+ O0+ U33 Vb1+ R22 M10+ T3 X2+ O1+ R1a0+ W20+ M11+ Ak2+ R1b0+ R1a1+ U00+
    M23 U10+ U20+ R23 Aq2+ X3+ R1b1+ U30+ Ak3+ Va2+ T0+ U01+ U11+ Aq3+ M20+ Vb2+ Va3+ R20+ U21+ Vb3+ O2+ U31+
    """)
DVE_ORDER = steps_of("""
    Av3 Va2 Vc2 T0 VN0 U01 U11 M20 Aq3 Va3 Vc3 U21 R20 O2 U31 M12 O3 WQ0+ VA0+ T1 M13 R1a2 Ak0+ M21 Aq0+ U02
    R1a3 VN2 U12 R21 Av0+ U22 WO0+ U32 Ak1+ Av1+ Va0+ T2 U03 Vc0+ U13 M22 Aq1+ Va1+ U23 W10+ Vc1+ O0+ U33
    M10+ R22 T3 O1+ VA2+ M11+ R1a0+ Ak2+ M23 Av2+ R1a1+ U00+ W20+ U10+ R23 Aq2+ U20+ U30+ Ak3+
    """)
POOL_ORDER = steps_of("""
    U30 T0 U01 M20 U11 Vb2 U21 Vb3 O2 U31 X0+ M12 O3 T1 M13 R1b2 M21 U02 U12 X1+ U22 U32 R1b3 U03 T2 Vb0+ U13
    M22 U23 O0+ U33 Vb1+ M10+ X2+ O1+ T3 M11+ R1b0+ M23 U00+ U10+ X3+ R1b1+ U20+
    """)
M_STEPS, R_STEPS = ("M1", "M2"), ("R1a", "R2")
JOBS = [(s[1] if s[0] == "A" else s[0].lower(), t, int(s[1]) if s[0] == "U" else 0, n)
        for s, t, n in PE_ORDER if s[0] in "AOU"]
assert len(JOBS) == TILES * (4 + FC // 2) and len(JOBS) % 2 == 0
JOB_AT = {j[:3]: i for i, j in enumerate(JOBS)}


def layers_stage(nc, sem, XF, ones_inv, consts, x_t, vecs, w_qkvo, w1, w2):
    with ExitStack() as ctx:
        def sb(name, shape, dt=F32):
            return ctx.enter_context(nc.sbuf_tensor(name, shape, dt))

        stgA = sb("stgA", [P, 4, KC, D])
        stgB = sb("stgB", [P, KC * FF])
        WAh, WAl = sb("WAh", [P, 4, KC, D], F32R), sb("WAl", [P, 4, KC, D], F32R)
        W1h, W1l = sb("W1h", [P, KC, FF], F32R), sb("W1l", [P, KC, FF], F32R)
        W2h, W2l = sb("W2h", [P, FC, D], F32R), sb("W2l", [P, FC, D], F32R)
        allvec = sb("allvec", [P, LAYERS * NVEC])
        vec = [sb(f"vec{b}", [P, VEC["ln2_s"]]) for b in range(BATCH)]
        vn = [sb(f"vn{b}", [P, 2 * KC]) for b in range(BATCH)]
        plus = [{n: sb(f"plus_{n}{b}", [P, KC]) for n in ("bq", "bk")} for b in range(BATCH)]
        minus = [{n: sb(f"minus_{n}{b}", [P, KC]) for n in ("bq", "bk", "ln1_s", "ln2_s")} for b in range(BATCH)]

        xh, xl = sb("xh", [P, 2, KC, TW], F32R), sb("xl", [P, 2, KC, TW], F32R)
        Ek, Eq = sb("Ek", [P, KC, TW]), sb("Eq", [P, KC, TW])
        Q = sb("Q", [P, KC, TOKENS])
        kpart, kvpart = sb("kpart", [P, KC, TILES]), sb("kvpart", [P, KC, TILES])
        ksum, nkvsum = sb("ksum", [P, KC, BATCH]), sb("nkvsum", [P, KC, BATCH])
        den, rec = sb("den", [P, KC, TW]), sb("rec", [P, KC, TW])
        vh, vl = sb("vh", [P, KC, TW], F32R), sb("vl", [P, KC, TW], F32R)
        R = {1: sb("R1", [P, 2, KC, TW]), 2: sb("R2", [P, 2, KC, TW])}
        RS = {n: sb(f"RS{n}", [P, TW]) for n in (1, 2)}
        SQ = sb("SQ", [P, KC, TW])
        SS = sb("SS", [P, TW])
        Y0, Y2 = sb("Y0", [P, TW]), sb("Y2", [P, TW])
        x1 = sb("x1", [P, 2, KC, TW])
        x1h, x1l = sb("x1h", [P, KC, TW], F32R), sb("x1l", [P, KC, TW], F32R)
        HF = sb("HF", [P, 4, TW])
        hh, hl = sb("hh", [P, 4, TW], F32R), sb("hl", [P, 4, TW], F32R)

        pair = [ctx.enter_context(nc.psum_tensor(f"pair{i}", [P, KC, TW], F32)) for i in range(2)]
        pD = ctx.enter_context(nc.psum_tensor("pD", [P, KC, TW], F32))
        pMean = ctx.enter_context(nc.psum_tensor("pMean", [P, TW], F32))
        pVar = ctx.enter_context(nc.psum_tensor("pVar", [P, TW], F32))

        per_tile = {"k_mm": 1, "v_mm": 1, "q_mm": 1, "o_mm": 1, "u_mm": 4, "d_mm": 4,
                    "nk": 2, "nq": 2, "ek": 1, "eq": 1, "ekr": 1, "eqr": 1, "kdone": 2, "qdone": 2, "kvdone": 2,
                    "den": 2, "lnd": 1, "rec0": 1, "dy": 1, "rec": 1, "vdone": 2, "vh": 1, "vl": 1, "xh": 1, "xl": 1,
                    "go": 2, "go2": 1, "gd": 2, "r1": 1, "r2": 1, "x1": 2, "x1h": 1, "x1l": 1,
                    "h": 8, "hh": 8, "hl_dve": 4, "hl_pool": 4, "xnew": 2}
        for kind in ("mean_mm", "var_mm", "rs", "xc", "sq", "ss", "newton", "rstd", "y"):
            per_tile[kind + "1"] = per_tile[kind + "2"] = 1
        per_tile["guess1"] = per_tile["guess2"] = 3
        per_layer = {"wh": 4, "wl": 4, "sums": 4, **{f"vec{b}": 6 for b in range(BATCH)},
                     **{f"vn{b}": 2 for b in range(BATCH)}}
        S = {n: sem("l_" + n) for n in (*per_tile, *per_layer)}
        s_stgA, s_stgB, s_allvec, s_x0 = (sem("l_" + n) for n in ("stgA", "stgB", "allvec", "x0"))
        both = lambda *names: [n + k for n in names for k in "12"]
        owners = {"pe": ["k_mm", "v_mm", "q_mm", "o_mm", "u_mm", "d_mm", *both("mean_mm", "var_mm")],
                  "act": ["lnd", "rec0", "nk", "nq", "ek", "eq", "vh", "xh", "go", "go2", "gd", "x1h", "h", "wh",
                          *both("sq", "guess")],
                  "dve": ["ekr", "eqr", "kdone", "qdone", "kvdone", "den", "dy", "rec", "vdone", "r1", "r2", "x1", "hh",
                          "hl_dve", "wl", "sums", "vec0", "vec1", "vn0", "vn1", *both("xc", "newton", "rstd", "y")],
                  "pool": ["vl", "xl", "x1l", "hl_pool", *both("rs", "ss")]}

        def start_counts(eng, who):
            for n in owners[who]:
                eng.sem_inc(S[n], TILES * per_tile[n] if n in per_tile else per_layer[n])

        def tile_event(eng, name, L, t, n=None):
            e = per_tile[name]
            eng.wait_ge(S[name], L * (e * TILES) + (e * t + (e if n is None else n + 1)))

        def weights_event(eng, name, L, i):
            eng.wait_ge(S[name], L * 4 + (i + 1))

        def vectors_event(eng, L, b, n=6):
            eng.wait_ge(S[f"vec{b}"], L * 6 + n)

        def norm_vectors_event(eng, L, b):
            eng.wait_ge(S[f"vn{b}"], L * 2 + 2)

        def before(seq, i, turn):
            found = []
            for k in range(1, len(seq)):
                item, n = seq[(i - k) % len(seq)]
                wrapped = k > i
                if turn == "first" and (wrapped or n == 0) or turn == "last" and not wrapped and n == 1:
                    if turn == "first" and wrapped:
                        break
                    continue
                if not found or n == 1:
                    found.append((item, n - wrapped))
                if n == 1 or not wrapped or turn == "last":
                    break
            return found

        PAIRS = [[(j[:3], j[3]) for j in JOBS[i::2]] for i in range(2)]

        def norm_before(eng, order, steps, name, norm, t, n, LT, turn):
            seq = [((steps.index(s) + 1, tt), nn) for s, tt, nn in order if s in steps]
            for (k, tt), nn in before(seq, seq.index(((norm, t), n)), turn):
                tile_event(eng, f"{name}{k}", LT + nn, tt)

        def slot(what, t, j=0):
            return pair[JOB_AT[what, t, j] % 2]

        def slot_free(eng, what, t, j, n, LT, turn):
            seq = PAIRS[JOB_AT[what, t, j] % 2]
            for (w, tt, jj), nn in before(seq, seq.index(((what, t, j), n)), turn):
                name, e = {"k": ("kdone", 1), "v": ("kvdone", 1), "q": ("qdone", 1), "o": ("go", 1),
                           "u": ("h", 2 * jj + 1)}[w]
                tile_event(eng, name, LT + nn, tt, e)

        def turns(eng, order, step):
            for s, t, n in order:
                if n == 1:
                    step(s, t, n, 1, 0, "first")
            with eng.Fori(1, LAYERS) as LT:
                for s, t, n in order:
                    step(s, t, n, LT + n, LT, "all")
            for s, t, n in order:
                if n == 0:
                    step(s, t, n, LAYERS, LAYERS, "last")

        def col(name, t, c):
            return vec[t // 2][:, VEC[name] + c:VEC[name] + c + 1]

        def chunks(t):
            return slice(t * TW, (t + 1) * TW)

        def three(eng, out, wh, wl, h, l, start, stop):
            eng.matmul(out, wh, l, start=start, stop=False)
            eng.matmul(out, wl, h, start=False, stop=False)
            return eng.matmul(out, wh, h, start=False, stop=stop)

        block = ctx.enter_context(nc.Block())

        @block.sync
        def _(sp):
            sp.dma_start(XF[:, :, :], x_t.rearrange("(k p) n -> p k n", p=P)).then_inc(s_x0, 16)
            sp.dma_start(allvec[:, :], vecs).then_inc(s_allvec, 16)
            with sp.Fori(1, LAYERS + 1) as L:
                weights_event(sp, "wl", L - 1, 1)
                sp.dma_start(stgA[:, :, :, :].rearrange("p w k n -> p (w k n)"),
                             w_qkvo[bass.ds((L - 1) * P, P), :]).then_inc(s_stgA, 16)
                weights_event(sp, "wl", L - 1, 3)
                sp.dma_start(stgB[:, :], w1[bass.ds((L - 1) * P, P), :]).then_inc(s_stgB, 16)
                weights_event(sp, "wl", L, 2)
                sp.dma_start(stgB[:, :], w2[bass.ds((L - 1) * P, P), :]).then_inc(s_stgB, 16)

        def weight_parts(i):
            if i < 2:
                w = slice(0, 3) if i == 0 else slice(3, 4)
                return tuple(x[:, w, :, :].rearrange("p w k n -> p (w k n)") for x in (stgA, WAh, WAl))
            a, b = ((W1h, W1l), (W2h, W2l))[i - 2]
            return stgB[:, :], a[:, :, :].rearrange("p k n -> p (k n)"), b[:, :, :].rearrange("p k n -> p (k n)")

        WSTEP = {"WQ": 0, "WO": 1, "W1": 2, "W2": 3}

        def weights_staged(eng, i, L):
            if i < 2:
                eng.wait_ge(s_stgA, L * 16)
            else:
                eng.wait_ge(s_stgB, L * 32 - 16 * (3 - i))

        def weights_used(eng, i, L):
            tile_event(eng, ("q_mm", "o_mm", "u_mm", "d_mm")[i], L - 1, TILES - 1)

        @block.scalar
        def _(act):
            start_counts(act, "act")
            table = {}

            def act_step(step, t, n, L, LT, turn):
                need = {"Ak": LOG_EXP, "Aq": LOG_EXP, "Va": LOG_EXP, "R1a": LOG_EXP, "R2": LOG_EXP, "O": GELU,
                        "T": GELU}.get(step, GELU if step[0] == "U" else None)
                if need and need != table.get(turn):
                    act.preload_act_table_set(need)
                    table[turn] = need
                if step in WSTEP:
                    i = WSTEP[step]
                    w, wh, _ = weight_parts(i)
                    weights_staged(act, i, L)
                    weights_used(act, i, L)
                    act.activation(wh, w, ACT.Copy).then_inc(S["wh"], 1)
                if step == "X":
                    tile_event(act, "xnew", L - 1, t)
                    tile_event(act, "q_mm", L, t - 2)
                    act.activation(xh[:, t % 2], XF[:, :, chunks(t)], ACT.Copy).then_inc(S["xh"], 1)
                if step in ("Ak", "Aq"):
                    what, E, neg, done, used = {"Ak": ("k", Ek, "nk", "ek", "kvdone"),
                                                "Aq": ("q", Eq, "nq", "eq", "qdone")}[step]
                    vectors_event(act, L, t // 2)
                    tile_event(act, what + "_mm", L, t)
                    for c in range(KC):
                        tile_event(act, used, L, t - 1, c)
                        act.activation(E[:, c], slot(what, t)[:, c], ACT.Relu,
                                       bias=minus[t // 2]["b" + what][:, c:c + 1], scale=-1.0).then_inc(S[neg], 1)
                    tile_event(act, neg, L, t)
                    act.activation(E[:, :, :], E[:, :, :], ACT.Exp, scale=-1.0).then_inc(S[done], 1)
                if step == "Va":
                    tile_event(act, "den", L, t)
                    tile_event(act, "rec", L, t - 1)
                    act.activation(rec[:, :, :], den[:, :, :], ACT.Ln).then_inc(S["lnd"], 1)
                    tile_event(act, "lnd", L, t)
                    act.activation(rec[:, :, :], rec[:, :, :], ACT.Exp, scale=-1.0).then_inc(S["rec0"], 1)
                if step == "Vb":
                    tile_event(act, "vdone", L, t)
                    tile_event(act, "o_mm", L, t - 1)
                    act.activation(vh[:, :, :], Q[:, :, chunks(t)], ACT.Copy).then_inc(S["vh"], 1)
                if step == "O":
                    tile_event(act, "o_mm", L, t)
                    tile_event(act, "x1", L, t - 2)
                    for c in range(KC):
                        act.activation(R[1][:, t % 2, c], slot("o", t)[:, c], ACT.Gelu_apprx_tanh,
                                       bias=col("bo", t, c)).then_inc(S["go"], 1)
                    tile_event(act, "go", L, t)
                    act.activation(R[1][:, t % 2], R[1][:, t % 2], ACT.Gelu_apprx_tanh).then_inc(S["go2"], 1)
                if step in ("M1", "M2"):
                    k = int(step[1])
                    tile_event(act, f"xc{k}", L, t)
                    norm_before(act, ACT_ORDER, M_STEPS, "ss", k, t, n, LT, turn)
                    act.activation(SQ[:, :, :], R[k][:, t % 2], ACT.Square).then_inc(S[f"sq{k}"], 1)
                if step in ("R1a", "R2"):
                    k = int(step[1])
                    guess = f"guess{k}"
                    tile_event(act, f"var_mm{k}", L, t)
                    norm_before(act, ACT_ORDER, R_STEPS, "y", k, t, n, LT, turn)
                    act.activation(Y0[:, :], pVar[:, :], ACT.Ln, bias=consts[:, 0:1]).then_inc(S[guess], 1)
                    tile_event(act, guess, L, t, 0)
                    act.activation(Y0[:, :], Y0[:, :], ACT.Exp, scale=-0.5).then_inc(S[guess], 1)
                    tile_event(act, guess, L, t, 1)
                    act.activation(Y2[:, :], Y0[:, :], ACT.Square, scale=0.5 ** 0.5).then_inc(S[guess], 1)
                if step == "R1b":
                    tile_event(act, "x1", L, t)
                    tile_event(act, "u_mm", L, t - 1)
                    act.activation(x1h[:, :, :], x1[:, t % 2], ACT.Copy).then_inc(S["x1h"], 1)
                if step[0] == "U":
                    for f in (2 * int(step[1]), 2 * int(step[1]) + 1):
                        tile_event(act, "u_mm", L, t, f // 2)
                        tile_event(act, "hl_pool" if f % 2 else "hl_dve", L, t, f // 2 - 2)
                        act.activation(HF[:, f % 4], slot("u", t, f // 2)[:, f % 2], ACT.Gelu_apprx_tanh,
                                       bias=col("b1", t, f)).then_inc(S["h"], 1)
                if step == "T":
                    tile_event(act, "d_mm", L, t)
                    tile_event(act, "xnew", L, t - 2)
                    for c in range(KC):
                        act.activation(R[2][:, t % 2, c], pD[:, c], ACT.Gelu_apprx_tanh,
                                       bias=col("b2", t, c)).then_inc(S["gd"], 1)

            turns(act, ACT_ORDER, act_step)

        @block.vector
        def _(dve):
            start_counts(dve, "dve")
            dve.wait_ge(s_x0, 16)
            dve.sem_inc(S["xnew"], TILES * per_tile["xnew"])
            dve.wait_ge(s_allvec, 16)

            def dve_step(step, t, n, L, LT, turn):
                b = t // 2
                if step == "VA":
                    vs = S[f"vec{b}"]
                    tile_event(dve, "h", L - 1, t + 1)
                    tile_event(dve, "gd", L - 1, t + 1)
                    tile_event(dve, "x1", L - 1, t + 1)
                    dve.tensor_scalar(vec[b][:, :], allvec[:, bass.ds((L - 1) * NVEC, VEC["ln2_s"])], 1.0, None,
                                      ALU.mult).then_inc(vs, 1)
                    vectors_event(dve, L, b, 1)
                    for name in ("bq", "bk"):
                        v = vec[b][:, VEC[name]:VEC[name] + KC]
                        dve.tensor_scalar(plus[b][name][:, :], v, 1.0, None, ALU.add).then_inc(vs, 1)
                        dve.tensor_scalar(minus[b][name][:, :], v, -1.0, None, ALU.mult).then_inc(vs, 1)
                    dve.tensor_scalar(minus[b]["ln1_s"][:, :], vec[b][:, VEC["ln1_s"]:VEC["ln1_s"] + KC], -1.0,
                                      None, ALU.mult).then_inc(vs, 1)
                    vectors_event(dve, L, b)
                if step == "VN":
                    tile_event(dve, "xnew", L - 1, t + 1)
                    dve.tensor_scalar(vn[b][:, :], allvec[:, bass.ds((L - 1) * NVEC + VEC["ln2_s"], 2 * KC)], 1.0, None,
                                      ALU.mult).then_inc(S[f"vn{b}"], 1)
                    dve.wait_ge(S[f"vn{b}"], L * 2 + 1)
                    dve.tensor_scalar(minus[b]["ln2_s"][:, :], vn[b][:, 0:KC], -1.0, None,
                                      ALU.mult).then_inc(S[f"vn{b}"], 1)
                if step in WSTEP:
                    i = WSTEP[step]
                    w, wh, wl = weight_parts(i)
                    weights_event(dve, "wh", L, i)
                    dve.tensor_tensor(wl, w, wh.bitcast(F32), ALU.subtract).then_inc(S["wl"], 1)
                if step == "Av":
                    tile_event(dve, "v_mm", L, t)
                    tile_event(dve, "kdone", L, t)
                    for c in range(KC):
                        dve.scalar_tensor_tensor(
                            out=Ek[:, c], in0=slot("v", t)[:, c], scalar=col("bv", t, c), in1=Ek[:, c],
                            op0=ALU.add, op1=ALU.mult, accum_out=kvpart[:, c, t:t + 1]).then_inc(S["kvdone"], 1)
                if step in ("Ak", "Aq"):
                    what, E, src, rnd = {"Ak": ("k", Ek, "ek", "ekr"), "Aq": ("q", Eq, "eq", "eqr")}[step]
                    ps, b1 = slot(what, t), plus[b]["b" + what]
                    tile_event(dve, src, L, t)
                    dve.tensor_scalar(E[:, :, :], E[:, :, :], -1.0, 1.0, ALU.add, ALU.add).then_inc(S[rnd], 1)
                    tile_event(dve, rnd, L, t)
                    for c in range(KC):
                        if what == "k":
                            if t % 2 == 0:
                                dve.wait_ge(S["sums"], L * 4 + (t - 2))
                            dve.scalar_tensor_tensor(
                                out=Ek[:, c], in0=ps[:, c], scalar=b1[:, c:c + 1], in1=E[:, c], op0=ALU.add,
                                op1=ALU.max, accum_out=kpart[:, c, t:t + 1]).then_inc(S["kdone"], 1)
                        else:
                            tile_event(dve, "vdone", L - 1, t, c)
                            dve.scalar_tensor_tensor(
                                out=Q[:, c, chunks(t)], in0=ps[:, c], scalar=b1[:, c:c + 1], in1=E[:, c],
                                op0=ALU.add, op1=ALU.max).then_inc(S["qdone"], 1)
                if step == "Va":
                    if t % 2 == 0:
                        tile_event(dve, "kvdone", L, t + 1)
                        tile_event(dve, "vdone", L - 1, t + 1)
                        dve.tensor_tensor(ksum[:, :, b:b + 1], kpart[:, :, t:t + 1], kpart[:, :, t + 1:t + 2],
                                          ALU.add).then_inc(S["sums"], 1)
                        dve.scalar_tensor_tensor(out=nkvsum[:, :, b], in0=kvpart[:, :, t], scalar=-1.0,
                                                 in1=kvpart[:, :, t + 1], op0=ALU.mult,
                                                 op1=ALU.subtract).then_inc(S["sums"], 1)
                        dve.wait_ge(S["sums"], L * 4 + (t + 2))
                    tile_event(dve, "qdone", L, t)
                    tile_event(dve, "vdone", L, t - 1)
                    for c in range(KC):
                        dve.tensor_scalar(den[:, c], Q[:, c, chunks(t)], ksum[:, c, b:b + 1], 1e-6,
                                          ALU.mult, ALU.add).then_inc(S["den"], 1)
                if step == "Vc":
                    tile_event(dve, "rec0", L, t)
                    dve.tensor_tensor(den[:, :, :], den[:, :, :], rec[:, :, :], ALU.mult).then_inc(S["dy"], 1)
                    tile_event(dve, "dy", L, t)
                    dve.scalar_tensor_tensor(out=den[:, :, :], in0=den[:, :, :], scalar=-2.0, in1=rec[:, :, :],
                                             op0=ALU.add, op1=ALU.mult).then_inc(S["rec"], 1)
                    tile_event(dve, "rec", L, t)
                    for c in range(KC):
                        dve.scalar_tensor_tensor(out=Q[:, c, chunks(t)], in0=Q[:, c, chunks(t)],
                                                 scalar=nkvsum[:, c, b:b + 1], in1=den[:, c], op0=ALU.mult,
                                                 op1=ALU.mult).then_inc(S["vdone"], 1)
                if step == "O":
                    tile_event(dve, "go2", L, t)
                    dve.tensor_tensor(R[1][:, t % 2], R[1][:, t % 2], XF[:, :, chunks(t)],
                                      ALU.add).then_inc(S["r1"], 1)
                if step == "T":
                    tile_event(dve, "gd", L, t)
                    dve.tensor_tensor(R[2][:, t % 2], R[2][:, t % 2], x1[:, t % 2],
                                      ALU.add).then_inc(S["r2"], 1)
                if step in ("M1", "M2"):
                    k = int(step[1])
                    tile_event(dve, f"mean_mm{k}", L, t)
                    r = R[k][:, t % 2]
                    dve.tensor_tensor(r, r, pMean[:, None, :].to_broadcast([P, KC, TW]),
                                      ALU.subtract).then_inc(S[f"xc{k}"], 1)
                if step in ("R1a", "R2"):
                    k = int(step[1])
                    tile_event(dve, f"guess{k}", L, t)
                    dve.scalar_tensor_tensor(out=Y2[:, :], in0=pVar[:, :], scalar=ATTN_LN_EPS, in1=Y2[:, :],
                                             op0=ALU.add, op1=ALU.mult).then_inc(S[f"newton{k}"], 1)
                    tile_event(dve, f"newton{k}", L, t)
                    dve.scalar_tensor_tensor(out=Y0[:, :], in0=Y2[:, :], scalar=-1.5, in1=Y0[:, :],
                                             op0=ALU.add, op1=ALU.mult).then_inc(S[f"rstd{k}"], 1)
                    tile_event(dve, f"rstd{k}", L, t)
                    tile_event(dve, f"sq{k}", L, t)
                    r = R[k][:, t % 2]
                    dve.tensor_tensor(r, r, Y0[:, None, :].to_broadcast([P, KC, TW]),
                                      ALU.mult).then_inc(S[f"y{k}"], 1)
                    tile_event(dve, f"y{k}", L, t)
                    if k == 1:
                        tile_event(dve, "r2", L, t - 2)
                        tile_event(dve, "x1l", L, t - 2)
                    else:
                        tile_event(dve, "xl", L, t)
                        norm_vectors_event(dve, L, b)
                    for c in range(KC):
                        to, done, shift = ((x1[:, t % 2, c], "x1", col("ln1_b", t, c)) if k == 1 else
                                           (XF[:, c, chunks(t)], "xnew", vn[b][:, KC + c:KC + c + 1]))
                        dve.tensor_scalar(to, r[:, c], minus[b][f"ln{k}_s"][:, c:c + 1], shift, ALU.mult,
                                          ALU.add).then_inc(S[done], 1)
                if step[0] == "U":
                    for f in (2 * int(step[1]), 2 * int(step[1]) + 1):
                        tile_event(dve, "h", L, t, f)
                        tile_event(dve, "d_mm", L, t, f // 2 - 2)
                        dve.tensor_copy(hh[:, f % 4], HF[:, f % 4]).then_inc(S["hh"], 1)
                        if f % 2 == 0:
                            tile_event(dve, "hh", L, t, f)
                            dve.tensor_tensor(hl[:, f % 4], HF[:, f % 4], hh[:, f % 4].bitcast(F32),
                                              ALU.subtract).then_inc(S["hl_dve"], 1)

            turns(dve, DVE_ORDER, dve_step)

        @block.gpsimd
        def _(pool):
            start_counts(pool, "pool")

            def pool_step(step, t, n, L, LT, turn):
                if step == "X":
                    tile_event(pool, "xh", L, t)
                    pool.tensor_tensor(xl[:, t % 2], XF[:, :, chunks(t)], xh[:, t % 2].bitcast(F32),
                                       ALU.subtract).then_inc(S["xl"], 1)
                if step == "Vb":
                    tile_event(pool, "vh", L, t)
                    pool.tensor_tensor(vl[:, :, :], Q[:, :, chunks(t)], vh[:, :, :].bitcast(F32),
                                       ALU.subtract).then_inc(S["vl"], 1)
                if step in ("O", "T"):
                    k = 1 if step == "O" else 2
                    tile_event(pool, f"r{k}", L, t)
                    tile_event(pool, f"mean_mm{k}", L, t - 1)
                    pool.tensor_tensor(RS[k][:, :], R[k][:, t % 2, 0], R[k][:, t % 2, 1],
                                       ALU.add).then_inc(S[f"rs{k}"], 1)
                if step in ("M1", "M2"):
                    k = int(step[1])
                    tile_event(pool, f"sq{k}", L, t)
                    norm_before(pool, POOL_ORDER, M_STEPS, "var_mm", k, t, n, LT, turn)
                    pool.tensor_tensor(SS[:, :], SQ[:, 0], SQ[:, 1], ALU.add).then_inc(S[f"ss{k}"], 1)
                if step == "R1b":
                    tile_event(pool, "x1h", L, t)
                    pool.tensor_tensor(x1l[:, :, :], x1[:, t % 2], x1h[:, :, :].bitcast(F32),
                                       ALU.subtract).then_inc(S["x1l"], 1)
                if step[0] == "U":
                    f = 2 * int(step[1]) + 1
                    tile_event(pool, "hh", L, t, f)
                    pool.tensor_tensor(hl[:, f % 4], HF[:, f % 4], hh[:, f % 4].bitcast(F32),
                                       ALU.subtract).then_inc(S["hl_pool"], 1)

            turns(pool, POOL_ORDER, pool_step)

        @block.tensor
        def _(pe):
            start_counts(pe, "pe")

            def project(what, w, t, n, L, LT, turn, h, l):
                slot_free(pe, what, t, 0, n, LT, turn)
                ps = slot(what, t)
                for m in range(KC):
                    cols = slice(m * P, (m + 1) * P)
                    for k in range(KC):
                        mm = three(pe, ps[:, m], WAh[:, w, k, cols], WAl[:, w, k, cols], h[:, k], l[:, k],
                                   k == 0, k == KC - 1)
                mm.then_inc(S[what + "_mm"], 1)

            def down(t, j, L):
                if t == 0 and j == 0:
                    weights_event(pe, "wl", L, 3)
                tile_event(pe, "hl_dve", L, t, j)
                tile_event(pe, "hl_pool", L, t, j)
                if j == 0:
                    tile_event(pe, "gd", L, t - 1)
                for m in range(KC):
                    for f in (2 * j, 2 * j + 1):
                        cols = slice(m * P, (m + 1) * P)
                        mm = three(pe, pD[:, m], W2h[:, f, cols], W2l[:, f, cols], hh[:, f % 4], hl[:, f % 4],
                                   f == 0, f == FC - 1)
                mm.then_inc(S["d_mm"], 1)

            def pe_step(step, t, n, L, LT, turn):
                if step in ("Ak", "Av", "Aq"):
                    if t == 0:
                        weights_event(pe, "wl", L, 0)
                    tile_event(pe, "xl", L, t)
                    project(step[1], "qkv".index(step[1]), t, n, L, LT, turn, xh[:, t % 2], xl[:, t % 2])
                if step == "O":
                    if t == 0:
                        weights_event(pe, "wl", L, 1)
                    tile_event(pe, "vl", L, t)
                    project("o", 3, t, n, L, LT, turn, vh, vl)
                if step in ("M1", "M2"):
                    k = int(step[1])
                    tile_event(pe, f"rs{k}", L, t)
                    norm_before(pe, PE_ORDER, M_STEPS, "xc", k, t, n, LT, turn)
                    pe.matmul(pMean[:, :], ones_inv[:, :], RS[k][:, :], start=True,
                              stop=True).then_inc(S[f"mean_mm{k}"], 1)
                if step in ("R1a", "R2"):
                    k = int(step[1])
                    tile_event(pe, f"ss{k}", L, t)
                    norm_before(pe, PE_ORDER, R_STEPS, "newton", k, t, n, LT, turn)
                    pe.matmul(pVar[:, :], ones_inv[:, :], SS[:, :], start=True,
                              stop=True).then_inc(S[f"var_mm{k}"], 1)
                if step[0] == "U":
                    j = int(step[1])
                    if t == 0 and j == 0:
                        weights_event(pe, "wl", L, 2)
                    tile_event(pe, "x1l", L, t)
                    slot_free(pe, "u", t, j, n, LT, turn)
                    for f in (2 * j, 2 * j + 1):
                        cols = slice(f * P, (f + 1) * P)
                        for k in range(KC):
                            mm = three(pe, slot("u", t, j)[:, f % 2], W1h[:, k, cols], W1l[:, k, cols],
                                       x1h[:, k], x1l[:, k], k == 0, k == KC - 1)
                    mm.then_inc(S["u_mm"], 1)
                if step[0] == "D":
                    down(t, int(step[1]), L)

            turns(pe, PE_ORDER, pe_step)


HEADS, HD, KEYS = 16, 16, 77
HC = P // HD
HB = HC // 2
SUB = TW // P
UNITS = SUB * KC
BT = SEQ // TW


def cross_order():
    order = [("L", 0, 0), ("L", 1, 0), ("M", 0, 0), ("M", 1, 0), ("R", 0, 0), ("R", 1, 0), ("Q", 0, 0), ("Q", 1, 0)]
    n = BT * UNITS
    order += [("S", 0, 0), ("S", 0, 1)]
    for i in range(n + 2):
        for step, j in (("T", i), ("P", i - 1), ("C", i - 2), ("S", i + 2)):
            if 0 <= j < n and not (step == "S" and j < 2):
                order.append((step, j // UNITS, j % UNITS))
        for t in range(BT):
            last = (t + 1) * UNITS - 1 + 2
            order += {last: [("O", t, 1)], last + 1: [("M", t, 1)], last + 3: [("R", t, 1)]}.get(i, [])
    order += [("M", BT - 1, 1), ("R", BT - 1, 1)]
    return order


def cross_stage(nc, sem, XF, ones_inv, consts, ident, headmask, x_t, ctx_t, cvecs, cw):
    ORDER2 = cross_order()
    NORMS2 = [(n, t) for s, t, n in ORDER2 if s == "M"]
    assert NORMS2 == [(n, t) for s, t, n in ORDER2 if s == "R"]
    assert NORMS2 == [(n, t) for s, t, n in ORDER2 if s in ("L", "O")]
    NN2 = len(NORMS2)
    with ExitStack() as ctx:
        def sb(name, shape, dt=F32):
            return ctx.enter_context(nc.sbuf_tensor(name, shape, dt))

        W = sb("c_W", [P, 4, KC, D])
        cvec = sb("c_vec", [P, 4, KC])
        cT = sb("c_T", [P, KC, BATCH * KEYS])
        kT = sb("c_kT", [P, KC, BATCH * KEYS])
        KB = sb("c_KB", [P, BATCH * KC, HC, KEYS])
        V17 = sb("c_V17", [KEYS, BATCH, HEADS, HD + 1])
        B = sb("c_B", [P, BT, KC, TW])
        RS, SS = sb("c_RS", [P, TW]), sb("c_SS", [P, TW])
        SQ = sb("c_SQ", [P, KC, TW])
        Y0, Y2 = sb("c_Y0", [P, TW]), sb("c_Y2", [P, TW])
        q2 = sb("c_q2", [P, BT, KC, TW])
        Pb = sb("c_Pb", [P, 2, HC, KEYS])
        PT = sb("c_PT", [KEYS, 2, HC, P])
        mx = sb("c_mx", [P, 2, HC])
        rec = sb("c_rec", [P, 2, HC])
        Cx = sb("c_Cx", [P, 2, HC, HD])
        cxT = sb("c_cxT", [P, BT, KC, TW])

        psS = [ctx.enter_context(nc.psum_tensor(f"c_psS{i}", [P, 2, 512], F32)) for i in range(2)]
        psT = ctx.enter_context(nc.psum_tensor("c_psT", [P, 2, HB, P], F32))
        psO = ctx.enter_context(nc.psum_tensor("c_psO", [P, 512], F32))
        psX = ctx.enter_context(nc.psum_tensor("c_psX", [P, TW], F32))

        per_tile = {"r0": 1, "r1": 2, "q_mm": 2, "q": 2, "s_mm": UNITS, "mx": UNITS, "sub": UNITS,
                    "exp": UNITS, "t_mm": 2 * UNITS, "ta": UNITS, "tv": UNITS, "pv": UNITS, "rec": UNITS,
                    "cx": UNITS, "c_mm": UNITS, "cxT": UNITS, "o_mm": 2}
        per_turn = {"rs": NN2, "mean_mm": NN2, "xc": NN2, "sq": NN2, "ss": NN2, "var_mm": NN2, "guess": 3 * NN2,
                    "newton": NN2, "rstd": NN2, "norm": NN2}
        S = {n: sem("c_" + n) for n in (*per_tile, *per_turn)}
        s_xo = [sem(f"c_xo{t}") for t in range(BT)]
        s_load, s_pre, s_kmm, s_kev, s_kb, s_vmm, s_vev = (sem("c_" + n) for n in
                                                           ("load", "pre", "kmm", "kev", "kb", "vmm", "vev"))
        owners = {"pe": ["q_mm", "s_mm", "t_mm", "pv", "c_mm", "o_mm", "mean_mm", "var_mm"],
                  "act": ["q", "exp", "ta", "cxT", "sq", "guess"],
                  "dve": ["r0", "r1", "mx", "sub", "tv", "rec", "cx", "xc", "newton", "rstd", "norm"],
                  "pool": ["rs", "ss"]}

        def start_counts(eng, who):
            for n in owners[who]:
                eng.sem_inc(S[n], BT * per_tile[n] if n in per_tile else per_turn[n])

        def tile_event(eng, name, L, t, n=None):
            e = per_tile[name]
            eng.wait_ge(S[name], L * (e * BT) + (e * t + (e if n is None else n + 1)))

        def guess_event(eng, L, i, n):
            eng.wait_ge(S["guess"], L * (3 * NN2) + (3 * i + n))

        def norm_event(eng, name, L, i):
            eng.wait_ge(S[name], L * NN2 + (i + 1))

        USES = []
        for step, t, n in ORDER2:
            i = NORMS2.index((n, t)) if step in "MR" else 0
            USES += {"M": [("mean", i, 0, ("xc", i))], "R": [("var", i, 0, ("newton", i))],
                     "Q": [("q", t, m, ("q", t, m)) for m in range(KC)],
                     "C": [("c", t, n, ("cxT", t, n))],
                     "O": [("o", t, m, ("r1", t, m)) for m in range(KC)]}.get(step, [])

        def bank_free(pe, what, a, b, L):
            i = [u[:3] for u in USES].index((what, a, b)) - 1
            name, *at = USES[i][3]
            back = i < 0
            if len(at) == 1:
                norm_event(pe, name, L, at[0] - NN2 * back)
            else:
                tile_event(pe, name, L, at[0] - BT * back, at[1])

        def x_tile(L, t):
            return XF[:, :, bass.ds((L - 1) * SEQ + t * TW, TW)]

        block = ctx.enter_context(nc.Block())

        @block.sync
        def _(sp):
            sp.dma_start(cT[:, :, :], ctx_t.rearrange("(k p) n -> p k n", p=P)).then_inc(s_load, 16)
            sp.dma_start(W[:, :, :, :].rearrange("p w k n -> p (w k n)"), cw).then_inc(s_load, 16)
            sp.dma_start(cvec[:, :, :].rearrange("p v c -> p (v c)"), cvecs).then_inc(s_load, 16)
            with sp.Fori(1, BATCH + 1) as L:
                for t in range(BT):
                    norm_event(sp, "norm", L - 1, NORMS2.index((1, t)))
                    sp.dma_start(B[:, t], x_t.rearrange("(k p) n -> p k n", p=P)[
                        :, :, bass.ds((L - 1) * SEQ + t * TW, TW)]).then_inc(s_xo[t], 16)

        @block.scalar
        def _(act):
            start_counts(act, "act")
            act.wait_ge(s_load, 48)
            act.preload_act_table_set(LOG_EXP)
            for m in range(KC):
                act.wait_ge(s_kmm, m + 1)
                act.activation(kT[:, m, :], psX[:, m * 256:m * 256 + BATCH * KEYS], ACT.Identity,
                               bias=cvec[:, 1, m:m + 1]).then_inc(s_kev, 1)
            with act.Fori(1, BATCH + 1) as L:
                for step, t, n in ORDER2:
                    if step == "M":
                        i = NORMS2.index((n, t))
                        norm_event(act, "xc", L, i)
                        norm_event(act, "ss", L, i - 1)
                        act.activation(SQ[:, :, :], B[:, t], ACT.Square).then_inc(S["sq"], 1)
                    if step == "R":
                        i = NORMS2.index((n, t))
                        norm_event(act, "var_mm", L, i)
                        norm_event(act, "norm", L, i - 1)
                        act.activation(Y0[:, :], psX[:, :], ACT.Ln, bias=consts[:, 1:2]).then_inc(S["guess"], 1)
                        guess_event(act, L, i, 1)
                        act.activation(Y0[:, :], Y0[:, :], ACT.Exp, scale=-0.5).then_inc(S["guess"], 1)
                        guess_event(act, L, i, 2)
                        act.activation(Y2[:, :], Y0[:, :], ACT.Square, scale=0.5 ** 0.5).then_inc(S["guess"], 1)
                    if step == "Q":
                        for m in range(KC):
                            tile_event(act, "q_mm", L, t, m)
                            tile_event(act, "s_mm", L - 1, t)
                            act.activation(q2[:, t, m], psX[:, :], ACT.Identity,
                                           bias=cvec[:, 0, m:m + 1]).then_inc(S["q"], 1)
                    if step == "S":
                        tile_event(act, "sub", L, t, n)
                        act.activation(Pb[:, n % 2], Pb[:, n % 2], ACT.Exp, scale=HD ** -0.5).then_inc(S["exp"], 1)
                    if step == "T":
                        tile_event(act, "t_mm", L, t, 2 * n)
                        tile_event(act, "pv", L, t, n - 2)
                        act.activation(PT[:, n % 2, 0:HB], psT[0:KEYS, 0], ACT.Copy).then_inc(S["ta"], 1)
                    if step == "C":
                        s, c = n // KC, n % KC
                        tile_event(act, "c_mm", L, t, n)
                        tile_event(act, "o_mm", L - 1, t)
                        act.activation(cxT[:, t, c, s * P:(s + 1) * P], psX[:, 0:P], ACT.Identity,
                                       bias=cvec[:, 2, c:c + 1]).then_inc(S["cxT"], 1)

        @block.vector
        def _(dve):
            start_counts(dve, "dve")
            dve.memset(V17[:, :, :, :], 1.0).then_inc(s_pre, 1)
            dve.wait_ge(s_kev, KC)
            for b in range(BATCH):
                for c in range(KC):
                    dve.tensor_tensor(KB[:, b * KC + c],
                                      kT[:, c, None, b * KEYS:(b + 1) * KEYS].to_broadcast([P, HC, KEYS]),
                                      headmask[:, :, None].to_broadcast([P, HC, KEYS]), ALU.mult).then_inc(s_kb, 1)
            dve.wait_ge(s_pre, 1)
            for b in range(BATCH):
                dve.wait_ge(s_vmm, b + 1)
                dve.tensor_copy(V17[:, b, :, 0:HD], psO[0:KEYS, b * D:(b + 1) * D]
                                .rearrange("p (h d) -> p h d", d=HD)).then_inc(s_vev, 1)
            with dve.Fori(1, BATCH + 1) as L:
                for step, t, n in ORDER2:
                    if step == "L":
                        dve.wait_ge(s_xo[t], L * 16)
                        dve.tensor_tensor(B[:, t], x_tile(L, t), B[:, t], ALU.add).then_inc(S["r0"], 1)
                    if step == "M":
                        i = NORMS2.index((n, t))
                        norm_event(dve, "mean_mm", L, i)
                        norm_event(dve, "rs", L, i)
                        dve.tensor_tensor(B[:, t], psX[:, None, :].to_broadcast([P, KC, TW]), B[:, t],
                                          ALU.subtract).then_inc(S["xc"], 1)
                    if step == "R":
                        i = NORMS2.index((n, t))
                        guess_event(dve, L, i, 3)
                        dve.scalar_tensor_tensor(out=Y2[:, :], in0=psX[:, :], scalar=LN_EPS, in1=Y2[:, :],
                                                 op0=ALU.add, op1=ALU.mult).then_inc(S["newton"], 1)
                        norm_event(dve, "newton", L, i)
                        dve.scalar_tensor_tensor(out=Y0[:, :], in0=Y2[:, :], scalar=-1.5, in1=Y0[:, :],
                                                 op0=ALU.add, op1=ALU.mult).then_inc(S["rstd"], 1)
                        norm_event(dve, "rstd", L, i)
                        norm_event(dve, "sq", L, i)
                        out = B[:, t] if n == 0 else x_tile(L, t)
                        dve.tensor_tensor(out, B[:, t], Y0[:, None, :].to_broadcast([P, KC, TW]),
                                          ALU.mult).then_inc(S["norm"], 1)
                    if step == "S":
                        tile_event(dve, "s_mm", L, t, n)
                        ps = psS[n % 2][:, :, 0:HB * KEYS].rearrange("p g (h k) -> p g h k", k=KEYS)
                        m = mx[:, n % 2].rearrange("p (g h) -> p g h", g=2)
                        dve.tensor_reduce(m, ps, AX.X, ALU.max).then_inc(S["mx"], 1)
                        tile_event(dve, "mx", L, t, n)
                        tile_event(dve, "t_mm", L, t, 2 * (n - 2) + 1)
                        dve.tensor_tensor(Pb[:, n % 2].rearrange("p (g h) k -> p g h k", g=2), ps,
                                          m[:, :, :, None].to_broadcast([P, 2, HB, KEYS]),
                                          ALU.subtract).then_inc(S["sub"], 1)
                    if step == "T":
                        tile_event(dve, "t_mm", L, t, 2 * n + 1)
                        tile_event(dve, "pv", L, t, n - 2)
                        dve.tensor_copy(PT[:, n % 2, HB:HC], psT[0:KEYS, 1]).then_inc(S["tv"], 1)
                    if step == "P":
                        o = psO[:, 0:HC * (HD + 1)].rearrange("p (h d) -> p h d", d=HD + 1)
                        tile_event(dve, "pv", L, t, n)
                        tile_event(dve, "cx", L, t, n - 2)
                        dve.reciprocal(rec[:, n % 2], o[:, :, HD]).then_inc(S["rec"], 1)
                        tile_event(dve, "rec", L, t, n)
                        tile_event(dve, "c_mm", L, t, n - 2)
                        dve.tensor_tensor(Cx[:, n % 2], o[:, :, 0:HD],
                                          rec[:, n % 2, :, None].to_broadcast([P, HC, HD]),
                                          ALU.mult).then_inc(S["cx"], 1)
                    if step == "O":
                        for m in range(KC):
                            tile_event(dve, "o_mm", L, t, m)
                            dve.scalar_tensor_tensor(out=B[:, t, m], in0=psX[:, :], scalar=cvec[:, 3, m:m + 1],
                                                     in1=B[:, t, m], op0=ALU.add, op1=ALU.add).then_inc(S["r1"], 1)

        @block.gpsimd
        def _(pool):
            start_counts(pool, "pool")
            with pool.Fori(1, BATCH + 1) as L:
                for step, t, n in ORDER2:
                    if step in ("L", "O"):
                        i = NORMS2.index((n, t))
                        tile_event(pool, f"r{n}", L, t)
                        norm_event(pool, "mean_mm", L, i - 1)
                        pool.tensor_tensor(RS[:, :], B[:, t, 0], B[:, t, 1], ALU.add).then_inc(S["rs"], 1)
                    if step == "M":
                        i = NORMS2.index((n, t))
                        norm_event(pool, "sq", L, i)
                        norm_event(pool, "var_mm", L, i - 1)
                        pool.tensor_tensor(SS[:, :], SQ[:, 0], SQ[:, 1], ALU.add).then_inc(S["ss"], 1)

        @block.tensor
        def _(pe):
            start_counts(pe, "pe")
            pe.wait_ge(s_load, 48)
            for m in range(KC):
                for k in range(KC):
                    mm = pe.matmul(psX[:, m * 256:m * 256 + BATCH * KEYS], W[:, 1, k, m * P:(m + 1) * P], cT[:, k, :],
                                   start=(k == 0), stop=(k == KC - 1))
                mm.then_inc(s_kmm, 1)
                if m == 0:
                    pe.wait_ge(s_kev, 1)
            for b in range(BATCH):
                for k in range(KC):
                    mm = pe.matmul(psO[0:KEYS, b * D:(b + 1) * D], cT[:, k, b * KEYS:(b + 1) * KEYS], W[:, 2, k, :],
                                   start=(k == 0), stop=(k == KC - 1))
                mm.then_inc(s_vmm, 1)
                pe.wait_ge(s_vev, b + 1)
            pe.wait_ge(s_kb, BATCH * KC)
            pe.wait_ge(s_kev, KC)
            with pe.Fori(1, BATCH + 1) as L:
                for step, t, n in ORDER2:
                    s, c = n // KC, n % KC
                    if step == "M":
                        i = NORMS2.index((n, t))
                        norm_event(pe, "rs", L, i)
                        bank_free(pe, "mean", i, 0, L)
                        pe.matmul(psX[:, :], ones_inv[:, :], RS[:, :], start=True, stop=True).then_inc(S["mean_mm"], 1)
                    if step == "R":
                        i = NORMS2.index((n, t))
                        norm_event(pe, "ss", L, i)
                        bank_free(pe, "var", i, 0, L)
                        pe.matmul(psX[:, :], ones_inv[:, :], SS[:, :], start=True, stop=True).then_inc(S["var_mm"], 1)
                    if step in ("Q", "O"):
                        w, src, done = (0, B, "q_mm") if step == "Q" else (3, cxT, "o_mm")
                        if step == "Q":
                            norm_event(pe, "norm", L, NORMS2.index((0, t)))
                        else:
                            tile_event(pe, "cxT", L, t)
                        for m in range(KC):
                            bank_free(pe, step.lower(), t, m, L)
                            for k in range(KC):
                                mm = pe.matmul(psX[:, :], W[:, w, k, m * P:(m + 1) * P], src[:, t, k],
                                               start=(k == 0), stop=(k == KC - 1))
                            mm.then_inc(S[done], 1)
                    if step == "S":
                        tile_event(pe, "q", L, t)
                        tile_event(pe, "sub", L, t, n - 2)
                        for g in range(2):
                            mm = pe.matmul(psS[n % 2][:, g, 0:HB * KEYS], q2[:, t, c, s * P:(s + 1) * P],
                                           KB[:, bass.ds((L - 1) * KC + c, 1), g * HB:(g + 1) * HB, :]
                                           .rearrange("p a h k -> p (a h k)"), start=True, stop=True)
                        mm.then_inc(S["s_mm"], 1)
                    if step == "T":
                        tile_event(pe, "exp", L, t, n)
                        for g in range(2):
                            tile_event(pe, ("ta", "tv")[g], L, t, n - 1)
                            for h in range(HB):
                                mm = pe.transpose(psT[0:KEYS, g, h], Pb[:, n % 2, g * HB + h], ident[:, :])
                            mm.then_inc(S["t_mm"], 1)
                    if step == "P":
                        tile_event(pe, "ta", L, t, n)
                        tile_event(pe, "tv", L, t, n)
                        tile_event(pe, "cx", L, t, n - 1)
                        for h in range(HC):
                            mm = pe.matmul(psO[:, h * (HD + 1):(h + 1) * (HD + 1)], PT[:, n % 2, h],
                                           V17[:, bass.ds(L - 1, 1), c * HC + h, :].rearrange("p a d -> p (a d)"),
                                           start=True, stop=True)
                        mm.then_inc(S["pv"], 1)
                    if step == "C":
                        tile_event(pe, "cx", L, t, n)
                        bank_free(pe, "c", t, n, L)
                        pe.transpose(psX[:, 0:P], Cx[:, n % 2].rearrange("p h d -> p (h d)"),
                                     ident[:, :]).then_inc(S["c_mm"], 1)


CAP = SEQ // 8
assert CAP == P
ST = SEQ // P
DFF = D * 4 * 2 // 3
DC = -(-DFF // P)
CR = BATCH * CAP
NEG = -1e30


def routed_stage(nc, sem, XF, ones_inv, consts, ident, headmask, x_out, fvecs, f_qkv, f_out, f_w12, f_w3):
    with ExitStack() as ctx:
        def sb(name, shape, dt=F32):
            return ctx.enter_context(nc.sbuf_tensor("f_" + name, shape, dt))

        fvec = sb("vec", [P, 3, KC])
        ng = sb("ng", [P, 2, KC])
        Wqkv = sb("Wqkv", [P, KC, 3 * D])
        Wout = sb("Wout", [P, KC, D])
        W12 = sb("W12", [P, 2, KC, DFF])
        W3 = sb("W3", [P, DC, D])
        wr = sb("wr", [P, KC, P])
        iota = sb("iota", [P, P])
        causal = sb("causal", [P, P])
        before = sb("before", [P, P])
        Srow = sb("Srow", [P, BATCH, SEQ])
        tmp = sb("tmp", [P, SEQ])
        scol = sb("scol", [P, BATCH, ST])
        cnt = sb("cnt", [P, BATCH, ST, 3])
        rank = sb("rank", [P, BATCH, ST])
        OH = sb("OH", [P, BATCH, ST, P])
        OHT = sb("OHT", [P, BATCH, SEQ])
        xN = sb("xN", [P, BATCH * ST, D])
        xs = sb("xs", [P, KC, CR])
        sq = sb("sq", [P, KC, CR])
        y0, y2 = sb("y0", [P, CR]), sb("y2", [P, CR])
        hT = sb("hT", [P, KC, CR])
        qT = sb("qT", [P, KC, CR])
        KB = sb("KB", [P, BATCH, KC, HC, P])
        V17 = sb("V17", [P, BATCH, HEADS, HD + 1])
        Pb = sb("Pb", [P, 2, HC, P])
        PT = sb("PT", [P, 2, HC, P])
        mx, rec = sb("mx", [P, 4, HC]), sb("rec", [P, 4, HC])
        Cx = sb("Cx", [P, 4, HC, HD])
        oT = sb("oT", [P, KC, CR])
        x1 = sb("x1", [P, KC, CR])
        sg = sb("sg", [P, DC, CR])
        dN = sb("dN", [P, BATCH, D])
        R = sb("R", [P, 2, KC, TW])
        RS, SS = sb("RS", [P, TW]), sb("SS", [P, TW])
        Z0, Z2 = sb("Z0", [P, TW]), sb("Z2", [P, TW])

        psS = [ctx.enter_context(nc.psum_tensor(f"f_psS{i}", [P, 2, 512], F32)) for i in range(2)]
        psT = ctx.enter_context(nc.psum_tensor("f_psT", [P, 2, 512], F32))
        psO = ctx.enter_context(nc.psum_tensor("f_psO", [P, 512], F32))
        psX = ctx.enter_context(nc.psum_tensor("f_psX", [P, 512], F32))

        names = ("vec w c_pool c_ng c_wr s_mm srow prod scol cnt rank oh xt_mm xn g_mm xs oht_mm oht "
                 "sq m_mm guess nw rs h qkv_mm q kb v sc_mm msk mx sub exp t_mm ta tv pv rec cx c_mm ot a_mm x1 "
                 "f1_mm f2_mm sil g d_mm d sct r rsum mean xc sqr ss var guess2 znw zrs out st").split()
        S = {n: sem("f_" + n) for n in names}

        NU = BATCH * KC
        block = ctx.enter_context(nc.Block())

        @block.sync
        def _(sp):
            sp.dma_start(fvec[:, :, :].rearrange("p v c -> p (v c)"), fvecs).then_inc(S["vec"], 16)
            sp.dma_start(Wqkv[:, :, :].rearrange("p k n -> p (k n)"), f_qkv).then_inc(S["w"], 16)
            sp.dma_start(Wout[:, :, :].rearrange("p k n -> p (k n)"), f_out).then_inc(S["w"], 16)
            sp.dma_start(W12[:, :, :, :].rearrange("p w k n -> p (w k n)"), f_w12).then_inc(S["w"], 16)
            sp.dma_start(W3[:, 0:DC - 1, :], f_w3[0:(DC - 1) * P, :].rearrange("(k p) n -> p k n", p=P)) \
                .then_inc(S["w"], 16)
            sp.dma_start(W3[0:DFF - (DC - 1) * P, DC - 1, :], f_w3[(DC - 1) * P:DFF, :]).then_inc(S["w"], 16)
            for t in range(TILES):
                sp.wait_ge(S["out"], t + 1)
                sp.dma_start(x_out.rearrange("(k p) n -> p k n", p=P)[:, :, t * TW:(t + 1) * TW],
                             R[:, t % 2]).then_inc(S["st"], 16)
                if t >= 1:
                    sp.wait_ge(S["st"], 16 * t)
            sp.wait_ge(S["st"], 16 * TILES)

        @block.gpsimd
        def _(pool):
            pool.iota(iota[:, :], pattern=[[1, P]], base=0, channel_multiplier=0,
                      allow_small_or_imprecise_dtypes=True).then_inc(S["c_pool"], 1)
            pool.memset(causal[:, :], 0.0).then_inc(S["c_pool"], 1)
            pool.memset(before[:, :], 1.0).then_inc(S["c_pool"], 1)
            pool.memset(V17[:, :, :, :], 1.0).then_inc(S["c_pool"], 1)
            pool.wait_ge(S["c_pool"], 4)
            pool.affine_select(out=causal[:, :], in_=causal[:, :], compare_op=ALU.is_ge, fill=NEG, base=0,
                               pattern=[[-1, P]], channel_multiplier=1).then_inc(S["c_pool"], 1)
            pool.affine_select(out=before[:, :], in_=before[:, :], compare_op=ALU.is_ge, fill=0.0, base=-1,
                               pattern=[[-1, P]], channel_multiplier=1).then_inc(S["c_pool"], 1)
            for t in range(TILES):
                pool.wait_ge(S["r"], 2 * t + 2)
                if t:
                    pool.wait_ge(S["mean"], t)
                pool.tensor_tensor(RS[:, :], R[:, t % 2, 0], R[:, t % 2, 1], ALU.add).then_inc(S["rsum"], 1)
                pool.wait_ge(S["sqr"], t + 1)
                if t:
                    pool.wait_ge(S["var"], t)
                pool.tensor_tensor(SS[:, :], tmp[:, 0:TW], tmp[:, TW:2 * TW], ALU.add).then_inc(S["ss"], 1)

        @block.scalar
        def _(act):
            act.preload_act_table_set(LOG_EXP)
            for b in range(BATCH):
                act.wait_ge(S["s_mm"], b + 1)
                act.activation(Srow[:, b].rearrange("p (g n) -> p g n", g=2), psS[b][:, :, :],
                               ACT.Copy).then_inc(S["srow"], 1)
            for i in range(BATCH * ST // 2):
                act.wait_ge(S["xt_mm"], i + 1)
                act.activation(xN[:, 2 * i:2 * i + 2, :].rearrange("p t n -> p (t n)"), psT[:, i % 2],
                               ACT.Copy).then_inc(S["xn"], 1)
            act.wait_ge(S["g_mm"], NU)
            act.activation(xs[:, :, :].rearrange("p c n -> p (c n)"), psO[:, :], ACT.Copy).then_inc(S["xs"], 1)
            for norm in range(2):
                src, ready, k = ((xs, "xs", 1), (x1, "x1", KC))[norm]
                act.wait_ge(S[ready], k)
                if norm:
                    act.wait_ge(S["m_mm"], norm)
                act.activation(sq[:, :, :], src[:, :, :], ACT.Square).then_inc(S["sq"], 1)
                act.wait_ge(S["m_mm"], norm + 1)
                ps = (psX, psO)[norm][:, 0:CR]
                if norm:
                    act.wait_ge(S["h"], KC * norm)
                act.activation(y0[:, :], ps, ACT.Ln, bias=consts[:, 0:1]).then_inc(S["guess"], 1)
                act.wait_ge(S["guess"], 3 * norm + 1)
                act.activation(y0[:, :], y0[:, :], ACT.Exp, scale=-0.5).then_inc(S["guess"], 1)
                act.wait_ge(S["guess"], 3 * norm + 2)
                act.activation(y2[:, :], y0[:, :], ACT.Square, scale=0.5 ** 0.5).then_inc(S["guess"], 1)
                if norm:
                    break
                for b in range(BATCH):
                    act.wait_ge(S["oht_mm"], b + 1)
                    act.activation(OHT[:, b].rearrange("p (g n) -> p g n", g=2), psS[b][:, :, :],
                                   ACT.Copy).then_inc(S["oht"], 1)
                act.wait_ge(S["qkv_mm"], 1)
                act.activation(qT[:, :, :].rearrange("p c n -> p (c n)"), psT[:, 0], ACT.Copy).then_inc(S["q"], 1)
                for i in range(NU + 2):
                    if i < NU:
                        act.wait_ge(S["sub"], i + 1)
                        act.activation(Pb[:, i % 2], Pb[:, i % 2], ACT.Exp, scale=HD ** -0.5).then_inc(S["exp"], 1)
                        act.wait_ge(S["t_mm"], 2 * i + 1)
                        if i >= 2:
                            act.wait_ge(S["pv"], i - 1)
                        act.activation(PT[:, i % 2, 0:HB].rearrange("p h n -> p (h n)"), psT[:, 0],
                                       ACT.Copy).then_inc(S["ta"], 1)
                    if i >= 2:
                        j = i - 2
                        b, c = j // KC, j % KC
                        act.wait_ge(S["c_mm"], j + 1)
                        act.activation(oT[:, c, b * P:(b + 1) * P], psX[:, 0:P], ACT.Copy).then_inc(S["ot"], 1)
            act.preload_act_table_set(SILU)
            for k in range(DC):
                w = min(P, DFF - k * P)
                act.wait_ge(S["f1_mm"], k // 2 * 2 + 2)
                act.activation(sg[0:w, k], (psS[0][0:w, k // 2, (k % 2) * CR:(k % 2 + 1) * CR] if k < 4 else
                                            psT[0:w, 0, (k % 2) * CR:(k % 2 + 1) * CR]),
                               ACT.Silu).then_inc(S["sil"], 1)
            act.preload_act_table_set(LOG_EXP)
            act.wait_ge(S["d_mm"], 1)
            act.activation(dN[:, :, :].rearrange("p b n -> p (b n)"), psO[:, :], ACT.Copy).then_inc(S["d"], 1)
            for t in range(TILES):
                act.wait_ge(S["xc"], t + 1)
                if t:
                    act.wait_ge(S["ss"], t)
                act.activation(tmp[:, :].rearrange("p (c n) -> p c n", c=KC), R[:, t % 2],
                               ACT.Square).then_inc(S["sqr"], 1)
                act.wait_ge(S["var"], t + 1)
                if t:
                    act.wait_ge(S["out"], t)
                act.activation(Z0[:, :], psX[:, :], ACT.Ln, bias=consts[:, 1:2]).then_inc(S["guess2"], 1)
                act.wait_ge(S["guess2"], 3 * t + 1)
                act.activation(Z0[:, :], Z0[:, :], ACT.Exp, scale=-0.5).then_inc(S["guess2"], 1)
                act.wait_ge(S["guess2"], 3 * t + 2)
                act.activation(Z2[:, :], Z0[:, :], ACT.Square, scale=0.5 ** 0.5).then_inc(S["guess2"], 1)

        @block.vector
        def _(dve):
            dve.wait_ge(S["vec"], 16)
            dve.tensor_copy(wr[:, :, :], fvec[:, 0, :, None].to_broadcast([P, KC, P])).then_inc(S["c_wr"], 1)
            dve.tensor_scalar(ng[:, :, :], fvec[:, 1:3, :], -1.0, None, ALU.mult).then_inc(S["c_ng"], 1)
            dve.memset(cnt[:, :, :, :], 0.0).then_inc(S["cnt"], 1)
            n_cnt = 1

            dve.wait_ge(S["c_pool"], 6)
            for b in range(BATCH):
                dve.wait_ge(S["srow"], b + 1)
                if n_cnt > 1:
                    dve.wait_ge(S["cnt"], n_cnt)
                row = Srow[:, b].rearrange("p (t n) -> p t n", n=P)
                t3 = tmp[:, :].rearrange("p (t n) -> p t n", n=P)
                dve.tensor_tensor(t3, row, ident[:, None, :].to_broadcast([P, ST, P]), ALU.mult).then_inc(S["prod"], 1)
                dve.wait_ge(S["prod"], b + 1)
                dve.tensor_reduce(scol[:, b], t3, AX.X, ALU.add).then_inc(S["scol"], 1)
                dve.wait_ge(S["scol"], b + 1)
                for t in range(ST):
                    s = scol[:, b, t:t + 1]
                    for part, lo, hi, op, mask in ((0, 0, t * P, ALU.is_ge, None), (1, t * P, SEQ, ALU.is_gt, None),
                                                   (2, t * P, (t + 1) * P, ALU.is_equal, before)):
                        if lo == hi:
                            continue
                        in1 = iota[:, 1:2].to_broadcast([P, hi - lo]) if mask is None else mask[:, :]
                        dve.wait_ge(S["cnt"], n_cnt)
                        dve.scalar_tensor_tensor(out=tmp[:, 0:hi - lo], in0=Srow[:, b, lo:hi], scalar=s, in1=in1,
                                                 op0=op, op1=ALU.mult,
                                                 accum_out=cnt[:, b, t, part:part + 1]).then_inc(S["cnt"], 1)
                        n_cnt += 1
                dve.wait_ge(S["cnt"], n_cnt)
                dve.tensor_reduce(rank[:, b], cnt[:, b], AX.X, ALU.add).then_inc(S["rank"], 1)
                dve.wait_ge(S["rank"], b + 1)
                dve.tensor_tensor(OH[:, b], iota[:, None, :].to_broadcast([P, ST, P]),
                                  rank[:, b, :, None].to_broadcast([P, ST, P]), ALU.is_equal).then_inc(S["oh"], 1)

            def rms(norm, src):
                ps = (psX, psO)[norm][:, 0:CR]
                dve.wait_ge(S["guess"], 3 * norm + 3)
                dve.scalar_tensor_tensor(out=y2[:, :], in0=ps, scalar=ATTN_LN_EPS, in1=y2[:, :], op0=ALU.add,
                                         op1=ALU.mult).then_inc(S["nw"], 1)
                dve.wait_ge(S["nw"], norm + 1)
                dve.scalar_tensor_tensor(out=y0[:, :], in0=y2[:, :], scalar=-1.5, in1=y0[:, :], op0=ALU.add,
                                         op1=ALU.mult).then_inc(S["rs"], 1)
                dve.wait_ge(S["rs"], norm + 1)
                dve.wait_ge(S["c_ng"], 1)
                if norm:
                    dve.wait_ge(S["qkv_mm"], 4)
                for c in range(KC):
                    dve.scalar_tensor_tensor(out=hT[:, c], in0=src[:, c], scalar=ng[:, norm, c:c + 1], in1=y0[:, :],
                                             op0=ALU.mult, op1=ALU.mult).then_inc(S["h"], 1)

            rms(0, xs)
            dve.wait_ge(S["qkv_mm"], 2)
            for b in range(BATCH):
                for c in range(KC):
                    dve.tensor_tensor(KB[:, b, c],
                                      psT[:, 1, None, c * CR + b * P:c * CR + (b + 1) * P].to_broadcast([P, HC, P]),
                                      headmask[:, :, None].to_broadcast([P, HC, P]), ALU.mult).then_inc(S["kb"], 1)
            dve.wait_ge(S["qkv_mm"], 4)
            for b in range(BATCH):
                dve.tensor_copy(V17[:, b, :, 0:HD], psO[:, b * D:(b + 1) * D].rearrange("p (h d) -> p h d", d=HD)) \
                    .then_inc(S["v"], 1)
            for i in range(NU + 1):
                if i < NU:
                    dve.wait_ge(S["sc_mm"], i + 1)
                    if i >= 2:
                        dve.wait_ge(S["t_mm"], 2 * (i - 1))
                    ps = psS[i % 2][:, :, :].rearrange("p g (h k) -> p (g h) k", k=P)
                    dve.tensor_tensor(Pb[:, i % 2], ps, causal[:, None, :].to_broadcast([P, HC, P]),
                                      ALU.add).then_inc(S["msk"], 1)
                    dve.wait_ge(S["msk"], i + 1)
                    dve.tensor_reduce(mx[:, i], Pb[:, i % 2], AX.X, ALU.max).then_inc(S["mx"], 1)
                    dve.wait_ge(S["mx"], i + 1)
                    dve.tensor_tensor(Pb[:, i % 2], Pb[:, i % 2], mx[:, i, :, None].to_broadcast([P, HC, P]),
                                      ALU.subtract).then_inc(S["sub"], 1)
                if i >= 1:
                    j = i - 1
                    dve.wait_ge(S["t_mm"], 2 * j + 2)
                    if j >= 2:
                        dve.wait_ge(S["pv"], j - 1)
                    dve.tensor_copy(PT[:, j % 2, HB:HC].rearrange("p h n -> p (h n)"), psT[:, 1]) \
                        .then_inc(S["tv"], 1)
                    dve.wait_ge(S["pv"], j + 1)
                    o = psO[:, 0:HC * (HD + 1)].rearrange("p (h d) -> p h d", d=HD + 1)
                    dve.reciprocal(rec[:, j], o[:, :, HD]).then_inc(S["rec"], 1)
                    dve.wait_ge(S["rec"], j + 1)
                    dve.tensor_tensor(Cx[:, j], o[:, :, 0:HD], rec[:, j, :, None].to_broadcast([P, HC, HD]),
                                      ALU.mult).then_inc(S["cx"], 1)
            dve.wait_ge(S["a_mm"], 1)
            dve.tensor_tensor(x1[:, 0], psX[:, 0:CR], xs[:, 0], ALU.add).then_inc(S["x1"], 1)
            dve.tensor_tensor(x1[:, 1], psX[:, CR:2 * CR], xs[:, 1], ALU.add).then_inc(S["x1"], 1)
            rms(1, x1)
            for k in range(DC):
                w = min(P, DFF - k * P)
                dve.wait_ge(S["sil"], k + 1)
                dve.wait_ge(S["f2_mm"], k // 2 * 2 + 2)
                ps = (psS[1][0:w, k // 2, (k % 2) * CR:(k % 2 + 1) * CR] if k < 4 else
                      psX[0:w, (k % 2) * CR:(k % 2 + 1) * CR])
                dve.tensor_tensor(sg[0:w, k], sg[0:w, k], ps, ALU.mult).then_inc(S["g"], 1)
            for i in range(TILES + 1):
                if i < TILES:
                    t = i
                    for c in range(KC):
                        dve.wait_ge(S["sct"], 2 * t + c + 1)
                        if t >= 2:
                            dve.wait_ge(S["st"], 16 * (t - 1))
                        dve.scalar_tensor_tensor(out=R[:, t % 2, c], in0=XF[:, c, t * TW:(t + 1) * TW], scalar=2.0,
                                                 in1=psS[t % 2][:, c], op0=ALU.mult, op1=ALU.add).then_inc(S["r"], 1)
                if i >= 1:
                    t = i - 1
                    dve.wait_ge(S["guess2"], 3 * t + 3)
                    dve.scalar_tensor_tensor(out=Z2[:, :], in0=psX[:, :], scalar=LN_EPS, in1=Z2[:, :], op0=ALU.add,
                                             op1=ALU.mult).then_inc(S["znw"], 1)
                    dve.wait_ge(S["znw"], t + 1)
                    dve.scalar_tensor_tensor(out=Z0[:, :], in0=Z2[:, :], scalar=-1.5, in1=Z0[:, :], op0=ALU.add,
                                             op1=ALU.mult).then_inc(S["zrs"], 1)
                    dve.wait_ge(S["zrs"], t + 1)
                    dve.tensor_tensor(R[:, t % 2], R[:, t % 2], Z0[:, None, :].to_broadcast([P, KC, TW]),
                                      ALU.mult).then_inc(S["out"], 1)
                if i < TILES:
                    dve.wait_ge(S["mean"], i + 1)
                    dve.tensor_tensor(R[:, i % 2], psT[:, 0, None, :].to_broadcast([P, KC, TW]), R[:, i % 2],
                                      ALU.subtract).then_inc(S["xc"], 1)

        @block.tensor
        def _(pe):
            pe.wait_ge(S["c_wr"], 1)
            for b in range(BATCH):
                for g in range(2):
                    cols = slice(b * SEQ + g * TW, b * SEQ + (g + 1) * TW)
                    for k in range(KC):
                        mm = pe.matmul(psS[b][:, g], wr[:, k], XF[:, k, cols], start=(k == 0), stop=(k == KC - 1))
                mm.then_inc(S["s_mm"], 1)
            for i in range(BATCH * ST // 2):
                if i >= 2:
                    pe.wait_ge(S["xn"], i - 1)
                for t in (2 * i, 2 * i + 1):
                    for c in range(KC):
                        o = (t % 2) * D + c * P
                        mm = pe.transpose(psT[:, i % 2, o:o + P], XF[:, c, t * P:(t + 1) * P], ident[:, :])
                mm.then_inc(S["xt_mm"], 1)
            for b in range(BATCH):
                pe.wait_ge(S["oh"], b + 1)
                pe.wait_ge(S["xn"], (b + 1) * ST // 2)
                pe.wait_ge(S["srow"], b + 1)
                for c in range(KC):
                    for t in range(ST):
                        mm = pe.matmul(psO[:, c * CR + b * P:c * CR + (b + 1) * P],
                                       xN[:, b * ST + t, c * P:(c + 1) * P], OH[:, b, t], start=(t == 0),
                                       stop=(t == ST - 1))
                    mm.then_inc(S["g_mm"], 1)
                for t in range(ST):
                    mm = pe.transpose(psS[b][:, t // 4, (t % 4) * P:(t % 4 + 1) * P], OH[:, b, t], ident[:, :])
                mm.then_inc(S["oht_mm"], 1)

            def mean_square(norm):
                pe.wait_ge(S["sq"], norm + 1)
                for k in range(KC):
                    mm = pe.matmul((psX, psO)[norm][:, 0:CR], ones_inv[:, :], sq[:, k], start=(k == 0),
                                   stop=(k == KC - 1))
                mm.then_inc(S["m_mm"], 1)

            mean_square(0)
            pe.wait_ge(S["w"], 80)
            pe.wait_ge(S["h"], KC)
            pe.wait_ge(S["xn"], BATCH * ST // 2)
            for part in range(2):
                for m in range(KC):
                    for k in range(KC):
                        mm = pe.matmul(psT[:, part, m * CR:(m + 1) * CR],
                                       Wqkv[:, k, part * D + m * P:part * D + (m + 1) * P], hT[:, k], start=(k == 0),
                                       stop=(k == KC - 1))
                mm.then_inc(S["qkv_mm"], 1)
            for b in range(BATCH):
                for k in range(KC):
                    mm = pe.matmul(psO[:, b * D:(b + 1) * D], hT[:, k, b * P:(b + 1) * P], Wqkv[:, k, 2 * D:3 * D],
                                   start=(k == 0), stop=(k == KC - 1))
                mm.then_inc(S["qkv_mm"], 1)
            for i in range(NU + 3):
                if i < NU:
                    b, c = i // KC, i % KC
                    if i == 0:
                        pe.wait_ge(S["q"], 1)
                        pe.wait_ge(S["oht"], BATCH)
                    pe.wait_ge(S["kb"], i + 1)
                    if i >= 2:
                        pe.wait_ge(S["msk"], i - 1)
                    for g in range(2):
                        mm = pe.matmul(psS[i % 2][:, g], qT[:, c, b * P:(b + 1) * P],
                                       KB[:, b, c, g * HB:(g + 1) * HB].rearrange("p h k -> p (h k)"), start=True,
                                       stop=True)
                    mm.then_inc(S["sc_mm"], 1)
                if 1 <= i <= NU:
                    j = i - 1
                    b, c = j // KC, j % KC
                    pe.wait_ge(S["exp"], j + 1)
                    if j == 0:
                        pe.wait_ge(S["kb"], NU)
                    for g in range(2):
                        if j:
                            pe.wait_ge(S[("ta", "tv")[g]], j)
                        for h in range(HB):
                            mm = pe.transpose(psT[:, g, h * P:(h + 1) * P], Pb[:, j % 2, g * HB + h], ident[:, :])
                        mm.then_inc(S["t_mm"], 1)
                    pe.wait_ge(S["ta"], j + 1)
                    pe.wait_ge(S["tv"], j + 1)
                    pe.wait_ge(S["v"], BATCH)
                    if j:
                        pe.wait_ge(S["cx"], j)
                    for h in range(HC):
                        mm = pe.matmul(psO[:, h * (HD + 1):(h + 1) * (HD + 1)], PT[:, j % 2, h],
                                       V17[:, b, c * HC + h], start=True, stop=True)
                    mm.then_inc(S["pv"], 1)
                if i >= 2 and i - 2 < NU:
                    j = i - 2
                    pe.wait_ge(S["cx"], j + 1)
                    pe.wait_ge(S["rs"], 1)
                    if j:
                        pe.wait_ge(S["ot"], j)
                    pe.transpose(psX[:, 0:P], Cx[:, j].rearrange("p h d -> p (h d)"), ident[:, :]) \
                        .then_inc(S["c_mm"], 1)
            pe.wait_ge(S["ot"], NU)
            for m in range(KC):
                for k in range(KC):
                    mm = pe.matmul(psX[:, m * CR:(m + 1) * CR], Wout[:, k, m * P:(m + 1) * P], oT[:, k],
                                   start=(k == 0), stop=(k == KC - 1))
            mm.then_inc(S["a_mm"], 1)
            mean_square(1)
            pe.wait_ge(S["h"], 2 * KC)
            pe.wait_ge(S["x1"], KC)
            for k in range(DC):
                w = min(P, DFF - k * P)
                for part, name in ((0, "f1_mm"), (1, "f2_mm")):
                    ps = (psS[part][0:w, k // 2, (k % 2) * CR:(k % 2 + 1) * CR] if k < 4 else
                          (psT[0:w, 0], psX[0:w])[part][:, (k % 2) * CR:(k % 2 + 1) * CR])
                    for j in range(KC):
                        mm = pe.matmul(ps, W12[:, part, j, k * P:k * P + w], hT[:, j], start=(j == 0),
                                       stop=(j == KC - 1))
                    mm.then_inc(S[name], 1)
            pe.wait_ge(S["rs"], 2)
            for b in range(BATCH):
                for k in range(KC):
                    pe.matmul(psO[:, b * D:(b + 1) * D], oT[:, k, b * P:(b + 1) * P], Wout[:, k, :], start=(k == 0),
                              stop=False)
                for k in range(DC):
                    w = min(P, DFF - k * P)
                    pe.wait_ge(S["g"], k + 1)
                    mm = pe.matmul(psO[:, b * D:(b + 1) * D], sg[0:w, k, b * P:(b + 1) * P], W3[0:w, k, :],
                                   start=False, stop=(k == DC - 1))
            mm.then_inc(S["d_mm"], 1)
            pe.wait_ge(S["d"], 1)
            for i in range(TILES + 2):
                if i < TILES:
                    b, t = i // BT, i
                    for c in range(KC):
                        if t >= 2:
                            pe.wait_ge(S["r"], 2 * (t - 2) + c + 1)
                        pe.matmul(psS[t % 2][:, c], dN[:, b, c * P:(c + 1) * P],
                                  OHT[:, b, (t % BT) * TW:(t % BT + 1) * TW], start=True,
                                  stop=True).then_inc(S["sct"], 1)
                if 1 <= i <= TILES:
                    t = i - 1
                    pe.wait_ge(S["rsum"], t + 1)
                    if t:
                        pe.wait_ge(S["xc"], t)
                    pe.matmul(psT[:, 0], ones_inv[:, :], RS[:, :], start=True, stop=True).then_inc(S["mean"], 1)
                    pe.wait_ge(S["ss"], t + 1)
                    if t:
                        pe.wait_ge(S["znw"], t)
                    pe.matmul(psX[:, :], ones_inv[:, :], SS[:, :], start=True, stop=True).then_inc(S["var"], 1)


def constants(nc, sem, ones_inv, consts):
    s = sem("const")
    with nc.Block() as block:
        @block.gpsimd
        def _(pool):
            pool.memset(ones_inv[:, :], 1.0 / D).then_inc(s, 1)
            pool.memset(consts[:, 0:1], ATTN_LN_EPS).then_inc(s, 1)
            pool.memset(consts[:, 1:2], LN_EPS).then_inc(s, 1)
            pool.wait_ge(s, 3)


def head_constants(nc, sem, ident, headmask):
    s = sem("headconst")
    with nc.Block() as block:
        @block.gpsimd
        def _(pool):
            pool.memset(ident[:, :], 0.0).then_inc(s, 1)
            pool.memset(headmask[:, :], 1.0).then_inc(s, 1)
            pool.wait_ge(s, 2)
            pool.affine_select(out=ident[:, :], in_=ident[:, :], compare_op=ALU.not_equal, fill=1.0, base=0,
                               pattern=[[-1, P]], channel_multiplier=1).then_inc(s, 1)
            pool.affine_select(out=headmask[:, :], in_=headmask[:, :], compare_op=ALU.is_ge, fill=0.0, base=0,
                               pattern=[[-HD, HC]], channel_multiplier=1).then_inc(s, 1)
            pool.wait_ge(s, 4)
            pool.affine_select(out=headmask[:, :], in_=headmask[:, :], compare_op=ALU.is_ge, fill=0.0, base=HD - 1,
                               pattern=[[HD, HC]], channel_multiplier=-1).then_inc(s, 1)
            pool.wait_ge(s, 5)


def program(nc, x_t, vecs, w_qkvo, w1, w2, ctx_t, cvecs, cw, fvecs, f_qkv, f_out, f_w12, f_w3, out_t):
    with ExitStack() as ctx:
        def sem(name):
            return ctx.enter_context(nc.semaphore(name))

        def sb(name, shape):
            return ctx.enter_context(nc.sbuf_tensor(name, shape, F32))

        XF = sb("XF", [P, KC, TOKENS])
        ones_inv, consts = sb("ones_inv", [P, P]), sb("consts", [P, 2])
        constants(nc, sem, ones_inv, consts)
        with ExitStack() as stage:
            own = []

            def layers_sem(name):
                own.append(stage.enter_context(nc.semaphore(name)))
                return own[-1]

            layers_stage(nc, layers_sem, XF, ones_inv, consts, x_t, vecs, w_qkvo, w1, w2)
            clear_semaphores(nc, own)
        ident, headmask = sb("ident", [P, P]), sb("headmask", [P, HC])
        head_constants(nc, sem, ident, headmask)
        cross_stage(nc, sem, XF, ones_inv, consts, ident, headmask, x_t, ctx_t, cvecs, cw)
        routed_stage(nc, sem, XF, ones_inv, consts, ident, headmask, out_t, fvecs, f_qkv, f_out, f_w12, f_w3)


def clear_semaphores(nc, sems):
    with nc.Block() as block:
        @block.gpsimd
        def _(pool):
            for s in sems:
                pool.sem_clear(s)


def kernel(**inputs):
    import numpy as np
    import concourse.bacc as bacc
    from concourse import mybir as _mybir
    from concourse.bass_utils import run_bass_kernel_spmd

    i = {k: np.asarray(v) for k, v in inputs.items()}
    a = lambda n: i["L0_attn_" + n]
    x = lambda n: i["L0_xattn_" + n]
    f = lambda n: i["L0_ffn_" + n]

    def per_feature(v):
        return np.moveaxis(v.reshape(*v.shape[:-1], -1, P), -1, 0)

    def rows_in(w):
        return np.moveaxis(w.reshape(*w.shape[:-2], -1, P, w.shape[-1]), -2, -3)

    arrays = {
        "x_t": i["x"].reshape(TOKENS, D).T,
        "vecs": np.concatenate([per_feature(a(n)) for n in ("bq", "bk", "bv", "bo", "ln1_s", "ln1_b", "b1", "b2",
                                                            "ln2_s", "ln2_b")], axis=2).reshape(P, -1),
        "w_qkvo": np.stack([rows_in(a(n)) for n in ("Wq", "Wk", "Wv", "Wo")], axis=2).reshape(LAYERS * P, -1),
        "w1": rows_in(a("W1")).reshape(LAYERS * P, -1),
        "w2": rows_in(a("W2")).reshape(LAYERS * P, -1),
        "ctx_t": i["ctx_1024"].reshape(BATCH * KEYS, D).T,
        "cvecs": per_feature(np.stack([x(n) for n in ("bq", "bk", "bv", "bo")])).reshape(P, -1),
        "cw": np.stack([rows_in(x(n).T) for n in ("Wq", "Wk", "Wv", "Wo")], axis=1).reshape(P, -1),
        "fvecs": per_feature(np.stack([f(n) for n in ("w_router", "g1", "g2")])).reshape(P, -1),
        "f_qkv": rows_in(f("W_qkv").T).reshape(P, -1),
        "f_out": rows_in(f("W_out").T).reshape(P, -1),
        "f_w12": np.stack([rows_in(f(n).T) for n in ("W1", "W2")], axis=1).reshape(P, -1),
        "f_w3": f("W3").T,
    }
    arrays = {k: np.ascontiguousarray(v) for k, v in arrays.items()}
    nc = bacc.Bacc("TRN2", target_bir_lowering=False, num_devices=1)
    args = {k: nc.dram_tensor(k, v.shape, _mybir.dt.from_np(v.dtype), kind="ExternalInput").ap()
            for k, v in arrays.items()}
    args["out_t"] = nc.dram_tensor("out_t", (D, TOKENS), F32, kind="ExternalOutput").ap()
    program(nc, **args)
    r = run_bass_kernel_spmd(nc, [arrays], core_ids=[0])
    return np.ascontiguousarray(r.results[0]["out_t"].T).reshape(BATCH, SEQ, D)
```

```python
from contextlib import ExitStack

import concourse.bass as bass
from concourse import mybir

F32 = mybir.dt.float32
F32R = mybir.dt.float32r
BF16 = mybir.dt.bfloat16
ALU = mybir.AluOpType
ACT = mybir.ActivationFunctionType
AX = mybir.AxisListType

P = 128
BATCH, SEQ, D = 2, 1024, 256
TOKENS = BATCH * SEQ
LAYERS = 4
FF = 1024
KC = D // P
FC = FF // P
TW = 512
TILES = TOKENS // TW
ATTN_LN_EPS = 1e-6
LN_EPS = 1e-5
LOG_EXP, GELU, SILU = "natural_log_exp_and_others", "gelu_apprx_tanh_and_others", "silu_and_others"

_PARTS = (("bq", KC), ("bk", KC), ("bv", KC), ("bo", KC), ("ln1_s", KC), ("ln1_b", KC),
          ("b1", FC), ("b2", KC), ("ln2_s", KC), ("ln2_b", KC))
VEC = {name: sum(n for _, n in _PARTS[:i]) for i, (name, _) in enumerate(_PARTS)}
NVEC = sum(n for _, n in _PARTS)

def steps_of(text):
    return [(w.rstrip("+")[:-1], int(w.rstrip("+")[-1]), int(w[-1] == "+")) for w in text.split()]


PE_ORDER = steps_of("""
    U11 U21 M20 O2 D01 R20 U31 D11 D21 O3 M12 D31 R1a2 M13 Ak0+ Aq0+ R1a3 M21 U02 U12 R21 U22 D02 U32 Av0+
    Ak1+ Av1+ D12 Aq1+ D22 D32 U03 U13 O0+ U23 M22 D03 U33 D13 R22 O1+ M10+ D23 D33 R1a0+ M11+ Ak2+ M23 R1a1+
    Av2+ U00+ U10+ R23 U20+ U30+ D00+ Aq2+ Ak3+ D10+ Av3+ Aq3+ D20+ D30+ U01+
    """)
ACT_ORDER = steps_of("""
    Va2 T0 U01 Vb2 U11 Va3 M20 U21 R20 Vb3 O2 U31 X0+ WQ0+ O3 M12 T1 R1a2 M13 Ak0+ R1b2 Aq0+ R1a3 M21 U02 R21
    U12 U22 WO0+ X1+ R1b3 U32 Ak1+ Va0+ Aq1+ T2 Vb0+ U03 U13 Va1+ O0+ Vb1+ M22 U23 U33 R22 O1+ W10+ M10+ X2+
    T3 R1a0+ M11+ Ak2+ R1b0+ W20+ R1a1+ M23 U00+ U10+ R23 U20+ U30+ X3+ R1b1+ Aq2+ Ak3+ Aq3+
    """)
DVE_ORDER = steps_of("""
    T0 U01 Va3 U11 M20 Vc3 U21 R20 O2 U31 M12 O3 WQ0+ T1 VA0+ M13 R1a2 Ak0+ M21 Aq0+ R1a3 U02 R21 U12 VN2
    WO0+ U22 Av0+ Ak1+ Av1+ Va0+ U32 Vc0+ Aq1+ U03 T2 VN0+ Va1+ U13 Vc1+ M22 U23 U33 O0+ R22 M10+ O1+ W10+
    VA2+ T3 M11+ R1a0+ M23 Ak2+ Av2+ W20+ R1a1+ U00+ U10+ R23 U20+ Aq2+ Ak3+ Av3+ U30+ Va2+ Aq3+ Vc2+
    """)
POOL_ORDER = steps_of("""
    X0+ M12 O3 T1 M13 R1b2 M21 U02 U12 X1+ R1b3 U22 U32 Vb0+ T2 U03 U13 Vb1+ M22 U23 O0+ U33 O1+ M10+ X2+ T3
    M11+ R1b0+ M23 U00+ U10+ X3+ U20+ R1b1+ U30+ T0+ Vb2+ U01+ M20+ U11+ U21+ Vb3+ O2+ U31+
    """)
PE_FIRST = steps_of("""
    Ak0+ Aq0+ Av0+ Ak1+ Av1+ Aq1+ O0+ M10+ O1+ R1a0+ Ak2+ M11+ Av2+ U00+ U10+ R1a1+ U20+ U30+ D00+ Aq2+ Ak3+
    D10+ Av3+ Aq3+ U01+ D20+ D30+
    """)
PE_LAST = steps_of("""
    U11 M20 U21 D01 O2 U31 D11 R20 M12 O3 R1a2 D21 D31 U02 M13 U12 M21 R1a3 U22 U32 D02 D12 U03 R21 U13 D22
    D32 U23 D03 D13 U33 D23 M22 D33 R22 M23 R23
    """)
ACT_FIRST = steps_of("""
    X0+ WQ0+ WO0+ X1+ Ak0+ Aq0+ Ak1+ Va0+ Aq1+ Vb0+ Va1+ O0+ X2+ Vb1+ W10+ M10+ O1+ R1a0+ Ak2+ R1b0+ M11+
    U00+ X3+ W20+ U10+ U20+ U30+ R1a1+ Aq2+ Ak3+ R1b1+ Aq3+
    """)
ACT_LAST = steps_of("""
    Va2 T0 U01 Vb2 U11 Va3 M20 U21 Vb3 O2 U31 R20 M12 R1a2 O3 R1b2 T1 U02 M13 U12 R1a3 U22 M21 R1b3 U32 U03
    R21 U13 T2 U23 U33 M22 T3 R22 M23 R23
    """)
DVE_FIRST = steps_of("""
    VA0+ WQ0+ Ak0+ Aq0+ Av0+ Ak1+ Av1+ Va0+ WO0+ Vc0+ Aq1+ Va1+ VN0+ Vc1+ O0+ M10+ VA2+ W10+ O1+ R1a0+ M11+
    Ak2+ Av2+ U00+ U10+ W20+ U20+ R1a1+ Aq2+ Ak3+ Av3+ U30+ Va2+ Aq3+ Vc2+
    """)
DVE_LAST = steps_of("""
    T0 U01 Va3 U11 M20 Vc3 U21 O2 U31 M12 R20 R1a2 T1 O3 M13 U02 M21 U12 R1a3 U22 VN2 U32 U03 U13 R21 U23 T2
    U33 M22 T3 M23 R22 R23
    """)
POOL_FIRST = steps_of("""
    X0+ X1+ Vb0+ O0+ Vb1+ X2+ M10+ O1+ R1b0+ M11+ U00+ X3+ U10+ U20+ R1b1+ U30+ T0+ Vb2+ U01+ U11+ M20+ U21+
    Vb3+ O2+ U31+
    """)
POOL_LAST = steps_of("""
    M12 R1b2 O3 T1 M13 U02 U12 R1b3 M21 U22 U32 U03 U13 U23 T2 U33 M22 T3 M23
    """)
M_STEPS, R_STEPS = ("M1", "M2"), ("R1a", "R2")
JOBS = [(s[1] if s[0] == "A" else s[0].lower(), t, int(s[1]) if s[0] == "U" else 0, n)
        for s, t, n in PE_ORDER if s[0] in "AOU"]
for first, order, last in ((PE_FIRST, PE_ORDER, PE_LAST), (ACT_FIRST, ACT_ORDER, ACT_LAST),
                           (DVE_FIRST, DVE_ORDER, DVE_LAST), (POOL_FIRST, POOL_ORDER, POOL_LAST)):
    for part, n in ((first, 1), (last, 0)):
        for steps in (M_STEPS, R_STEPS, ("Ak", "Av", "Aq", "O", "U0", "U1", "U2", "U3")):
            assert [x for x in part if x[0] in steps] == [x for x in order if x[0] in steps and x[2] == n]
        assert sorted(part) == sorted(x for x in order if x[2] == n)
assert len(JOBS) == TILES * (4 + FC // 2) and len(JOBS) % 2 == 0
JOB_AT = {j[:3]: i for i, j in enumerate(JOBS)}


def layers_stage(nc, sem, XF, ones_inv, consts, x_t, vecs, w_qkvo, w1, w2):
    with ExitStack() as ctx:
        def sb(name, shape, dt=F32):
            return ctx.enter_context(nc.sbuf_tensor(name, shape, dt))

        stgA = sb("stgA", [P, 4, KC, D])
        stgB = sb("stgB", [P, KC * FF])
        WAh, WAl = sb("WAh", [P, 4, KC, D], F32R), sb("WAl", [P, 4, KC, D], F32R)
        W1h, W1l = sb("W1h", [P, KC, FF], F32R), sb("W1l", [P, KC, FF], F32R)
        W2h, W2l = sb("W2h", [P, FC, D], F32R), sb("W2l", [P, FC, D], F32R)
        allvec = sb("allvec", [P, LAYERS * NVEC])
        vec = [sb(f"vec{b}", [P, VEC["ln2_s"]]) for b in range(BATCH)]
        vn = [sb(f"vn{b}", [P, 2 * KC]) for b in range(BATCH)]
        plus = [{n: sb(f"plus_{n}{b}", [P, KC]) for n in ("bq", "bk")} for b in range(BATCH)]
        minus = [{n: sb(f"minus_{n}{b}", [P, KC]) for n in ("bq", "bk", "ln1_s", "ln2_s")} for b in range(BATCH)]

        xh, xl = sb("xh", [P, 2, KC, TW], F32R), sb("xl", [P, 2, KC, TW], F32R)
        Ek, Eq = sb("Ek", [P, KC, TW]), sb("Eq", [P, KC, TW])
        Q = sb("Q", [P, KC, TOKENS])
        kpart, kvpart = sb("kpart", [P, KC, TILES]), sb("kvpart", [P, KC, TILES])
        ksum, nkvsum = sb("ksum", [P, KC, BATCH]), sb("nkvsum", [P, KC, BATCH])
        den, rec = sb("den", [P, KC, TW]), sb("rec", [P, KC, TW])
        vh, vl = sb("vh", [P, KC, TW], F32R), sb("vl", [P, KC, TW], F32R)
        R = {1: sb("R1", [P, 2, KC, TW]), 2: sb("R2", [P, 2, KC, TW])}
        RS = {n: sb(f"RS{n}", [P, TW]) for n in (1, 2)}
        SQ = sb("SQ", [P, KC, TW])
        SS = sb("SS", [P, TW])
        Y0, Y2 = sb("Y0", [P, TW]), sb("Y2", [P, TW])
        x1 = sb("x1", [P, 2, KC, TW])
        x1h, x1l = sb("x1h", [P, KC, TW], F32R), sb("x1l", [P, KC, TW], F32R)
        HF = sb("HF", [P, 4, TW])
        hh, hl = sb("hh", [P, 4, TW], F32R), sb("hl", [P, 4, TW], F32R)

        pair = [ctx.enter_context(nc.psum_tensor(f"pair{i}", [P, KC, TW], F32)) for i in range(2)]
        pD = ctx.enter_context(nc.psum_tensor("pD", [P, KC, TW], F32))
        pMean = ctx.enter_context(nc.psum_tensor("pMean", [P, TW], F32))
        pVar = ctx.enter_context(nc.psum_tensor("pVar", [P, TW], F32))

        per_tile = {"k_mm": 1, "v_mm": 1, "q_mm": 1, "o_mm": 1, "u_mm": 4, "d_mm": 4,
                    "nk": 2, "nq": 2, "ek": 1, "eq": 1, "ekr": 1, "eqr": 1, "kdone": 2, "qdone": 2, "kvdone": 2,
                    "den": 2, "lnd": 1, "rec0": 1, "dy": 1, "rec": 1, "vdone": 2, "vh": 1, "vl": 1, "xh": 1, "xl": 1,
                    "go": 2, "go2": 1, "gd": 2, "r1": 1, "r2": 1, "x1": 2, "x1h": 1, "x1l": 1,
                    "h": 8, "hh": 8, "hl_dve": 4, "hl_pool": 4, "xnew": 2}
        for kind in ("mean_mm", "var_mm", "rs", "xc", "sq", "ss", "newton", "rstd", "y"):
            per_tile[kind + "1"] = per_tile[kind + "2"] = 1
        per_tile["guess1"] = per_tile["guess2"] = 3
        per_layer = {"wh": 4, "wl": 4, "sums": 4, **{f"vec{b}": 6 for b in range(BATCH)},
                     **{f"vn{b}": 2 for b in range(BATCH)}}
        S = {n: sem("l_" + n) for n in (*per_tile, *per_layer)}
        s_stgA, s_stgB, s_allvec = (sem("l_" + n) for n in ("stgA", "stgB", "allvec"))
        s_x = [sem(f"l_xload{t}") for t in range(TILES)]
        both = lambda *names: [n + k for n in names for k in "12"]
        owners = {"pe": ["k_mm", "v_mm", "q_mm", "o_mm", "u_mm", "d_mm", *both("mean_mm", "var_mm")],
                  "act": ["lnd", "rec0", "nk", "nq", "ek", "eq", "vh", "xh", "go", "go2", "gd", "x1h", "h", "wh",
                          *both("sq", "guess")],
                  "dve": ["ekr", "eqr", "kdone", "qdone", "kvdone", "den", "dy", "rec", "vdone", "r1", "r2", "x1", "hh",
                          "hl_dve", "wl", "sums", "vec0", "vec1", "vn0", "vn1", *both("xc", "newton", "rstd", "y")],
                  "pool": ["vl", "xl", "x1l", "hl_pool", *both("rs", "ss")]}

        def start_counts(eng, who):
            for n in owners[who]:
                eng.sem_inc(S[n], TILES * per_tile[n] if n in per_tile else per_layer[n])

        def tile_event(eng, name, L, t, n=None):
            e = per_tile[name]
            eng.wait_ge(S[name], L * (e * TILES) + (e * t + (e if n is None else n + 1)))

        def weights_event(eng, name, L, i):
            eng.wait_ge(S[name], L * 4 + (i + 1))

        def vectors_event(eng, L, b, n=6):
            eng.wait_ge(S[f"vec{b}"], L * 6 + n)

        def norm_vectors_event(eng, L, b):
            eng.wait_ge(S[f"vn{b}"], L * 2 + 2)

        def before(seq, i, turn):
            found = []
            for k in range(1, len(seq)):
                item, n = seq[(i - k) % len(seq)]
                wrapped = k > i
                if turn == "first" and (wrapped or n == 0) or turn == "last" and not wrapped and n == 1:
                    if turn == "first" and wrapped:
                        break
                    continue
                if not found or n == 1:
                    found.append((item, n - wrapped))
                if n == 1 or not wrapped or turn == "last":
                    break
            return found

        PAIRS = [[(j[:3], j[3]) for j in JOBS[i::2]] for i in range(2)]

        def norm_before(eng, order, steps, name, norm, t, n, LT, turn):
            seq = [((steps.index(s) + 1, tt), nn) for s, tt, nn in order if s in steps]
            for (k, tt), nn in before(seq, seq.index(((norm, t), n)), turn):
                tile_event(eng, f"{name}{k}", LT + nn, tt)

        def slot(what, t, j=0):
            return pair[JOB_AT[what, t, j] % 2]

        def slot_free(eng, what, t, j, n, LT, turn):
            seq = PAIRS[JOB_AT[what, t, j] % 2]
            for (w, tt, jj), nn in before(seq, seq.index(((what, t, j), n)), turn):
                name, e = {"k": ("kdone", 1), "v": ("kvdone", 1), "q": ("qdone", 1), "o": ("go", 1),
                           "u": ("h", 2 * jj + 1)}[w]
                tile_event(eng, name, LT + nn, tt, e)

        def turns(eng, first, order, last, step):
            for s, t, n in first:
                step(s, t, n, 1, 0, "first")
            with eng.Fori(1, LAYERS) as LT:
                for s, t, n in order:
                    step(s, t, n, LT + n, LT, "all")
            for s, t, n in last:
                step(s, t, n, LAYERS, LAYERS, "last")

        def col(name, t, c):
            return vec[t // 2][:, VEC[name] + c:VEC[name] + c + 1]

        def chunks(t):
            return slice(t * TW, (t + 1) * TW)

        def three(eng, out, wh, wl, h, l, start, stop):
            eng.matmul(out, wh, l, start=start, stop=False)
            eng.matmul(out, wl, h, start=False, stop=False)
            return eng.matmul(out, wh, h, start=False, stop=stop)

        block = ctx.enter_context(nc.Block())

        @block.sync
        def _(sp):
            x_in = x_t.rearrange("(k p) n -> p k n", p=P)
            sp.dma_start(XF[:, :, chunks(0)], x_in[:, :, chunks(0)]).then_inc(s_x[0], 16)
            sp.dma_start(allvec[:, :], vecs).then_inc(s_allvec, 16)
            with sp.Fori(1, LAYERS + 1) as L:
                weights_event(sp, "wl", L - 1, 1)
                sp.dma_start(stgA[:, :, :, :].rearrange("p w k n -> p (w k n)"),
                             w_qkvo[bass.ds((L - 1) * P, P), :]).then_inc(s_stgA, 16)
                weights_event(sp, "wl", L - 1, 3)
                sp.dma_start(stgB[:, :], w1[bass.ds((L - 1) * P, P), :]).then_inc(s_stgB, 16)
                weights_event(sp, "wl", L, 2)
                sp.dma_start(stgB[:, :], w2[bass.ds((L - 1) * P, P), :]).then_inc(s_stgB, 16)

        def weight_parts(i):
            if i < 2:
                w = slice(0, 3) if i == 0 else slice(3, 4)
                return tuple(x[:, w, :, :].rearrange("p w k n -> p (w k n)") for x in (stgA, WAh, WAl))
            a, b = ((W1h, W1l), (W2h, W2l))[i - 2]
            return stgB[:, :], a[:, :, :].rearrange("p k n -> p (k n)"), b[:, :, :].rearrange("p k n -> p (k n)")

        WSTEP = {"WQ": 0, "WO": 1, "W1": 2, "W2": 3}

        def weights_staged(eng, i, L):
            if i < 2:
                eng.wait_ge(s_stgA, L * 16)
            else:
                eng.wait_ge(s_stgB, L * 32 - 16 * (3 - i))

        def weights_used(eng, i, L):
            tile_event(eng, ("q_mm", "o_mm", "u_mm", "d_mm")[i], L - 1, TILES - 1)

        @block.scalar
        def _(act):
            x_in = x_t.rearrange("(k p) n -> p k n", p=P)
            for t in range(1, TILES):
                act.dma_start(XF[:, :, chunks(t)], x_in[:, :, chunks(t)]).then_inc(s_x[t], 16)
            start_counts(act, "act")
            table = {}

            def act_step(step, t, n, L, LT, turn):
                need = {"Ak": LOG_EXP, "Aq": LOG_EXP, "Va": LOG_EXP, "R1a": LOG_EXP, "R2": LOG_EXP, "O": GELU,
                        "T": GELU}.get(step, GELU if step[0] == "U" else None)
                if need and need != table.get(turn):
                    act.preload_act_table_set(need)
                    table[turn] = need
                if step in WSTEP:
                    i = WSTEP[step]
                    w, wh, _ = weight_parts(i)
                    weights_staged(act, i, L)
                    weights_used(act, i, L)
                    act.activation(wh, w, ACT.Copy).then_inc(S["wh"], 1)
                if step == "X":
                    tile_event(act, "xnew", L - 1, t)
                    tile_event(act, "q_mm", L, t - 2)
                    act.activation(xh[:, t % 2], XF[:, :, chunks(t)], ACT.Copy).then_inc(S["xh"], 1)
                if step in ("Ak", "Aq"):
                    what, E, neg, done, used = {"Ak": ("k", Ek, "nk", "ek", "kvdone"),
                                                "Aq": ("q", Eq, "nq", "eq", "qdone")}[step]
                    vectors_event(act, L, t // 2)
                    tile_event(act, what + "_mm", L, t)
                    for c in range(KC):
                        tile_event(act, used, L, t - 1, c)
                        act.activation(E[:, c], slot(what, t)[:, c], ACT.Relu,
                                       bias=minus[t // 2]["b" + what][:, c:c + 1], scale=-1.0).then_inc(S[neg], 1)
                    tile_event(act, neg, L, t)
                    act.activation(E[:, :, :], E[:, :, :], ACT.Exp, scale=-1.0).then_inc(S[done], 1)
                if step == "Va":
                    tile_event(act, "den", L, t)
                    tile_event(act, "rec", L, t - 1)
                    act.activation(rec[:, :, :], den[:, :, :], ACT.Ln).then_inc(S["lnd"], 1)
                    tile_event(act, "lnd", L, t)
                    act.activation(rec[:, :, :], rec[:, :, :], ACT.Exp, scale=-1.0).then_inc(S["rec0"], 1)
                if step == "Vb":
                    tile_event(act, "vdone", L, t)
                    tile_event(act, "o_mm", L, t - 1)
                    act.activation(vh[:, :, :], Q[:, :, chunks(t)], ACT.Copy).then_inc(S["vh"], 1)
                if step == "O":
                    tile_event(act, "o_mm", L, t)
                    tile_event(act, "x1", L, t - 2)
                    for c in range(KC):
                        act.activation(R[1][:, t % 2, c], slot("o", t)[:, c], ACT.Gelu_apprx_tanh,
                                       bias=col("bo", t, c)).then_inc(S["go"], 1)
                    tile_event(act, "go", L, t)
                    act.activation(R[1][:, t % 2], R[1][:, t % 2], ACT.Gelu_apprx_tanh).then_inc(S["go2"], 1)
                if step in ("M1", "M2"):
                    k = int(step[1])
                    tile_event(act, f"xc{k}", L, t)
                    norm_before(act, ACT_ORDER, M_STEPS, "ss", k, t, n, LT, turn)
                    act.activation(SQ[:, :, :], R[k][:, t % 2], ACT.Square).then_inc(S[f"sq{k}"], 1)
                if step in ("R1a", "R2"):
                    k = int(step[1])
                    guess = f"guess{k}"
                    tile_event(act, f"var_mm{k}", L, t)
                    norm_before(act, ACT_ORDER, R_STEPS, "y", k, t, n, LT, turn)
                    act.activation(Y0[:, :], pVar[:, :], ACT.Ln, bias=consts[:, 0:1]).then_inc(S[guess], 1)
                    tile_event(act, guess, L, t, 0)
                    act.activation(Y0[:, :], Y0[:, :], ACT.Exp, scale=-0.5).then_inc(S[guess], 1)
                    tile_event(act, guess, L, t, 1)
                    act.activation(Y2[:, :], Y0[:, :], ACT.Square, scale=0.5 ** 0.5).then_inc(S[guess], 1)
                if step == "R1b":
                    tile_event(act, "x1", L, t)
                    tile_event(act, "u_mm", L, t - 1)
                    act.activation(x1h[:, :, :], x1[:, t % 2], ACT.Copy).then_inc(S["x1h"], 1)
                if step[0] == "U":
                    for f in (2 * int(step[1]), 2 * int(step[1]) + 1):
                        tile_event(act, "u_mm", L, t, f // 2)
                        tile_event(act, "hl_pool" if f % 2 else "hl_dve", L, t, f // 2 - 2)
                        act.activation(HF[:, f % 4], slot("u", t, f // 2)[:, f % 2], ACT.Gelu_apprx_tanh,
                                       bias=col("b1", t, f)).then_inc(S["h"], 1)
                if step == "T":
                    tile_event(act, "d_mm", L, t)
                    tile_event(act, "xnew", L, t - 2)
                    for c in range(KC):
                        act.activation(R[2][:, t % 2, c], pD[:, c], ACT.Gelu_apprx_tanh,
                                       bias=col("b2", t, c)).then_inc(S["gd"], 1)

            turns(act, ACT_FIRST, ACT_ORDER, ACT_LAST, act_step)

        @block.vector
        def _(dve):
            start_counts(dve, "dve")
            for t in range(TILES):
                dve.wait_ge(s_x[t], 16)
                dve.sem_inc(S["xnew"], per_tile["xnew"])
            dve.wait_ge(s_allvec, 16)

            def dve_step(step, t, n, L, LT, turn):
                b = t // 2
                if step == "VA":
                    vs = S[f"vec{b}"]
                    tile_event(dve, "h", L - 1, t + 1)
                    tile_event(dve, "gd", L - 1, t + 1)
                    tile_event(dve, "x1", L - 1, t + 1)
                    dve.tensor_scalar(vec[b][:, :], allvec[:, bass.ds((L - 1) * NVEC, VEC["ln2_s"])], 1.0, None,
                                      ALU.mult).then_inc(vs, 1)
                    vectors_event(dve, L, b, 1)
                    for name in ("bq", "bk"):
                        v = vec[b][:, VEC[name]:VEC[name] + KC]
                        dve.tensor_scalar(plus[b][name][:, :], v, 1.0, None, ALU.add).then_inc(vs, 1)
                        dve.tensor_scalar(minus[b][name][:, :], v, -1.0, None, ALU.mult).then_inc(vs, 1)
                    dve.tensor_scalar(minus[b]["ln1_s"][:, :], vec[b][:, VEC["ln1_s"]:VEC["ln1_s"] + KC], -1.0,
                                      None, ALU.mult).then_inc(vs, 1)
                    vectors_event(dve, L, b)
                if step == "VN":
                    tile_event(dve, "xnew", L - 1, t + 1)
                    dve.tensor_scalar(vn[b][:, :], allvec[:, bass.ds((L - 1) * NVEC + VEC["ln2_s"], 2 * KC)], 1.0, None,
                                      ALU.mult).then_inc(S[f"vn{b}"], 1)
                    dve.wait_ge(S[f"vn{b}"], L * 2 + 1)
                    dve.tensor_scalar(minus[b]["ln2_s"][:, :], vn[b][:, 0:KC], -1.0, None,
                                      ALU.mult).then_inc(S[f"vn{b}"], 1)
                if step in WSTEP:
                    i = WSTEP[step]
                    w, wh, wl = weight_parts(i)
                    weights_event(dve, "wh", L, i)
                    dve.tensor_tensor(wl, w, wh.bitcast(F32), ALU.subtract).then_inc(S["wl"], 1)
                if step == "Av":
                    tile_event(dve, "v_mm", L, t)
                    tile_event(dve, "kdone", L, t)
                    for c in range(KC):
                        dve.scalar_tensor_tensor(
                            out=Ek[:, c], in0=slot("v", t)[:, c], scalar=col("bv", t, c), in1=Ek[:, c],
                            op0=ALU.add, op1=ALU.mult, accum_out=kvpart[:, c, t:t + 1]).then_inc(S["kvdone"], 1)
                if step in ("Ak", "Aq"):
                    what, E, src, rnd = {"Ak": ("k", Ek, "ek", "ekr"), "Aq": ("q", Eq, "eq", "eqr")}[step]
                    ps, b1 = slot(what, t), plus[b]["b" + what]
                    tile_event(dve, src, L, t)
                    dve.tensor_scalar(E[:, :, :], E[:, :, :], -1.0, 1.0, ALU.add, ALU.add).then_inc(S[rnd], 1)
                    tile_event(dve, rnd, L, t)
                    for c in range(KC):
                        if what == "k":
                            if t % 2 == 0:
                                dve.wait_ge(S["sums"], L * 4 + (t - 2))
                            dve.scalar_tensor_tensor(
                                out=Ek[:, c], in0=ps[:, c], scalar=b1[:, c:c + 1], in1=E[:, c], op0=ALU.add,
                                op1=ALU.max, accum_out=kpart[:, c, t:t + 1]).then_inc(S["kdone"], 1)
                        else:
                            tile_event(dve, "vdone", L - 1, t, c)
                            dve.scalar_tensor_tensor(
                                out=Q[:, c, chunks(t)], in0=ps[:, c], scalar=b1[:, c:c + 1], in1=E[:, c],
                                op0=ALU.add, op1=ALU.max).then_inc(S["qdone"], 1)
                if step == "Va":
                    if t % 2 == 0:
                        tile_event(dve, "kvdone", L, t + 1)
                        tile_event(dve, "vdone", L - 1, t + 1)
                        dve.tensor_tensor(ksum[:, :, b:b + 1], kpart[:, :, t:t + 1], kpart[:, :, t + 1:t + 2],
                                          ALU.add).then_inc(S["sums"], 1)
                        dve.scalar_tensor_tensor(out=nkvsum[:, :, b], in0=kvpart[:, :, t], scalar=-1.0,
                                                 in1=kvpart[:, :, t + 1], op0=ALU.mult,
                                                 op1=ALU.subtract).then_inc(S["sums"], 1)
                        dve.wait_ge(S["sums"], L * 4 + (t + 2))
                    tile_event(dve, "qdone", L, t)
                    tile_event(dve, "vdone", L, t - 1)
                    for c in range(KC):
                        dve.tensor_scalar(den[:, c], Q[:, c, chunks(t)], ksum[:, c, b:b + 1], 1e-6,
                                          ALU.mult, ALU.add).then_inc(S["den"], 1)
                if step == "Vc":
                    tile_event(dve, "rec0", L, t)
                    dve.tensor_tensor(den[:, :, :], den[:, :, :], rec[:, :, :], ALU.mult).then_inc(S["dy"], 1)
                    tile_event(dve, "dy", L, t)
                    dve.scalar_tensor_tensor(out=den[:, :, :], in0=den[:, :, :], scalar=-2.0, in1=rec[:, :, :],
                                             op0=ALU.add, op1=ALU.mult).then_inc(S["rec"], 1)
                    tile_event(dve, "rec", L, t)
                    for c in range(KC):
                        dve.scalar_tensor_tensor(out=Q[:, c, chunks(t)], in0=Q[:, c, chunks(t)],
                                                 scalar=nkvsum[:, c, b:b + 1], in1=den[:, c], op0=ALU.mult,
                                                 op1=ALU.mult).then_inc(S["vdone"], 1)
                if step == "O":
                    tile_event(dve, "go2", L, t)
                    dve.tensor_tensor(R[1][:, t % 2], R[1][:, t % 2], XF[:, :, chunks(t)],
                                      ALU.add).then_inc(S["r1"], 1)
                if step == "T":
                    tile_event(dve, "gd", L, t)
                    dve.tensor_tensor(R[2][:, t % 2], R[2][:, t % 2], x1[:, t % 2],
                                      ALU.add).then_inc(S["r2"], 1)
                if step in ("M1", "M2"):
                    k = int(step[1])
                    tile_event(dve, f"mean_mm{k}", L, t)
                    r = R[k][:, t % 2]
                    dve.tensor_tensor(r, r, pMean[:, None, :].to_broadcast([P, KC, TW]),
                                      ALU.subtract).then_inc(S[f"xc{k}"], 1)
                if step in ("R1a", "R2"):
                    k = int(step[1])
                    tile_event(dve, f"guess{k}", L, t)
                    dve.scalar_tensor_tensor(out=Y2[:, :], in0=pVar[:, :], scalar=ATTN_LN_EPS, in1=Y2[:, :],
                                             op0=ALU.add, op1=ALU.mult).then_inc(S[f"newton{k}"], 1)
                    tile_event(dve, f"newton{k}", L, t)
                    dve.scalar_tensor_tensor(out=Y0[:, :], in0=Y2[:, :], scalar=-1.5, in1=Y0[:, :],
                                             op0=ALU.add, op1=ALU.mult).then_inc(S[f"rstd{k}"], 1)
                    tile_event(dve, f"rstd{k}", L, t)
                    tile_event(dve, f"sq{k}", L, t)
                    r = R[k][:, t % 2]
                    dve.tensor_tensor(r, r, Y0[:, None, :].to_broadcast([P, KC, TW]),
                                      ALU.mult).then_inc(S[f"y{k}"], 1)
                    tile_event(dve, f"y{k}", L, t)
                    if k == 1:
                        tile_event(dve, "r2", L, t - 2)
                        tile_event(dve, "x1l", L, t - 2)
                    else:
                        tile_event(dve, "xl", L, t)
                        norm_vectors_event(dve, L, b)
                    for c in range(KC):
                        to, done, shift = ((x1[:, t % 2, c], "x1", col("ln1_b", t, c)) if k == 1 else
                                           (XF[:, c, chunks(t)], "xnew", vn[b][:, KC + c:KC + c + 1]))
                        dve.tensor_scalar(to, r[:, c], minus[b][f"ln{k}_s"][:, c:c + 1], shift, ALU.mult,
                                          ALU.add).then_inc(S[done], 1)
                if step[0] == "U":
                    for f in (2 * int(step[1]), 2 * int(step[1]) + 1):
                        tile_event(dve, "h", L, t, f)
                        tile_event(dve, "d_mm", L, t, f // 2 - 2)
                        dve.tensor_copy(hh[:, f % 4], HF[:, f % 4]).then_inc(S["hh"], 1)
                        if f % 2 == 0:
                            tile_event(dve, "hh", L, t, f)
                            dve.tensor_tensor(hl[:, f % 4], HF[:, f % 4], hh[:, f % 4].bitcast(F32),
                                              ALU.subtract).then_inc(S["hl_dve"], 1)

            turns(dve, DVE_FIRST, DVE_ORDER, DVE_LAST, dve_step)

        @block.gpsimd
        def _(pool):
            start_counts(pool, "pool")

            def pool_step(step, t, n, L, LT, turn):
                if step == "X":
                    tile_event(pool, "xh", L, t)
                    pool.tensor_tensor(xl[:, t % 2], XF[:, :, chunks(t)], xh[:, t % 2].bitcast(F32),
                                       ALU.subtract).then_inc(S["xl"], 1)
                if step == "Vb":
                    tile_event(pool, "vh", L, t)
                    pool.tensor_tensor(vl[:, :, :], Q[:, :, chunks(t)], vh[:, :, :].bitcast(F32),
                                       ALU.subtract).then_inc(S["vl"], 1)
                if step in ("O", "T"):
                    k = 1 if step == "O" else 2
                    tile_event(pool, f"r{k}", L, t)
                    tile_event(pool, f"mean_mm{k}", L, t - 1)
                    pool.tensor_tensor(RS[k][:, :], R[k][:, t % 2, 0], R[k][:, t % 2, 1],
                                       ALU.add).then_inc(S[f"rs{k}"], 1)
                if step in ("M1", "M2"):
                    k = int(step[1])
                    tile_event(pool, f"sq{k}", L, t)
                    norm_before(pool, POOL_ORDER, M_STEPS, "var_mm", k, t, n, LT, turn)
                    pool.tensor_tensor(SS[:, :], SQ[:, 0], SQ[:, 1], ALU.add).then_inc(S[f"ss{k}"], 1)
                if step == "R1b":
                    tile_event(pool, "x1h", L, t)
                    pool.tensor_tensor(x1l[:, :, :], x1[:, t % 2], x1h[:, :, :].bitcast(F32),
                                       ALU.subtract).then_inc(S["x1l"], 1)
                if step[0] == "U":
                    f = 2 * int(step[1]) + 1
                    tile_event(pool, "hh", L, t, f)
                    pool.tensor_tensor(hl[:, f % 4], HF[:, f % 4], hh[:, f % 4].bitcast(F32),
                                       ALU.subtract).then_inc(S["hl_pool"], 1)

            turns(pool, POOL_FIRST, POOL_ORDER, POOL_LAST, pool_step)

        @block.tensor
        def _(pe):
            start_counts(pe, "pe")

            def project(what, w, t, n, L, LT, turn, h, l):
                slot_free(pe, what, t, 0, n, LT, turn)
                ps = slot(what, t)
                for m in range(KC):
                    cols = slice(m * P, (m + 1) * P)
                    for k in range(KC):
                        mm = three(pe, ps[:, m], WAh[:, w, k, cols], WAl[:, w, k, cols], h[:, k], l[:, k],
                                   k == 0, k == KC - 1)
                mm.then_inc(S[what + "_mm"], 1)

            def down(t, j, L):
                if t == 0 and j == 0:
                    weights_event(pe, "wl", L, 3)
                tile_event(pe, "hl_dve", L, t, j)
                tile_event(pe, "hl_pool", L, t, j)
                if j == 0:
                    tile_event(pe, "gd", L, t - 1)
                for m in range(KC):
                    for f in (2 * j, 2 * j + 1):
                        cols = slice(m * P, (m + 1) * P)
                        mm = three(pe, pD[:, m], W2h[:, f, cols], W2l[:, f, cols], hh[:, f % 4], hl[:, f % 4],
                                   f == 0, f == FC - 1)
                mm.then_inc(S["d_mm"], 1)

            def pe_step(step, t, n, L, LT, turn):
                if step in ("Ak", "Av", "Aq"):
                    if t == 0:
                        weights_event(pe, "wl", L, 0)
                    tile_event(pe, "xl", L, t)
                    project(step[1], "qkv".index(step[1]), t, n, L, LT, turn, xh[:, t % 2], xl[:, t % 2])
                if step == "O":
                    if t == 0:
                        weights_event(pe, "wl", L, 1)
                    tile_event(pe, "vl", L, t)
                    project("o", 3, t, n, L, LT, turn, vh, vl)
                if step in ("M1", "M2"):
                    k = int(step[1])
                    tile_event(pe, f"rs{k}", L, t)
                    norm_before(pe, PE_ORDER, M_STEPS, "xc", k, t, n, LT, turn)
                    pe.matmul(pMean[:, :], ones_inv[:, :], RS[k][:, :], start=True,
                              stop=True).then_inc(S[f"mean_mm{k}"], 1)
                if step in ("R1a", "R2"):
                    k = int(step[1])
                    tile_event(pe, f"ss{k}", L, t)
                    norm_before(pe, PE_ORDER, R_STEPS, "newton", k, t, n, LT, turn)
                    pe.matmul(pVar[:, :], ones_inv[:, :], SS[:, :], start=True,
                              stop=True).then_inc(S[f"var_mm{k}"], 1)
                if step[0] == "U":
                    j = int(step[1])
                    if t == 0 and j == 0:
                        weights_event(pe, "wl", L, 2)
                    tile_event(pe, "x1l", L, t)
                    slot_free(pe, "u", t, j, n, LT, turn)
                    for f in (2 * j, 2 * j + 1):
                        cols = slice(f * P, (f + 1) * P)
                        for k in range(KC):
                            mm = three(pe, slot("u", t, j)[:, f % 2], W1h[:, k, cols], W1l[:, k, cols],
                                       x1h[:, k], x1l[:, k], k == 0, k == KC - 1)
                    mm.then_inc(S["u_mm"], 1)
                if step[0] == "D":
                    down(t, int(step[1]), L)

            turns(pe, PE_FIRST, PE_ORDER, PE_LAST, pe_step)


HEADS, HD, KEYS = 16, 16, 77
HC = P // HD
HB = HC // 2
SUB = TW // P
UNITS = SUB * KC
BT = SEQ // TW


CROSS_PLACES = {
    "pe": {"M0": -1, "R0": 12, "Q0": 19, "Q1": 26, "O0": 8, "O1": 10, "M1": 20, "R1": 34},
    "act": {"M0": 11, "R0": 16, "Q0": 20, "Q1": 28, "M1": 27, "R1": 36},
    "dve": {"L": -8, "M0": -1, "R0": 15, "O0": 7, "O1": 9, "M1": 23, "R1": 35},
    "pool": {"A0": -9, "M0": 0, "A1": 4, "M1": 14},
}


def cross_order(engine):
    ahead = 1 if engine == "act" else 2
    first = "LAMKRQ" if engine == "dve" else "LAMRQK"
    at = [(j - 3, 1, "S", 0, j) for j in range(ahead)]
    for i in range(TILES * UNITS + UNITS):
        for quarter, (step, j) in enumerate((("C", i - 2), ("T", i), ("P", i - 1), ("S", i + ahead))):
            if 0 <= j < TILES * UNITS and (step != "S" or j >= ahead):
                at.append((4 * i + quarter, 1, step, j // UNITS, j % UNITS))
    for name, place in CROSS_PLACES[engine].items():
        step, n = name[0], int(name[1:] or 0)
        for t in range(TILES):
            period = t + 1 if n == 1 and step != "Q" or step == "O" else t - 1
            if period < 0:
                at.append((-99, first.index(step), step, t, n))
            else:
                at.append((4 * UNITS * period + place, 0, step, t, n))
    at.append((-99, first.index("K"), "K", 0, 0))
    return [x[2:] for x in sorted(at, key=lambda x: x[:2])]


def cross_stage(nc, sem, XF, ones_inv, consts, ident, headmask, x_t, ctx_t, cvecs, cw):
    PE2, ACT2, DVE2, POOL2 = (cross_order(engine) for engine in ("pe", "act", "dve", "pool"))
    NORMS2 = [(n, t) for s, t, n in PE2 if s == "M"]
    for order, steps in ((PE2, "R"), (ACT2, "M"), (ACT2, "R"), (DVE2, "M"), (DVE2, "R"), (POOL2, "A"), (POOL2, "M")):
        assert NORMS2 == [(n, t) for s, t, n in order if s in steps]
    with ExitStack() as ctx:
        def sb(name, shape, dt=F32):
            return ctx.enter_context(nc.sbuf_tensor(name, shape, dt))

        W = sb("c_W", [P, 4, KC, D])
        cvec = sb("c_vec", [P, 4, KC])
        cT = sb("c_T", [P, KC, BATCH * KEYS])
        kT = sb("c_kT", [P, KC, BATCH * KEYS])
        KB = sb("c_KB", [P, BATCH * KC, HC, KEYS])
        V17 = sb("c_V17", [KEYS, BATCH, HEADS, HD + 1])
        B = sb("c_B", [P, TILES, KC, TW])
        RS, SS = sb("c_RS", [P, TW]), sb("c_SS", [P, TW])
        SQ = sb("c_SQ", [P, KC, TW])
        Y0, Y2 = sb("c_Y0", [P, TW]), sb("c_Y2", [P, TW])
        q2 = sb("c_q2", [P, 2, KC, TW])
        Pb = sb("c_Pb", [P, 2, HC, KEYS])
        PT = sb("c_PT", [KEYS, 2, HC, P])
        mx = sb("c_mx", [P, 2, HC])
        rec = sb("c_rec", [P, 2, HC])
        Cx = sb("c_Cx", [P, 2, HC, HD])
        cxT = sb("c_cxT", [P, 2, KC, TW])

        psS = [ctx.enter_context(nc.psum_tensor(f"c_psS{i}", [P, 2, 512], F32)) for i in range(2)]
        psT = ctx.enter_context(nc.psum_tensor("c_psT", [P, 2, HB, P], F32))
        psO = ctx.enter_context(nc.psum_tensor("c_psO", [P, 512], F32))
        psX = ctx.enter_context(nc.psum_tensor("c_psX", [P, TW], F32))

        per_tile = {"r0": 1, "r1": 2, "q_mm": 2, "q": 2, "s_mm": UNITS, "mx": UNITS, "sub": UNITS,
                    "exp": UNITS, "t_mm": 2 * UNITS, "ta": UNITS, "tv": UNITS, "pv": UNITS, "rec": UNITS,
                    "cx": UNITS, "c_mm": UNITS, "cxT": UNITS, "o_mm": 2}
        per_norm = ("rs", "mean_mm", "xc", "sq", "ss", "var_mm", "guess", "newton", "rstd", "norm")
        S = {n: sem("c_" + n) for n in (*per_tile, *per_norm)}
        s_xo = [sem(f"c_xo{t}") for t in range(TILES)]
        s_load, s_pre, s_kmm, s_kev, s_kb, s_vmm, s_vev = (sem("c_" + n) for n in
                                                           ("load", "pre", "kmm", "kev", "kb", "vmm", "vev"))
        def wait(eng, s, value):
            if value > 0:
                eng.wait_ge(s, value)

        def tile_event(eng, name, t, n=None):
            e = per_tile[name]
            wait(eng, S[name], e * t + (e if n is None else n + 1))

        def guess_event(eng, i, n):
            wait(eng, S["guess"], 3 * i + n)

        def norm_event(eng, name, i):
            wait(eng, S[name], i + 1)

        USES = []
        for step, t, n in PE2:
            i = NORMS2.index((n, t)) if step in ("M", "R") else 0
            USES += {"M": [("mean", i, 0, ("xc", i))], "R": [("var", i, 0, ("newton", i))],
                     "Q": [("q", t, n, ("q", t, n))], "O": [("o", t, n, ("r1", t, n))]}.get(step, [])

        def bank_free(pe, what, a, b):
            i = [u[:3] for u in USES].index((what, a, b))
            if i:
                name, *at = USES[i - 1][3]
                (norm_event if len(at) == 1 else tile_event)(pe, name, *at)

        def x_tile(t):
            return XF[:, :, t * TW:(t + 1) * TW]

        CB = HC * (HD + 1)

        block = ctx.enter_context(nc.Block())

        @block.sync
        def _(sp):
            x_0 = x_t.rearrange("(k p) n -> p k n", p=P)
            sp.dma_start(B[:, 0], x_0[:, :, 0:TW]).then_inc(s_xo[0], 16)
            sp.dma_start(cT[:, :, :], ctx_t.rearrange("(k p) n -> p k n", p=P)).then_inc(s_load, 16)
            sp.dma_start(W[:, :, :, :].rearrange("p w k n -> p (w k n)"), cw).then_inc(s_load, 16)
            sp.dma_start(cvec[:, :, :].rearrange("p v c -> p (v c)"), cvecs).then_inc(s_load, 16)
            for t in range(1, TILES):
                sp.dma_start(B[:, t], x_0[:, :, t * TW:(t + 1) * TW]).then_inc(s_xo[t], 16)

        @block.scalar
        def _(act):
            act.wait_ge(s_load, 48)
            act.preload_act_table_set(LOG_EXP)
            for m in range(KC):
                act.wait_ge(s_kmm, m + 1)
                act.activation(kT[:, m, :], psS[0][:, m, 0:BATCH * KEYS], ACT.Identity,
                               bias=cvec[:, 1, m:m + 1]).then_inc(s_kev, 1)
            for step, t, n in ACT2:
                if step == "M":
                    i = NORMS2.index((n, t))
                    norm_event(act, "xc", i)
                    norm_event(act, "ss", i - 1)
                    act.activation(SQ[:, :, :], B[:, t], ACT.Square).then_inc(S["sq"], 1)
                if step == "R":
                    i = NORMS2.index((n, t))
                    norm_event(act, "var_mm", i)
                    norm_event(act, "norm", i - 1)
                    act.activation(Y0[:, :], psX[:, :], ACT.Ln, bias=consts[:, 1:2]).then_inc(S["guess"], 1)
                    guess_event(act, i, 1)
                    act.activation(Y0[:, :], Y0[:, :], ACT.Exp, scale=-0.5).then_inc(S["guess"], 1)
                    guess_event(act, i, 2)
                    act.activation(Y2[:, :], Y0[:, :], ACT.Square, scale=0.5 ** 0.5).then_inc(S["guess"], 1)
                if step == "Q":
                    tile_event(act, "q_mm", t, n)
                    tile_event(act, "s_mm", t - 2)
                    act.activation(q2[:, t % 2, n], psX[:, :], ACT.Identity,
                                   bias=cvec[:, 0, n:n + 1]).then_inc(S["q"], 1)
                if step == "S":
                    tile_event(act, "sub", t, n)
                    act.activation(Pb[:, n % 2], Pb[:, n % 2], ACT.Exp, scale=HD ** -0.5).then_inc(S["exp"], 1)
                if step == "T":
                    tile_event(act, "t_mm", t, 2 * n)
                    tile_event(act, "pv", t, n - 2)
                    act.activation(PT[:, n % 2, 0:HB], psT[0:KEYS, 0], ACT.Copy).then_inc(S["ta"], 1)
                if step == "C":
                    s, c = n // KC, n % KC
                    tile_event(act, "c_mm", t, n)
                    tile_event(act, "o_mm", t - 2)
                    act.activation(cxT[:, t % 2, c, s * P:(s + 1) * P], psO[:, CB:CB + P], ACT.Identity,
                                   bias=cvec[:, 2, c:c + 1]).then_inc(S["cxT"], 1)

        @block.vector
        def _(dve):
            dve.memset(V17[:, :, :, :], 1.0).then_inc(s_pre, 1)
            for step, t, n in DVE2:
                if step == "K":
                    dve.wait_ge(s_kev, KC)
                    for b in range(BATCH):
                        for c in range(KC):
                            dve.tensor_tensor(KB[:, b * KC + c],
                                              kT[:, c, None, b * KEYS:(b + 1) * KEYS].to_broadcast([P, HC, KEYS]),
                                              headmask[:, :, None].to_broadcast([P, HC, KEYS]),
                                              ALU.mult).then_inc(s_kb, 1)
                    dve.wait_ge(s_pre, 1)
                    dve.wait_ge(s_vmm, 1)
                    for b in range(BATCH):
                        dve.tensor_copy(V17[:, b, :, 0:HD], psO[0:KEYS, b * D:(b + 1) * D]
                                        .rearrange("p (h d) -> p h d", d=HD)).then_inc(s_vev, 1)
                if step == "L":
                    dve.wait_ge(s_xo[t], 16)
                    dve.tensor_tensor(B[:, t], x_tile(t), B[:, t], ALU.add).then_inc(S["r0"], 1)
                if step == "M":
                    i = NORMS2.index((n, t))
                    norm_event(dve, "mean_mm", i)
                    norm_event(dve, "rs", i)
                    dve.tensor_tensor(B[:, t], psX[:, None, :].to_broadcast([P, KC, TW]), B[:, t],
                                      ALU.subtract).then_inc(S["xc"], 1)
                if step == "R":
                    i = NORMS2.index((n, t))
                    guess_event(dve, i, 3)
                    dve.scalar_tensor_tensor(out=Y2[:, :], in0=psX[:, :], scalar=LN_EPS, in1=Y2[:, :],
                                             op0=ALU.add, op1=ALU.mult).then_inc(S["newton"], 1)
                    norm_event(dve, "newton", i)
                    dve.scalar_tensor_tensor(out=Y0[:, :], in0=Y2[:, :], scalar=-1.5, in1=Y0[:, :],
                                             op0=ALU.add, op1=ALU.mult).then_inc(S["rstd"], 1)
                    norm_event(dve, "rstd", i)
                    norm_event(dve, "sq", i)
                    out = B[:, t] if n == 0 else x_tile(t)
                    dve.tensor_tensor(out, B[:, t], Y0[:, None, :].to_broadcast([P, KC, TW]),
                                      ALU.mult).then_inc(S["norm"], 1)
                if step == "S":
                    tile_event(dve, "s_mm", t, n)
                    ps = psS[n % 2][:, :, 0:HB * KEYS].rearrange("p g (h k) -> p g h k", k=KEYS)
                    m = mx[:, n % 2].rearrange("p (g h) -> p g h", g=2)
                    dve.tensor_reduce(m, ps, AX.X, ALU.max).then_inc(S["mx"], 1)
                    tile_event(dve, "mx", t, n)
                    tile_event(dve, "t_mm", t, 2 * (n - 2) + 1)
                    dve.tensor_tensor(Pb[:, n % 2].rearrange("p (g h) k -> p g h k", g=2), ps,
                                      m[:, :, :, None].to_broadcast([P, 2, HB, KEYS]),
                                      ALU.subtract).then_inc(S["sub"], 1)
                if step == "T":
                    tile_event(dve, "t_mm", t, 2 * n + 1)
                    tile_event(dve, "pv", t, n - 2)
                    dve.tensor_copy(PT[:, n % 2, HB:HC], psT[0:KEYS, 1]).then_inc(S["tv"], 1)
                if step == "P":
                    o = psO[:, 0:HC * (HD + 1)].rearrange("p (h d) -> p h d", d=HD + 1)
                    tile_event(dve, "pv", t, n)
                    tile_event(dve, "cx", t, n - 2)
                    dve.reciprocal(rec[:, n % 2], o[:, :, HD]).then_inc(S["rec"], 1)
                    tile_event(dve, "rec", t, n)
                    tile_event(dve, "c_mm", t, n - 2)
                    dve.tensor_tensor(Cx[:, n % 2], o[:, :, 0:HD],
                                      rec[:, n % 2, :, None].to_broadcast([P, HC, HD]),
                                      ALU.mult).then_inc(S["cx"], 1)
                if step == "O":
                    tile_event(dve, "o_mm", t, n)
                    dve.scalar_tensor_tensor(out=B[:, t, n], in0=psX[:, :], scalar=cvec[:, 3, n:n + 1],
                                             in1=B[:, t, n], op0=ALU.add, op1=ALU.add).then_inc(S["r1"], 1)

        @block.gpsimd
        def _(pool):
            for step, t, n in POOL2:
                if step == "A":
                    i = NORMS2.index((n, t))
                    tile_event(pool, f"r{n}", t)
                    norm_event(pool, "mean_mm", i - 1)
                    pool.tensor_tensor(RS[:, :], B[:, t, 0], B[:, t, 1], ALU.add).then_inc(S["rs"], 1)
                if step == "M":
                    i = NORMS2.index((n, t))
                    norm_event(pool, "sq", i)
                    norm_event(pool, "var_mm", i - 1)
                    pool.tensor_tensor(SS[:, :], SQ[:, 0], SQ[:, 1], ALU.add).then_inc(S["ss"], 1)

        @block.tensor
        def _(pe):
            pe.wait_ge(s_load, 48)
            for m in range(KC):
                for k in range(KC):
                    mm = pe.matmul(psS[0][:, m, 0:BATCH * KEYS], W[:, 1, k, m * P:(m + 1) * P], cT[:, k, :],
                                   start=(k == 0), stop=(k == KC - 1))
                mm.then_inc(s_kmm, 1)
            for b in range(BATCH):
                for k in range(KC):
                    mm = pe.matmul(psO[0:KEYS, b * D:(b + 1) * D], cT[:, k, b * KEYS:(b + 1) * KEYS], W[:, 2, k, :],
                                   start=(k == 0), stop=(k == KC - 1))
            mm.then_inc(s_vmm, 1)
            for step, t, n in PE2:
                s, c = n // KC, n % KC
                if step == "K":
                    pe.wait_ge(s_kb, BATCH * KC)
                    pe.wait_ge(s_kev, KC)
                    pe.wait_ge(s_vev, BATCH)
                if step == "M":
                    i = NORMS2.index((n, t))
                    norm_event(pe, "rs", i)
                    bank_free(pe, "mean", i, 0)
                    pe.matmul(psX[:, :], ones_inv[:, :], RS[:, :], start=True, stop=True).then_inc(S["mean_mm"], 1)
                if step == "R":
                    i = NORMS2.index((n, t))
                    norm_event(pe, "ss", i)
                    bank_free(pe, "var", i, 0)
                    pe.matmul(psX[:, :], ones_inv[:, :], SS[:, :], start=True, stop=True).then_inc(S["var_mm"], 1)
                if step in ("Q", "O"):
                    w, src, done = (0, B[:, t], "q_mm") if step == "Q" else (3, cxT[:, t % 2], "o_mm")
                    if step == "Q":
                        norm_event(pe, "norm", NORMS2.index((0, t)))
                    else:
                        tile_event(pe, "cxT", t)
                    bank_free(pe, step.lower(), t, n)
                    for k in range(KC):
                        mm = pe.matmul(psX[:, :], W[:, w, k, n * P:(n + 1) * P], src[:, k],
                                       start=(k == 0), stop=(k == KC - 1))
                    mm.then_inc(S[done], 1)
                if step == "S":
                    tile_event(pe, "q", t)
                    tile_event(pe, "sub", t, n - 2)
                    for g in range(2):
                        mm = pe.matmul(psS[n % 2][:, g, 0:HB * KEYS], q2[:, t % 2, c, s * P:(s + 1) * P],
                                       KB[:, t // BT * KC + c, g * HB:(g + 1) * HB, :]
                                       .rearrange("p h k -> p (h k)"), start=True, stop=True)
                    mm.then_inc(S["s_mm"], 1)
                if step == "T":
                    tile_event(pe, "exp", t, n)
                    for g in range(2):
                        tile_event(pe, ("ta", "tv")[g], t, n - 1)
                        for h in range(HB):
                            mm = pe.transpose(psT[0:KEYS, g, h], Pb[:, n % 2, g * HB + h], ident[:, :])
                        mm.then_inc(S["t_mm"], 1)
                if step == "P":
                    tile_event(pe, "ta", t, n)
                    tile_event(pe, "tv", t, n)
                    tile_event(pe, "cx", t, n - 1)
                    tile_event(pe, "cxT", t, n - 1)
                    for h in range(HC):
                        mm = pe.matmul(psO[:, h * (HD + 1):(h + 1) * (HD + 1)], PT[:, n % 2, h],
                                       V17[:, t // BT, c * HC + h, :],
                                       start=True, stop=True)
                    mm.then_inc(S["pv"], 1)
                if step == "C":
                    tile_event(pe, "cx", t, n)
                    pe.transpose(psO[:, CB:CB + P], Cx[:, n % 2].rearrange("p h d -> p (h d)"),
                                 ident[:, :]).then_inc(S["c_mm"], 1)


CAP = SEQ // 8
assert CAP == P
ST = SEQ // P
DFF = D * 4 * 2 // 3
DC = -(-DFF // P)
CR = BATCH * CAP
NEG = -1e30


def steps_in(text):
    return [(w[:-1], int(w[-1])) for w in text.split()]


ATTN_PE = steps_in("scores0 scores1 turn0 scores2 out0 turn1 scores3 out1 back0 turn2 out2 back1 turn3 out3 "
                   "back2 back3")
ATTN_DVE = steps_in("max0 max1 turn0 max2 out0 turn1 max3 out1 turn2 out2 turn3 out3")
ATTN_ACT = steps_in("exp0 exp1 turn0 exp2 turn1 exp3 back0 turn2 back1 turn3 back2 back3")
FINAL_PE = steps_in("scatter0 scatter1 mean0 scatter2 mean1 var0 scatter3 mean2 var1 mean3 var2 var3")
FINAL_DVE = steps_in("add0 add1 centre0 add2 centre1 out0 add3 centre2 out1 centre3 out2 out3")
FINAL_ACT = steps_in("square0 square1 guess0 square2 guess1 square3 guess2 guess3")
FINAL_POOL = steps_in("sum0 sum1 squares0 sum2 squares1 sum3 squares2 squares3")


def routed_stage(nc, sem, XF, ones_inv, consts, ident, headmask, x_out, fvecs, f_qkv, f_out, f_w12, f_w3):
    with ExitStack() as ctx:
        def sb(name, shape, dt=F32):
            return ctx.enter_context(nc.sbuf_tensor("f_" + name, shape, dt))

        fvec = sb("vec", [P, 3, KC])
        ng = sb("ng", [P, 2, KC])
        Wqkv = sb("Wqkv", [P, KC, 3 * D])
        Wout = sb("Wout", [P, KC, D])
        W12 = sb("W12", [P, 2, KC, DFF])
        W3 = sb("W3", [P, DC, D])
        wr = sb("wr", [P, KC, P])
        causal = sb("causal", [P, P])
        after = sb("after", [P, P])
        lane = sb("lane", [P, 1])
        ones = sb("ones", [P, P], BF16)
        Srow = sb("Srow", [P, BATCH, SEQ])
        tmp, tmp2 = sb("tmp", [P, SEQ]), sb("tmp2", [P, SEQ])
        scol = sb("scol", [P, BATCH, ST])
        ahead = sb("ahead", [P, ST, SEQ], BF16)
        tie = sb("tie", [P, ST, P], BF16)
        OH = sb("OH", [P, BATCH, ST, P])
        OHT = sb("OHT", [P, BATCH, SEQ])
        xN = sb("xN", [P, BATCH * ST, D])
        xs = sb("xs", [P, KC, CR])
        sq = sb("sq", [P, KC, CR])
        y0, y2 = sb("y0", [P, CR]), sb("y2", [P, CR])
        hT = sb("hT", [P, KC, CR])
        qT = sb("qT", [P, KC, CR])
        KB = sb("KB", [P, BATCH, KC, HC, P])
        V17 = sb("V17", [P, BATCH, HEADS, HD + 1])
        Pb = sb("Pb", [P, 2, HC, P])
        PT = sb("PT", [P, 2, HC, P])
        mx, rec = sb("mx", [P, 4, HC]), sb("rec", [P, 4, HC])
        Cx = sb("Cx", [P, 4, HC, HD])
        oT = sb("oT", [P, KC, CR])
        x1 = sb("x1", [P, KC, CR])
        sg = sb("sg", [P, DC, CR])
        dN = sb("dN", [P, BATCH, D])
        R = sb("R", [P, TILES, KC, TW])
        RS, SS = sb("RS", [P, TW]), sb("SS", [P, 2, TW])
        Z0, Z2 = sb("Z0", [P, TW]), sb("Z2", [P, TW])

        psS = [ctx.enter_context(nc.psum_tensor(f"f_psS{i}", [P, 2, 512], F32)) for i in range(2)]
        psT = ctx.enter_context(nc.psum_tensor("f_psT", [P, 2, 512], F32))
        psO = ctx.enter_context(nc.psum_tensor("f_psO", [P, 512], F32))
        psX = ctx.enter_context(nc.psum_tensor("f_psX", [P, 512], F32))

        names = ("vec w c_pool c_ng c_wr c_one s_mm srow turn_mm scol cmp rank_mm oh xt_mm xn g_mm xs oh_mm oht "
                 "sq m_mm guess nw rs h qkv_mm q kb v sc_mm msk mx sub exp t_mm ta tv pv rec cx c_mm ot a_mm x1 "
                 "f1_mm f2_mm sil g d_mm d sct r rsum mean xc sqr ss var guess2 znw zrs out st").split()
        S = {n: sem("f_" + n) for n in names}

        NU = BATCH * KC
        def squares(t):
            return tmp if t % 2 == 0 else tmp2

        block = ctx.enter_context(nc.Block())

        @block.sync
        def _(sp):
            sp.dma_start(fvec[:, :, :].rearrange("p v c -> p (v c)"), fvecs).then_inc(S["vec"], 16)
            sp.dma_start(Wqkv[:, :, :].rearrange("p k n -> p (k n)"), f_qkv).then_inc(S["w"], 16)
            sp.dma_start(Wout[:, :, :].rearrange("p k n -> p (k n)"), f_out).then_inc(S["w"], 16)
            sp.dma_start(W12[:, :, :, :].rearrange("p w k n -> p (w k n)"), f_w12).then_inc(S["w"], 16)
            sp.dma_start(W3[:, 0:DC - 1, :], f_w3[0:(DC - 1) * P, :].rearrange("(k p) n -> p k n", p=P)) \
                .then_inc(S["w"], 16)
            sp.dma_start(W3[0:DFF - (DC - 1) * P, DC - 1, :], f_w3[(DC - 1) * P:DFF, :]).then_inc(S["w"], 16)
            for t in range(TILES):
                sp.wait_ge(S["out"], t + 1)
                sp.dma_start(x_out.rearrange("(k p) n -> p k n", p=P)[:, :, t * TW:(t + 1) * TW],
                             R[:, t]).then_inc(S["st"], 16)
            sp.wait_ge(S["st"], 16 * TILES)

        @block.gpsimd
        def _(pool):
            pool.memset(causal[:, :], 0.0).then_inc(S["c_pool"], 1)
            pool.memset(after[:, :], 1.0).then_inc(S["c_pool"], 1)
            pool.iota(lane[:, :], pattern=[[1, 1]], base=0, channel_multiplier=1,
                      allow_small_or_imprecise_dtypes=True).then_inc(S["c_pool"], 1)
            pool.memset(V17[:, :, :, :], 1.0).then_inc(S["c_pool"], 1)
            pool.wait_ge(S["c_pool"], 4)
            pool.affine_select(out=causal[:, :], in_=causal[:, :], compare_op=ALU.is_ge, fill=NEG, base=0,
                               pattern=[[-1, P]], channel_multiplier=1).then_inc(S["c_pool"], 1)
            pool.affine_select(out=after[:, :], in_=after[:, :], compare_op=ALU.is_ge, fill=0.0, base=-1,
                               pattern=[[1, P]], channel_multiplier=-1).then_inc(S["c_pool"], 1)
            for step, t in FINAL_POOL:
                if step == "sum":
                    pool.wait_ge(S["r"], 2 * t + 2)
                    if t:
                        pool.wait_ge(S["mean"], t)
                    pool.tensor_tensor(RS[:, :], R[:, t, 0], R[:, t, 1], ALU.add).then_inc(S["rsum"], 1)
                if step == "squares":
                    pool.wait_ge(S["sqr"], t + 1)
                    if t >= 2:
                        pool.wait_ge(S["var"], t - 1)
                    pool.tensor_tensor(SS[:, t % 2], squares(t)[:, 0:TW], squares(t)[:, TW:2 * TW],
                                       ALU.add).then_inc(S["ss"], 1)

        @block.scalar
        def _(act):
            act.preload_act_table_set(LOG_EXP)
            for b in range(BATCH):
                act.wait_ge(S["s_mm"], b + 1)
                act.activation(Srow[:, b].rearrange("p (g n) -> p g n", g=2), psS[b][:, :, :],
                               ACT.Copy).then_inc(S["srow"], 1)
                for i in range(b * ST // 2, (b + 1) * ST // 2):
                    act.wait_ge(S["xt_mm"], i + 1)
                    act.activation(xN[:, 2 * i:2 * i + 2, :].rearrange("p t n -> p (t n)"), psT[:, i % 2],
                                   ACT.Copy).then_inc(S["xn"], 1)
            for b in range(BATCH):
                act.wait_ge(S["oh_mm"], b + 1)
                act.activation(OH[:, b].rearrange("p t n -> p (t n)").rearrange("p (g n) -> p g n", g=2),
                               psT[:, :, :], ACT.Copy).then_inc(S["oh"], 1)
            act.wait_ge(S["g_mm"], NU)
            act.activation(xs[:, :, :].rearrange("p c n -> p (c n)"), psO[:, :], ACT.Copy).then_inc(S["xs"], 1)
            for norm in range(2):
                src, ready, k = ((xs, "xs", 1), (x1, "x1", KC))[norm]
                act.wait_ge(S[ready], k)
                if norm:
                    act.wait_ge(S["m_mm"], norm)
                act.activation(sq[:, :, :], src[:, :, :], ACT.Square).then_inc(S["sq"], 1)
                act.wait_ge(S["m_mm"], norm + 1)
                ps = (psX, psO)[norm][:, 0:CR]
                if norm:
                    act.wait_ge(S["h"], KC * norm)
                act.activation(y0[:, :], ps, ACT.Ln, bias=consts[:, 0:1]).then_inc(S["guess"], 1)
                act.wait_ge(S["guess"], 3 * norm + 1)
                act.activation(y0[:, :], y0[:, :], ACT.Exp, scale=-0.5).then_inc(S["guess"], 1)
                act.wait_ge(S["guess"], 3 * norm + 2)
                act.activation(y2[:, :], y0[:, :], ACT.Square, scale=0.5 ** 0.5).then_inc(S["guess"], 1)
                if norm:
                    break
                act.wait_ge(S["qkv_mm"], 1)
                act.activation(qT[:, :, :].rearrange("p c n -> p (c n)"), psT[:, 0], ACT.Copy).then_inc(S["q"], 1)
                for step, i in ATTN_ACT:
                    if step == "exp":
                        act.wait_ge(S["sub"], i + 1)
                        act.activation(Pb[:, i % 2], Pb[:, i % 2], ACT.Exp, scale=HD ** -0.5).then_inc(S["exp"], 1)
                    if step == "turn":
                        act.wait_ge(S["t_mm"], 2 * i + 1)
                        if i >= 2:
                            act.wait_ge(S["pv"], i - 1)
                        act.activation(PT[:, i % 2, 0:HB].rearrange("p h n -> p (h n)"), psT[:, 0],
                                       ACT.Copy).then_inc(S["ta"], 1)
                    if step == "back":
                        b, c = i // KC, i % KC
                        act.wait_ge(S["c_mm"], i + 1)
                        act.activation(oT[:, c, b * P:(b + 1) * P], psX[:, 0:P], ACT.Copy).then_inc(S["ot"], 1)
            act.preload_act_table_set(SILU)
            for k in range(DC):
                w = min(P, DFF - k * P)
                act.wait_ge(S["f1_mm"], k // 2 * 2 + 2)
                act.activation(sg[0:w, k], (psS[0][0:w, k // 2, (k % 2) * CR:(k % 2 + 1) * CR] if k < 4 else
                                            psT[0:w, 0, (k % 2) * CR:(k % 2 + 1) * CR]),
                               ACT.Silu).then_inc(S["sil"], 1)
            act.preload_act_table_set(LOG_EXP)
            act.wait_ge(S["d_mm"], 1)
            act.activation(dN[:, :, :].rearrange("p b n -> p (b n)"), psO[:, :], ACT.Copy).then_inc(S["d"], 1)
            for step, t in FINAL_ACT:
                if step == "square":
                    act.wait_ge(S["xc"], t + 1)
                    if t >= 2:
                        act.wait_ge(S["ss"], t - 1)
                    act.activation(squares(t)[:, :].rearrange("p (c n) -> p c n", c=KC), R[:, t],
                                   ACT.Square).then_inc(S["sqr"], 1)
                if step == "guess":
                    act.wait_ge(S["var"], t + 1)
                    if t:
                        act.wait_ge(S["out"], t)
                    act.activation(Z0[:, :], psX[:, :], ACT.Ln, bias=consts[:, 1:2]).then_inc(S["guess2"], 1)
                    act.wait_ge(S["guess2"], 3 * t + 1)
                    act.activation(Z0[:, :], Z0[:, :], ACT.Exp, scale=-0.5).then_inc(S["guess2"], 1)
                    act.wait_ge(S["guess2"], 3 * t + 2)
                    act.activation(Z2[:, :], Z0[:, :], ACT.Square, scale=0.5 ** 0.5).then_inc(S["guess2"], 1)

        @block.vector
        def _(dve):
            dve.wait_ge(S["vec"], 16)
            dve.tensor_copy(wr[:, :, :], fvec[:, 0, :, None].to_broadcast([P, KC, P])).then_inc(S["c_wr"], 1)
            dve.tensor_scalar(ng[:, :, :], fvec[:, 1:3, :], -1.0, None, ALU.mult).then_inc(S["c_ng"], 1)
            dve.memset(ones[:, :], 1.0).then_inc(S["c_one"], 1)
            dve.wait_ge(S["c_pool"], 6)

            def score_columns(b):
                dve.wait_ge(S["turn_mm"], b + 1)
                dve.tensor_copy(scol[:, b], psX[:, b * ST:(b + 1) * ST]).then_inc(S["scol"], 1)
                dve.wait_ge(S["scol"], b + 1)

            def compare(b, t):
                s = scol[:, b, t:t + 1]
                if b:
                    dve.wait_ge(S["rank_mm"], t + 1)
                for lo, hi, op in ((0, (t + 1) * P, ALU.is_lt), ((t + 1) * P, SEQ, ALU.is_le)):
                    if lo < hi:
                        dve.tensor_scalar(ahead[:, t, lo:hi], Srow[:, b, lo:hi], s, None, op).then_inc(S["cmp"], 1)
                dve.scalar_tensor_tensor(out=tie[:, t], in0=Srow[:, b, t * P:(t + 1) * P], scalar=s,
                                         in1=after[:, :], op0=ALU.is_equal, op1=ALU.mult).then_inc(S["cmp"], 1)

            def one_hot(b):
                dve.wait_ge(S["rank_mm"], (b + 1) * ST)
                dve.tensor_scalar(OHT[:, b].rearrange("p (g n) -> p g n", g=2), psS[b][:, :, :], lane[:, 0:1], None,
                                  ALU.is_equal).then_inc(S["oht"], 1)

            score_columns(0)
            for t in range(ST):
                compare(0, t)
            score_columns(1)
            for t in range(ST):
                if t == ST // 2:
                    one_hot(0)
                compare(1, t)
            one_hot(1)

            def rms(norm, src):
                ps = (psX, psO)[norm][:, 0:CR]
                dve.wait_ge(S["guess"], 3 * norm + 3)
                dve.scalar_tensor_tensor(out=y2[:, :], in0=ps, scalar=ATTN_LN_EPS, in1=y2[:, :], op0=ALU.add,
                                         op1=ALU.mult).then_inc(S["nw"], 1)
                dve.wait_ge(S["nw"], norm + 1)
                dve.scalar_tensor_tensor(out=y0[:, :], in0=y2[:, :], scalar=-1.5, in1=y0[:, :], op0=ALU.add,
                                         op1=ALU.mult).then_inc(S["rs"], 1)
                dve.wait_ge(S["rs"], norm + 1)
                dve.wait_ge(S["c_ng"], 1)
                if norm:
                    dve.wait_ge(S["qkv_mm"], 4)
                for c in range(KC):
                    dve.scalar_tensor_tensor(out=hT[:, c], in0=src[:, c], scalar=ng[:, norm, c:c + 1], in1=y0[:, :],
                                             op0=ALU.mult, op1=ALU.mult).then_inc(S["h"], 1)

            rms(0, xs)
            dve.wait_ge(S["qkv_mm"], 2)
            for b in range(BATCH):
                for c in range(KC):
                    dve.tensor_tensor(KB[:, b, c],
                                      psT[:, 1, None, c * CR + b * P:c * CR + (b + 1) * P].to_broadcast([P, HC, P]),
                                      headmask[:, :, None].to_broadcast([P, HC, P]), ALU.mult).then_inc(S["kb"], 1)
            dve.wait_ge(S["qkv_mm"], 4)
            for b in range(BATCH):
                dve.tensor_copy(V17[:, b, :, 0:HD], psO[:, b * D:(b + 1) * D].rearrange("p (h d) -> p h d", d=HD)) \
                    .then_inc(S["v"], 1)
            for step, i in ATTN_DVE:
                if step == "max":
                    dve.wait_ge(S["sc_mm"], i + 1)
                    if i >= 2:
                        dve.wait_ge(S["t_mm"], 2 * (i - 1))
                    ps = psS[i % 2][:, :, :].rearrange("p g (h k) -> p (g h) k", k=P)
                    dve.tensor_tensor(Pb[:, i % 2], ps, causal[:, None, :].to_broadcast([P, HC, P]),
                                      ALU.add).then_inc(S["msk"], 1)
                    dve.wait_ge(S["msk"], i + 1)
                    dve.tensor_reduce(mx[:, i], Pb[:, i % 2], AX.X, ALU.max).then_inc(S["mx"], 1)
                    dve.wait_ge(S["mx"], i + 1)
                    dve.tensor_tensor(Pb[:, i % 2], Pb[:, i % 2], mx[:, i, :, None].to_broadcast([P, HC, P]),
                                      ALU.subtract).then_inc(S["sub"], 1)
                if step == "turn":
                    dve.wait_ge(S["t_mm"], 2 * i + 2)
                    if i >= 2:
                        dve.wait_ge(S["pv"], i - 1)
                    dve.tensor_copy(PT[:, i % 2, HB:HC].rearrange("p h n -> p (h n)"), psT[:, 1]) \
                        .then_inc(S["tv"], 1)
                if step == "out":
                    dve.wait_ge(S["pv"], i + 1)
                    o = psO[:, 0:HC * (HD + 1)].rearrange("p (h d) -> p h d", d=HD + 1)
                    dve.reciprocal(rec[:, i], o[:, :, HD]).then_inc(S["rec"], 1)
                    dve.wait_ge(S["rec"], i + 1)
                    dve.tensor_tensor(Cx[:, i], o[:, :, 0:HD], rec[:, i, :, None].to_broadcast([P, HC, HD]),
                                      ALU.mult).then_inc(S["cx"], 1)
            dve.wait_ge(S["a_mm"], 1)
            dve.tensor_tensor(x1[:, 0], psX[:, 0:CR], xs[:, 0], ALU.add).then_inc(S["x1"], 1)
            dve.tensor_tensor(x1[:, 1], psX[:, CR:2 * CR], xs[:, 1], ALU.add).then_inc(S["x1"], 1)
            rms(1, x1)
            for k in range(DC):
                w = min(P, DFF - k * P)
                dve.wait_ge(S["sil"], k + 1)
                dve.wait_ge(S["f2_mm"], k // 2 * 2 + 2)
                ps = (psS[1][0:w, k // 2, (k % 2) * CR:(k % 2 + 1) * CR] if k < 4 else
                      psX[0:w, (k % 2) * CR:(k % 2 + 1) * CR])
                dve.tensor_tensor(sg[0:w, k], sg[0:w, k], ps, ALU.mult).then_inc(S["g"], 1)
            for step, t in FINAL_DVE:
                if step == "add":
                    for c in range(KC):
                        dve.wait_ge(S["sct"], 2 * t + c + 1)
                        dve.scalar_tensor_tensor(out=R[:, t, c], in0=XF[:, c, t * TW:(t + 1) * TW], scalar=2.0,
                                                 in1=psS[t % 2][:, c], op0=ALU.mult, op1=ALU.add).then_inc(S["r"], 1)
                if step == "centre":
                    dve.wait_ge(S["mean"], t + 1)
                    dve.wait_ge(S["rsum"], t + 1)
                    dve.tensor_tensor(R[:, t], psT[:, 0, None, :].to_broadcast([P, KC, TW]), R[:, t],
                                      ALU.subtract).then_inc(S["xc"], 1)
                if step == "out":
                    dve.wait_ge(S["guess2"], 3 * t + 3)
                    dve.scalar_tensor_tensor(out=Z2[:, :], in0=psX[:, :], scalar=LN_EPS, in1=Z2[:, :], op0=ALU.add,
                                             op1=ALU.mult).then_inc(S["znw"], 1)
                    dve.wait_ge(S["znw"], t + 1)
                    dve.scalar_tensor_tensor(out=Z0[:, :], in0=Z2[:, :], scalar=-1.5, in1=Z0[:, :], op0=ALU.add,
                                             op1=ALU.mult).then_inc(S["zrs"], 1)
                    dve.wait_ge(S["zrs"], t + 1)
                    dve.tensor_tensor(R[:, t], R[:, t], Z0[:, None, :].to_broadcast([P, KC, TW]),
                                      ALU.mult).then_inc(S["out"], 1)

        @block.tensor
        def _(pe):
            pe.wait_ge(S["c_wr"], 1)

            def scores(b):
                for g in range(2):
                    cols = slice(b * SEQ + g * TW, b * SEQ + (g + 1) * TW)
                    for k in range(KC):
                        mm = pe.matmul(psS[b][:, g], wr[:, k], XF[:, k, cols], start=(k == 0), stop=(k == KC - 1))
                mm.then_inc(S["s_mm"], 1)

            def turn_scores(b):
                pe.wait_ge(S["srow"], b + 1)
                if b:
                    pe.wait_ge(S["scol"], b)
                for t in range(ST):
                    mm = pe.matmul(psX[:, b * ST + t:b * ST + t + 1], Srow[0:1, b, t * P:(t + 1) * P],
                                   ident[0:1, 0:1], start=True, stop=True)
                mm.then_inc(S["turn_mm"], 1)

            def turn_x(i):
                if i >= 2:
                    pe.wait_ge(S["xn"], i - 1)
                for t in (2 * i, 2 * i + 1):
                    for c in range(KC):
                        o = (t % 2) * D + c * P
                        mm = pe.transpose(psT[:, i % 2, o:o + P], XF[:, c, t * P:(t + 1) * P], ident[:, :])
                mm.then_inc(S["xt_mm"], 1)

            for b in range(BATCH):
                scores(b)
                turn_x(b * ST // 2)
                turn_x(b * ST // 2 + 1)
                turn_scores(b)
                for i in range(b * ST // 2 + 2, (b + 1) * ST // 2):
                    turn_x(i)
            pe.wait_ge(S["c_one"], 1)
            for b in range(BATCH):
                pe.wait_ge(S["srow"], b + 1)
                for t in range(ST):
                    pe.wait_ge(S["cmp"], b * (3 * ST - 1) + min(3 * (t + 1), 3 * ST - 1))
                    halves = [(psS[b][:, g], ahead[:, t, g * TW:(g + 1) * TW], t == 0, t == ST - 1) for g in range(2)]
                    ties = [(psS[b][:, t * P // TW, t * P % TW:t * P % TW + P], tie[:, t], False, False)]
                    for out, x, start, stop in halves + ties if t == 0 else ties + halves:
                        mm = pe.matmul(out, ones[:, :], x, start=start, stop=stop)
                    mm.then_inc(S["rank_mm"], 1)
                pe.wait_ge(S["oht"], b + 1)
                pe.wait_ge(S["xn"], BATCH * ST // 2)
                if b:
                    pe.wait_ge(S["oh"], b)
                for t in range(ST):
                    mm = pe.transpose(psT[:, t * P // TW, t * P % TW:t * P % TW + P], OHT[:, b, t * P:(t + 1) * P],
                                      ident[:, :])
                mm.then_inc(S["oh_mm"], 1)
            for b in range(BATCH):
                pe.wait_ge(S["oh"], b + 1)
                for c in range(KC):
                    for t in range(ST):
                        mm = pe.matmul(psO[:, c * CR + b * P:c * CR + (b + 1) * P],
                                       xN[:, b * ST + t, c * P:(c + 1) * P], OH[:, b, t], start=(t == 0),
                                       stop=(t == ST - 1))
                    mm.then_inc(S["g_mm"], 1)

            def mean_square(norm):
                pe.wait_ge(S["sq"], norm + 1)
                for k in range(KC):
                    mm = pe.matmul((psX, psO)[norm][:, 0:CR], ones_inv[:, :], sq[:, k], start=(k == 0),
                                   stop=(k == KC - 1))
                mm.then_inc(S["m_mm"], 1)

            mean_square(0)
            pe.wait_ge(S["w"], 80)
            pe.wait_ge(S["h"], KC)
            for part in range(2):
                for m in range(KC):
                    for k in range(KC):
                        mm = pe.matmul(psT[:, part, m * CR:(m + 1) * CR],
                                       Wqkv[:, k, part * D + m * P:part * D + (m + 1) * P], hT[:, k], start=(k == 0),
                                       stop=(k == KC - 1))
                mm.then_inc(S["qkv_mm"], 1)
            for b in range(BATCH):
                for k in range(KC):
                    mm = pe.matmul(psO[:, b * D:(b + 1) * D], hT[:, k, b * P:(b + 1) * P], Wqkv[:, k, 2 * D:3 * D],
                                   start=(k == 0), stop=(k == KC - 1))
                mm.then_inc(S["qkv_mm"], 1)
            for step, i in ATTN_PE:
                b, c = i // KC, i % KC
                if step == "scores":
                    if i == 0:
                        pe.wait_ge(S["q"], 1)
                        pe.wait_ge(S["oht"], BATCH)
                    pe.wait_ge(S["kb"], i + 1)
                    if i >= 2:
                        pe.wait_ge(S["msk"], i - 1)
                    for g in range(2):
                        mm = pe.matmul(psS[i % 2][:, g], qT[:, c, b * P:(b + 1) * P],
                                       KB[:, b, c, g * HB:(g + 1) * HB].rearrange("p h k -> p (h k)"), start=True,
                                       stop=True)
                    mm.then_inc(S["sc_mm"], 1)
                if step == "turn":
                    pe.wait_ge(S["exp"], i + 1)
                    if i == 0:
                        pe.wait_ge(S["kb"], NU)
                    for g in range(2):
                        if i:
                            pe.wait_ge(S[("ta", "tv")[g]], i)
                        for h in range(HB):
                            mm = pe.transpose(psT[:, g, h * P:(h + 1) * P], Pb[:, i % 2, g * HB + h], ident[:, :])
                        mm.then_inc(S["t_mm"], 1)
                if step == "out":
                    pe.wait_ge(S["ta"], i + 1)
                    pe.wait_ge(S["tv"], i + 1)
                    pe.wait_ge(S["v"], BATCH)
                    if i:
                        pe.wait_ge(S["cx"], i)
                    for h in range(HC):
                        mm = pe.matmul(psO[:, h * (HD + 1):(h + 1) * (HD + 1)], PT[:, i % 2, h],
                                       V17[:, b, c * HC + h], start=True, stop=True)
                    mm.then_inc(S["pv"], 1)
                if step == "back":
                    pe.wait_ge(S["cx"], i + 1)
                    pe.wait_ge(S["rs"], 1)
                    if i:
                        pe.wait_ge(S["ot"], i)
                    pe.transpose(psX[:, 0:P], Cx[:, i].rearrange("p h d -> p (h d)"), ident[:, :]) \
                        .then_inc(S["c_mm"], 1)
            pe.wait_ge(S["ot"], NU)
            for m in range(KC):
                for k in range(KC):
                    mm = pe.matmul(psX[:, m * CR:(m + 1) * CR], Wout[:, k, m * P:(m + 1) * P], oT[:, k],
                                   start=(k == 0), stop=(k == KC - 1))
            mm.then_inc(S["a_mm"], 1)
            mean_square(1)
            pe.wait_ge(S["h"], 2 * KC)
            pe.wait_ge(S["x1"], KC)
            for k in range(DC):
                w = min(P, DFF - k * P)
                for part, name in ((0, "f1_mm"), (1, "f2_mm")):
                    ps = (psS[part][0:w, k // 2, (k % 2) * CR:(k % 2 + 1) * CR] if k < 4 else
                          (psT[0:w, 0], psX[0:w])[part][:, (k % 2) * CR:(k % 2 + 1) * CR])
                    for j in range(KC):
                        mm = pe.matmul(ps, W12[:, part, j, k * P:k * P + w], hT[:, j], start=(j == 0),
                                       stop=(j == KC - 1))
                    mm.then_inc(S[name], 1)
            pe.wait_ge(S["rs"], 2)
            for b in range(BATCH):
                for k in range(KC):
                    pe.matmul(psO[:, b * D:(b + 1) * D], oT[:, k, b * P:(b + 1) * P], Wout[:, k, :], start=(k == 0),
                              stop=False)
                for k in range(DC):
                    w = min(P, DFF - k * P)
                    pe.wait_ge(S["g"], k + 1)
                    mm = pe.matmul(psO[:, b * D:(b + 1) * D], sg[0:w, k, b * P:(b + 1) * P], W3[0:w, k, :],
                                   start=False, stop=(k == DC - 1))
            mm.then_inc(S["d_mm"], 1)
            pe.wait_ge(S["d"], 1)
            for step, t in FINAL_PE:
                if step == "scatter":
                    b = t // BT
                    for c in range(KC):
                        if t >= 2:
                            pe.wait_ge(S["r"], 2 * (t - 2) + c + 1)
                        pe.matmul(psS[t % 2][:, c], dN[:, b, c * P:(c + 1) * P],
                                  OHT[:, b, (t % BT) * TW:(t % BT + 1) * TW], start=True,
                                  stop=True).then_inc(S["sct"], 1)
                if step == "mean":
                    pe.wait_ge(S["rsum"], t + 1)
                    if t:
                        pe.wait_ge(S["xc"], t)
                    pe.matmul(psT[:, 0], ones_inv[:, :], RS[:, :], start=True, stop=True).then_inc(S["mean"], 1)
                if step == "var":
                    pe.wait_ge(S["ss"], t + 1)
                    if t:
                        pe.wait_ge(S["znw"], t)
                    pe.matmul(psX[:, :], ones_inv[:, :], SS[:, t % 2], start=True, stop=True).then_inc(S["var"], 1)


def constants(nc, sem, ones_inv, consts):
    s = sem("const")
    with nc.Block() as block:
        @block.gpsimd
        def _(pool):
            pool.memset(ones_inv[:, :], 1.0 / D).then_inc(s, 1)
            pool.memset(consts[:, 0:1], ATTN_LN_EPS).then_inc(s, 1)
            pool.memset(consts[:, 1:2], LN_EPS).then_inc(s, 1)
            pool.wait_ge(s, 3)


def head_constants(nc, sem, ident, headmask, used):
    s = sem("headconst")
    with nc.Block() as block:
        @block.gpsimd
        def _(pool):
            numbers = [x.num for x in used]
            assert numbers == list(range(numbers[0], numbers[-1] + 1))
            pool.sem_clear(range(numbers[0], numbers[-1] + 1))
            pool.memset(ident[:, :], 0.0).then_inc(s, 1)
            pool.memset(headmask[:, :], 1.0).then_inc(s, 1)
            pool.wait_ge(s, 2)
            pool.affine_select(out=ident[:, :], in_=ident[:, :], compare_op=ALU.not_equal, fill=1.0, base=0,
                               pattern=[[-1, P]], channel_multiplier=1).then_inc(s, 1)
            pool.affine_select(out=headmask[:, :], in_=headmask[:, :], compare_op=ALU.is_ge, fill=0.0, base=0,
                               pattern=[[-HD, HC]], channel_multiplier=1).then_inc(s, 1)
            pool.wait_ge(s, 4)
            pool.affine_select(out=headmask[:, :], in_=headmask[:, :], compare_op=ALU.is_ge, fill=0.0, base=HD - 1,
                               pattern=[[HD, HC]], channel_multiplier=-1).then_inc(s, 1)
            pool.wait_ge(s, 5)


def program(nc, x_t, vecs, w_qkvo, w1, w2, ctx_t, cvecs, cw, fvecs, f_qkv, f_out, f_w12, f_w3, out_t):
    with ExitStack() as ctx:
        def sem(name):
            return ctx.enter_context(nc.semaphore(name))

        def sb(name, shape):
            return ctx.enter_context(nc.sbuf_tensor(name, shape, F32))

        XF = sb("XF", [P, KC, TOKENS])
        ones_inv, consts = sb("ones_inv", [P, P]), sb("consts", [P, 2])
        constants(nc, sem, ones_inv, consts)
        with ExitStack() as stage:
            own = []

            def layers_sem(name):
                own.append(stage.enter_context(nc.semaphore(name)))
                return own[-1]

            layers_stage(nc, layers_sem, XF, ones_inv, consts, x_t, vecs, w_qkvo, w1, w2)
        ident, headmask = sb("ident", [P, P]), sb("headmask", [P, HC])
        head_constants(nc, sem, ident, headmask, own)
        cross_stage(nc, sem, XF, ones_inv, consts, ident, headmask, x_t, ctx_t, cvecs, cw)
        routed_stage(nc, sem, XF, ones_inv, consts, ident, headmask, out_t, fvecs, f_qkv, f_out, f_w12, f_w3)


def kernel(**inputs):
    import numpy as np
    import concourse.bacc as bacc
    from concourse import mybir as _mybir
    from concourse.bass_utils import run_bass_kernel_spmd

    i = {k: np.asarray(v) for k, v in inputs.items()}
    a = lambda n: i["L0_attn_" + n]
    x = lambda n: i["L0_xattn_" + n]
    f = lambda n: i["L0_ffn_" + n]

    def per_feature(v):
        return np.moveaxis(v.reshape(*v.shape[:-1], -1, P), -1, 0)

    def rows_in(w):
        return np.moveaxis(w.reshape(*w.shape[:-2], -1, P, w.shape[-1]), -2, -3)

    arrays = {
        "x_t": i["x"].reshape(TOKENS, D).T,
        "vecs": np.concatenate([per_feature(a(n)) for n in ("bq", "bk", "bv", "bo", "ln1_s", "ln1_b", "b1", "b2",
                                                            "ln2_s", "ln2_b")], axis=2).reshape(P, -1),
        "w_qkvo": np.stack([rows_in(a(n)) for n in ("Wq", "Wk", "Wv", "Wo")], axis=2).reshape(LAYERS * P, -1),
        "w1": rows_in(a("W1")).reshape(LAYERS * P, -1),
        "w2": rows_in(a("W2")).reshape(LAYERS * P, -1),
        "ctx_t": i["ctx_1024"].reshape(BATCH * KEYS, D).T,
        "cvecs": per_feature(np.stack([x(n) for n in ("bq", "bk", "bv", "bo")])).reshape(P, -1),
        "cw": np.stack([rows_in(x(n).T) for n in ("Wq", "Wk", "Wv", "Wo")], axis=1).reshape(P, -1),
        "fvecs": per_feature(np.stack([f(n) for n in ("w_router", "g1", "g2")])).reshape(P, -1),
        "f_qkv": rows_in(f("W_qkv").T).reshape(P, -1),
        "f_out": rows_in(f("W_out").T).reshape(P, -1),
        "f_w12": np.stack([rows_in(f(n).T) for n in ("W1", "W2")], axis=1).reshape(P, -1),
        "f_w3": f("W3").T,
    }
    arrays = {k: np.ascontiguousarray(v) for k, v in arrays.items()}
    nc = bacc.Bacc("TRN2", target_bir_lowering=False, num_devices=1)
    args = {k: nc.dram_tensor(k, v.shape, _mybir.dt.from_np(v.dtype), kind="ExternalInput").ap()
            for k, v in arrays.items()}
    args["out_t"] = nc.dram_tensor("out_t", (D, TOKENS), F32, kind="ExternalOutput").ap()
    program(nc, **args)
    r = run_bass_kernel_spmd(nc, [arrays], core_ids=[0])
    return np.ascontiguousarray(r.results[0]["out_t"].T).reshape(BATCH, SEQ, D)
```
